# Optimizing a Trainium2 kernel written in Bass

```python
import numpy as np
import jax
import jax.numpy as jnp

def _softmax(x, axis=-1):
    return jax.nn.softmax(x, axis=axis)

def _gelu(x):
    return jax.nn.gelu(x, approximate=True)

def _silu(x):
    return jax.nn.silu(x)

def _sigmoid(x):
    return jax.nn.sigmoid(x)

def _layernorm(x, axis=-1, eps=1e-05):
    m = jnp.mean(x, axis=axis, keepdims=True)
    v = jnp.var(x, axis=axis, keepdims=True)
    return (x - m) / jnp.sqrt(v + eps)

def _scatter_add(tgt, idx, src, axis=0):
    return tgt.at[idx].add(src)

def _segment_sum(src, seg, n):
    return jax.ops.segment_sum(src, seg, n)
kernel_name = 'mk_macaron_d2_jaxref_r8_ecf07e'

def setup_inputs(seed: int=0):
    np.random.seed(seed)
    _w = jnp.asarray

    def _L0_attn_setup():
        import jax, jax.numpy as jnp
        import numpy as np
        H = 32
        DN = 128
        DR = 64
        DV = 128
        DQ = DN + DR
        HID = 512
        NEG_INF = -1e+30
        key = jax.random.key(seed)
        k0, k1, k2, k3 = jax.random.split(key, 4)
        B, S = (4, 128)
        hidden_states = jax.random.normal(k0, (B, S, HID), dtype=jnp.float32)
        wq = jax.random.normal(k1, (HID, H * DQ), dtype=jnp.float32) * 0.02
        wkv = jax.random.normal(k2, (HID, H * (DN + DV) + DR), dtype=jnp.float32) * 0.02
        wo = jax.random.normal(k3, (H * DV, HID), dtype=jnp.float32) * 0.02
        return {'hidden_states': hidden_states, 'wq': wq, 'wkv': wkv, 'wo': wo}
    _L0_attn_in = _L0_attn_setup()

    def _L0_ffn_setup():
        import jax, jax.numpy as jnp
        import numpy as np
        TOP_K = 2
        key = jax.random.key(seed)
        k0, k1, k2 = jax.random.split(key, 3)
        B, S, D, H, E = (4, 256, 512, 512, 8)
        sc = 1.0 / np.sqrt(D).astype(np.float32)
        x = jax.random.normal(k0, (B, S, D), dtype=jnp.float32)
        W_gate = jax.random.normal(k1, (D, E), dtype=jnp.float32) * sc
        b_gate = jnp.zeros((E,), dtype=jnp.float32)
        W_e = jax.random.normal(k2, (E, D, H), dtype=jnp.float32) * sc
        b_e = jnp.zeros((E, H), dtype=jnp.float32)
        return {'x': x, 'W_gate': W_gate, 'b_gate': b_gate, 'W_e': W_e, 'b_e': b_e}
    _L0_ffn_in = _L0_ffn_setup()

    def _L1_attn_setup():
        import jax, jax.numpy as jnp
        import numpy as np
        from jax import lax
        H = 64
        P = 64
        N = 128
        G = 8
        K = 4
        D_MODEL = 512
        I = H * P
        GN = G * N
        CONV_DIM = I + 2 * GN
        PROJ = I + CONV_DIM + H
        EPS = 1e-05
        GROUP_SIZE = I // G

        def _reference_tuple_inner(hidden_states, in_proj_w, conv_weight, conv_bias, dt_bias, A_log, D, norm_weight, out_proj_w):
            B, L, _ = hidden_states.shape
            proj = jnp.einsum('bld,pd->blp', hidden_states, in_proj_w)
            gate = proj[..., :I]
            hbc = proj[..., I:I + CONV_DIM]
            dt = proj[..., -H:]
            pad = jnp.pad(hbc, ((0, 0), (K - 1, 0), (0, 0)))
            conv = conv_bias
            for k in range(K):
                conv = conv + pad[:, k:k + L, :] * conv_weight[:, k]
            xBC = jax.nn.silu(conv)
            x = xBC[..., :I].reshape(B, L, H, P)
            Bm = xBC[..., I:I + GN].reshape(B, L, G, N)
            Cm = xBC[..., I + GN:].reshape(B, L, G, N)
            hpg = H // G
            B_h = jnp.repeat(Bm, hpg, axis=2)
            C_h = jnp.repeat(Cm, hpg, axis=2)
            dt_p = jax.nn.softplus(dt + dt_bias)
            A = -jnp.exp(A_log)
            dA = jnp.exp(dt_p * A)
            dtx = dt_p[..., None] * x

            def step(state, inp):
                dA_t, dtx_t, B_t, C_t = inp
                state = state * dA_t[..., None, None] + dtx_t[..., None] * B_t[:, :, None, :]
                y_t = jnp.einsum('bhpn,bhn->bhp', state, C_t)
                return (state, y_t)
            xs = (jnp.moveaxis(dA, 1, 0), jnp.moveaxis(dtx, 1, 0), jnp.moveaxis(B_h, 1, 0), jnp.moveaxis(C_h, 1, 0))
            state0 = jnp.zeros((B, H, P, N), jnp.float32)
            final_state, ys = lax.scan(step, state0, xs)
            y = jnp.moveaxis(ys, 0, 1) + x * D[None, None, :, None]
            y = y.reshape(B, L, I)
            yg = y.reshape(B, L, G, GROUP_SIZE)
            var = jnp.mean(yg * yg, axis=-1, keepdims=True)
            yn = (yg * lax.rsqrt(var + EPS)).reshape(B, L, I) * norm_weight
            yn = yn * jax.nn.silu(gate)
            out = jnp.einsum('bli,di->bld', yn, out_proj_w)
            conv_state_new = jnp.moveaxis(hbc[:, L - (K - 1):, :], 1, 2)
            return (out, conv_state_new, final_state)
        key = jax.random.key(seed)
        ks = jax.random.split(key, 6)
        B, L = (2, 256)
        s = 0.02
        return {'hidden_states': jax.random.normal(ks[0], (B, L, D_MODEL), jnp.float32), 'in_proj_w': jax.random.normal(ks[1], (PROJ, D_MODEL), jnp.float32) * s, 'conv_weight': jax.random.normal(ks[2], (CONV_DIM, K), jnp.float32) * s, 'conv_bias': jnp.zeros((CONV_DIM,), jnp.float32), 'dt_bias': jnp.ones((H,), jnp.float32), 'A_log': jnp.log(jnp.arange(1, H + 1, dtype=jnp.float32)), 'D': jnp.ones((H,), jnp.float32), 'norm_weight': jnp.ones((I,), jnp.float32), 'out_proj_w': jax.random.normal(ks[3], (D_MODEL, I), jnp.float32) * s}
    _L1_attn_in = _L1_attn_setup()

    def _L1_ffn_setup():
        import jax, jax.numpy as jnp
        import numpy as np
        NUM_EXPERTS = 4
        HIDDEN = 512
        RANK = 8
        ALPHA = 8.0
        SCALE = ALPHA / RANK
        key = jax.random.key(seed)
        ks = jax.random.split(key, 6)
        B, T, H, E, R = (4, 512, HIDDEN, NUM_EXPERTS, RANK)
        x = jax.random.normal(ks[0], (B, T, H), dtype=jnp.float32)
        W_up = jax.random.normal(ks[1], (H, H), dtype=jnp.float32) / np.sqrt(H)
        gate_w = jax.random.normal(ks[2], (E, H), dtype=jnp.float32) / np.sqrt(H)
        expert_bias = jnp.zeros((E,), dtype=jnp.float32)
        lora_A = jax.random.normal(ks[3], (E, R, H), dtype=jnp.float32) / np.sqrt(H)
        lora_B = jax.random.normal(ks[4], (E, H, R), dtype=jnp.float32) * 0.01
        return {'x': x, 'W_up': W_up, 'gate_w': gate_w, 'expert_bias': expert_bias, 'lora_A': lora_A, 'lora_B': lora_B}
    _L1_ffn_in = _L1_ffn_setup()
    _d = {'L0_attn_hidden_states': _L0_attn_in['hidden_states'], 'L0_attn_wq': _L0_attn_in['wq'], 'L0_attn_wkv': _L0_attn_in['wkv'], 'L0_attn_wo': _L0_attn_in['wo'], 'L0_ffn_W_gate': _L0_ffn_in['W_gate'], 'L0_ffn_b_gate': _L0_ffn_in['b_gate'], 'L0_ffn_W_e': _L0_ffn_in['W_e'], 'L0_ffn_b_e': _L0_ffn_in['b_e'], 'L1_attn_in_proj_w': _L1_attn_in['in_proj_w'], 'L1_attn_conv_weight': _L1_attn_in['conv_weight'], 'L1_attn_conv_bias': _L1_attn_in['conv_bias'], 'L1_attn_dt_bias': _L1_attn_in['dt_bias'], 'L1_attn_A_log': _L1_attn_in['A_log'], 'L1_attn_D': _L1_attn_in['D'], 'L1_attn_norm_weight': _L1_attn_in['norm_weight'], 'L1_attn_out_proj_w': _L1_attn_in['out_proj_w'], 'L1_ffn_W_up': _L1_ffn_in['W_up'], 'L1_ffn_gate_w': _L1_ffn_in['gate_w'], 'L1_ffn_expert_bias': _L1_ffn_in['expert_bias'], 'L1_ffn_lora_A': _L1_ffn_in['lora_A'], 'L1_ffn_lora_B': _L1_ffn_in['lora_B']}
    _x0 = _d['L0_attn_hidden_states']
    _d['L0_attn_hidden_states'] = jax.random.normal(jax.random.fold_in(jax.random.key(seed), 1), (1, 1024, 512), dtype=_x0.dtype)
    del _x0
    return _d

def reference(L0_attn_hidden_states, L0_attn_wq, L0_attn_wkv, L0_attn_wo, L0_ffn_W_gate, L0_ffn_b_gate, L0_ffn_W_e, L0_ffn_b_e, L1_attn_in_proj_w, L1_attn_conv_weight, L1_attn_conv_bias, L1_attn_dt_bias, L1_attn_A_log, L1_attn_D, L1_attn_norm_weight, L1_attn_out_proj_w, L1_ffn_W_up, L1_ffn_gate_w, L1_ffn_expert_bias, L1_ffn_lora_A, L1_ffn_lora_B):

    def _L0_attn_ref(hidden_states, wq, wkv, wo):
        import jax, jax.numpy as jnp
        import numpy as np
        H = 32
        DN = 128
        DR = 64
        DV = 128
        DQ = DN + DR
        HID = 512
        NEG_INF = -1e+30
        B, S, D = hidden_states.shape
        q = jnp.einsum('bsd,de->bse', hidden_states, wq).reshape(B, S, H, DQ)
        kv = jnp.einsum('bsd,de->bse', hidden_states, wkv)
        k = kv[..., :H * DN].reshape(B, S, H, DN)
        v = kv[..., H * DN:H * (DN + DV)].reshape(B, S, H, DV)
        scale = DQ ** (-0.5)
        scores = jnp.einsum('bqhd,bkhd->bhqk', q[..., :DN], k) * scale
        causal = jnp.tril(jnp.ones((S, S), dtype=bool))
        scores = jnp.where(causal[None, None], scores, NEG_INF)
        probs = jax.nn.softmax(scores, axis=-1)
        attn = jnp.einsum('bhqk,bkhd->bqhd', probs, v).reshape(B, S, H * DV)
        return jnp.einsum('bse,ed->bsd', attn, wo)

    def _L0_ffn_ref(x, W_gate, b_gate, W_e, b_e):
        import jax, jax.numpy as jnp
        import numpy as np
        TOP_K = 2
        logits = x @ W_gate + b_gate
        _, top_idx = jax.lax.top_k(logits, TOP_K)
        y_all = jax.nn.relu(jnp.einsum('bsd,edh->bseh', x, W_e) + b_e)
        y = jnp.take_along_axis(y_all, top_idx[..., None], axis=2)
        return y.mean(axis=2)

    def _L1_attn_ref(hidden_states, in_proj_w, conv_weight, conv_bias, dt_bias, A_log, D, norm_weight, out_proj_w):
        import jax, jax.numpy as jnp
        import numpy as np
        from jax import lax
        H = 64
        P = 64
        N = 128
        G = 8
        K = 4
        D_MODEL = 512
        I = H * P
        GN = G * N
        CONV_DIM = I + 2 * GN
        PROJ = I + CONV_DIM + H
        EPS = 1e-05
        GROUP_SIZE = I // G

        def _reference_tuple_inner(hidden_states, in_proj_w, conv_weight, conv_bias, dt_bias, A_log, D, norm_weight, out_proj_w):
            B, L, _ = hidden_states.shape
            proj = jnp.einsum('bld,pd->blp', hidden_states, in_proj_w)
            gate = proj[..., :I]
            hbc = proj[..., I:I + CONV_DIM]
            dt = proj[..., -H:]
            pad = jnp.pad(hbc, ((0, 0), (K - 1, 0), (0, 0)))
            conv = conv_bias
            for k in range(K):
                conv = conv + pad[:, k:k + L, :] * conv_weight[:, k]
            xBC = jax.nn.silu(conv)
            x = xBC[..., :I].reshape(B, L, H, P)
            Bm = xBC[..., I:I + GN].reshape(B, L, G, N)
            Cm = xBC[..., I + GN:].reshape(B, L, G, N)
            hpg = H // G
            B_h = jnp.repeat(Bm, hpg, axis=2)
            C_h = jnp.repeat(Cm, hpg, axis=2)
            dt_p = jax.nn.softplus(dt + dt_bias)
            A = -jnp.exp(A_log)
            dA = jnp.exp(dt_p * A)
            dtx = dt_p[..., None] * x

            def step(state, inp):
                dA_t, dtx_t, B_t, C_t = inp
                state = state * dA_t[..., None, None] + dtx_t[..., None] * B_t[:, :, None, :]
                y_t = jnp.einsum('bhpn,bhn->bhp', state, C_t)
                return (state, y_t)
            xs = (jnp.moveaxis(dA, 1, 0), jnp.moveaxis(dtx, 1, 0), jnp.moveaxis(B_h, 1, 0), jnp.moveaxis(C_h, 1, 0))
            state0 = jnp.zeros((B, H, P, N), jnp.float32)
            final_state, ys = lax.scan(step, state0, xs)
            y = jnp.moveaxis(ys, 0, 1) + x * D[None, None, :, None]
            y = y.reshape(B, L, I)
            yg = y.reshape(B, L, G, GROUP_SIZE)
            var = jnp.mean(yg * yg, axis=-1, keepdims=True)
            yn = (yg * lax.rsqrt(var + EPS)).reshape(B, L, I) * norm_weight
            yn = yn * jax.nn.silu(gate)
            out = jnp.einsum('bli,di->bld', yn, out_proj_w)
            conv_state_new = jnp.moveaxis(hbc[:, L - (K - 1):, :], 1, 2)
            return (out, conv_state_new, final_state)
        return _reference_tuple_inner(hidden_states, in_proj_w, conv_weight, conv_bias, dt_bias, A_log, D, norm_weight, out_proj_w)[0]

    def _L1_ffn_ref(x, W_up, gate_w, expert_bias, lora_A, lora_B):
        import jax, jax.numpy as jnp
        import numpy as np
        NUM_EXPERTS = 4
        HIDDEN = 512
        RANK = 8
        ALPHA = 8.0
        SCALE = ALPHA / RANK
        B, T, H = x.shape
        E = gate_w.shape[0]
        x_flat = x.reshape(-1, H)
        logits = x_flat @ gate_w.T + expert_bias
        top1 = jnp.argmax(logits, axis=-1)
        one_hot = jax.nn.one_hot(top1, E, dtype=x_flat.dtype)
        base_out = jnp.einsum('bth,oh->bto', x, W_up)
        z = jnp.einsum('nh,erh->ner', x_flat, lora_A)
        d = jnp.einsum('ner,ehr->neh', z, lora_B) * SCALE
        delta = jnp.einsum('neh,ne->nh', d, one_hot)
        return base_out + delta.reshape(B, T, H)
    x = L0_attn_hidden_states
    x = x + 0.5 * _L0_ffn_ref(_layernorm(x, axis=-1), L0_ffn_W_gate, L0_ffn_b_gate, L0_ffn_W_e, L0_ffn_b_e)
    x = x + _L0_attn_ref(_layernorm(x, axis=-1), L0_attn_wq, L0_attn_wkv, L0_attn_wo)
    x = x + 0.5 * _L0_ffn_ref(_layernorm(x, axis=-1), L0_ffn_W_gate, L0_ffn_b_gate, L0_ffn_W_e, L0_ffn_b_e)
    x = x + 0.5 * _L1_ffn_ref(_layernorm(x, axis=-1), L1_ffn_W_up, L1_ffn_gate_w, L1_ffn_expert_bias, L1_ffn_lora_A, L1_ffn_lora_B)
    x = x + _L1_attn_ref(_layernorm(x, axis=-1), L1_attn_in_proj_w, L1_attn_conv_weight, L1_attn_conv_bias, L1_attn_dt_bias, L1_attn_A_log, L1_attn_D, L1_attn_norm_weight, L1_attn_out_proj_w)
    x = x + 0.5 * _L1_ffn_ref(_layernorm(x, axis=-1), L1_ffn_W_up, L1_ffn_gate_w, L1_ffn_expert_bias, L1_ffn_lora_A, L1_ffn_lora_B)
    return x

_drawn_inputs = setup_inputs


def setup_inputs(seed=0):
    import zlib

    import numpy as np

    out = dict(_drawn_inputs(seed))
    spreads = {'L0_ffn_b_gate': (0.0, 0.1),
     'L0_ffn_b_e': (0.0, 0.1),
     'L1_attn_conv_bias': (0.0, 0.1),
     'L1_attn_dt_bias': (1.0, 0.6),
     'L1_attn_D': (1.0, 0.2),
     'L1_attn_norm_weight': (1.0, 0.2),
     'L1_ffn_expert_bias': (0.0, 0.8)}
    factors = {'L0_attn_wq': 3.645,
     'L1_attn_A_log': 8.0,
     'L1_ffn_gate_w': 4.126,
     'L1_ffn_lora_A': 3.571,
     'L1_ffn_lora_B': 3.498}
    for name, (base, spread) in spreads.items():
        noise = np.random.default_rng([zlib.crc32(name.encode()), seed]).standard_normal(out[name].shape)
        drawn = base * np.exp(spread * noise) if base else spread * noise
        out[name] = jnp.asarray(drawn.astype(out[name].dtype))
    for name, factor in factors.items():
        out[name] = (out[name] * factor).astype(out[name].dtype)
    return out
```

```python
import concourse.bass as bass
from concourse import mybir
from contextlib import ExitStack

F32 = mybir.dt.float32
F32R = mybir.dt.float32r
BF16 = mybir.dt.bfloat16
ALU = mybir.AluOpType
ACT = mybir.ActivationFunctionType
AX = mybir.AxisListType

P = 128
D = 512
S = 1024
T = S // P
C = D // P
HALF = 512
EPS = 1e-5


def build(nc, stages, hidden, wq, wkv, wo, w_gate, b_gate, w_e, b_e, in_proj_w, conv_weight, conv_bias,
          dt_bias, a_log, d_skip, norm_weight, out_proj_w, w_up, gate_w, expert_bias, lora_a, lora_b, out):
    whole = ExitStack()
    with whole:
        def sb(stack, name, shape, dtype=F32):
            return stack.enter_context(nc.sbuf_tensor(name, shape, dtype))

        def sem(stack, name):
            return stack.enter_context(nc.semaphore(name))

        x_res = sb(whole, "x_res", [P, T, D])
        xnT_hi = sb(whole, "xnT_hi", [P, C, S], F32R)
        xnT_lo = sb(whole, "xnT_lo", [P, C, S], F32R)
        ident = sb(whole, "ident", [P, P])
        zero_col = sb(whole, "zero_col", [P, 1])
        ps = whole.enter_context(nc.psum_tensor("ps", [P, 8, HALF], F32))

        def mm3(pe, out, lhs, rhs, first, last):
            pe.matmul(out, lhs[0], rhs[0], start=first, stop=False, skip_group_check=True)
            pe.matmul(out, lhs[0], rhs[1], start=False, stop=False, skip_group_check=True)
            return pe.matmul(out, lhs[1], rhs[0], start=False, stop=last, skip_group_check=True)

        def xn_cols(c, a, b):
            return xnT_hi[:, c, a:b], xnT_lo[:, c, a:b]

        with ExitStack() as st:
            x_loaded = sem(st, "x_loaded")
            ident_zeroed = sem(st, "ident_zeroed")
            with nc.Block() as block:
                @block.sync
                def _(sp):
                    src = hidden.rearrange("a (t p) d -> p (a t) d", p=P)
                    sp.dma_start(x_res[:, :, :], src).then_inc(x_loaded, 16)
                    sp.wait_ge(x_loaded, 16)

                @block.gpsimd
                def _(pool):
                    pool.memset(zero_col[:, :], 0.0)
                    pool.memset(ident[:, :], 0.0).then_inc(ident_zeroed, 1)
                    pool.wait_ge(ident_zeroed, 1)
                    pool.affine_select(out=ident[:, :], in_=ident[:, :], compare_op=ALU.not_equal, fill=1.0,
                                       base=0, pattern=[[-1, P]], channel_multiplier=1)

        def inverse_root(dve, step, n0, r, root, v, tmp):
            dve.reciprocal(r, root).then_inc(step, 1)
            dve.wait_ge(step, n0 + 1)
            dve.tensor_tensor(tmp, r, r, ALU.mult).then_inc(step, 1)
            dve.wait_ge(step, n0 + 2)
            dve.tensor_tensor(tmp, tmp, v, ALU.mult).then_inc(step, 1)
            dve.wait_ge(step, n0 + 3)
            dve.tensor_scalar(tmp, tmp, -0.5, 1.5, ALU.mult, ALU.add).then_inc(step, 1)
            dve.wait_ge(step, n0 + 4)
            dve.tensor_tensor(r, r, tmp, ALU.mult).then_inc(step, 1)

        def layer_norm(tag):
            with ExitStack() as st:
                stats = sb(st, f"stats{tag}", [P, T, 6])
                mean_var = sb(st, f"mean_var{tag}", [P, T, 2])
                rstd = sb(st, f"rstd{tag}", [P, T])
                xn = sb(st, f"xn{tag}", [P, T, D])
                dve_step = sem(st, f"ln_dve_step{tag}")
                xn_ready = sem(st, f"xn_ready{tag}")
                turned = sem(st, f"xn_turned{tag}")
                hi_done = sem(st, f"xn_hi_done{tag}")
                lo_done = sem(st, f"xn_lo_done{tag}")
                var = sb(st, f"var{tag}", [P, T])
                root = sb(st, f"root{tag}", [P, T])
                r2v = sb(st, f"r2v{tag}", [P, T])
                var_ready = sem(st, f"var_ready{tag}")
                root_ready = sem(st, f"root_ready{tag}")
                banks = 4
                with nc.Block() as block:
                    @block.vector
                    def _(dve):
                        for t in range(T):
                            dve.bn_stats(stats[:, t, :], x_res[:, t, :]).then_inc(dve_step, 1)
                        for t in range(T):
                            dve.wait_ge(dve_step, t + 1)
                            dve.bn_aggr(mean_var[:, t, :], stats[:, t, :]).then_inc(dve_step, 1)
                        dve.wait_ge(dve_step, 2 * T)
                        dve.tensor_scalar(var[:, :], mean_var[:, :, 1], EPS, None, ALU.add).then_inc(var_ready, 1)
                        dve.wait_ge(root_ready, 1)
                        inverse_root(dve, dve_step, 2 * T, rstd[:, :], root[:, :], var[:, :], r2v[:, :])
                        dve.wait_ge(dve_step, 2 * T + 5)
                        for t in range(T):
                            dve.tensor_scalar(xn[:, t, :], x_res[:, t, :], mean_var[:, t, 0:1],
                                              rstd[:, t:t + 1], ALU.subtract, ALU.mult).then_inc(xn_ready, 1)
                        for t in range(T):
                            dve.wait_ge(hi_done, t + 1)
                            cols = slice(t * P, (t + 1) * P)
                            dve.tensor_tensor(xnT_lo[:, :, cols],
                                              ps[:, t % banks, :].rearrange("p (c n) -> p c n", c=C),
                                              xnT_hi[:, :, cols].bitcast(F32), ALU.subtract).then_inc(lo_done, 1)

                    @block.tensor
                    def _(pe):
                        for t in range(T):
                            pe.wait_ge(xn_ready, t + 1)
                            if t >= banks:
                                pe.wait_ge(lo_done, t - banks + 1)
                            for c in range(C):
                                last = pe.transpose(ps[:, t % banks, c * P:(c + 1) * P],
                                                    xn[:, t, c * P:(c + 1) * P], ident[:, :])
                            last.then_inc(turned, 1)

                    @block.scalar
                    def _(act):
                        act.wait_ge(var_ready, 1)
                        act.activation(root[:, :], var[:, :], ACT.Sqrt).then_inc(root_ready, 1)
                        for t in range(T):
                            act.wait_ge(turned, t + 1)
                            act.activation(xnT_hi[:, :, t * P:(t + 1) * P],
                                           ps[:, t % banks, :].rearrange("p (c n) -> p c n", c=C),
                                           ACT.Copy).then_inc(hi_done, 1)

        def rank_mask(dve, step, n0, logits, mask, gt, eq, before, E, K, scale):
            shape = [P, T, E, E]
            rival = logits.rearrange("p (t j) -> p t j", j=E).unsqueeze(2).to_broadcast(shape)
            own = logits.rearrange("p (t e) -> p t e", e=E).unsqueeze(3).to_broadcast(shape)
            v = [a.rearrange("p (t e j) -> p t e j", e=E, j=E) for a in (gt, eq)]
            for k, ins in enumerate((
                lambda: dve.tensor_tensor(v[0], rival, own, ALU.is_gt),
                lambda: dve.tensor_tensor(v[1], rival, own, ALU.is_equal),
                lambda: dve.tensor_tensor(v[1], v[1], before.unsqueeze(1).to_broadcast(shape), ALU.mult),
                lambda: dve.tensor_tensor(v[0], v[0], v[1], ALU.add),
                lambda: dve.tensor_reduce(mask, v[0].rearrange("p t e j -> p (t e) j"), AX.X, ALU.add),
                lambda: dve.tensor_scalar(mask, mask, K - 0.5, scale, ALU.is_lt, ALU.mult),
            )):
                dve.wait_ge(step, n0 + k)
                ins().then_inc(step, 1)
            return n0 + 6

        def experts_ffn(tag):
            E, K, SCALE, RING = 8, 2, 0.25, 4
            with ExitStack() as st:
                w_raw = sb(st, f"ew_raw{tag}", [P, 2, C, D])
                w_hi = [sb(st, f"ew_hi{k}{tag}", [P, C, D], F32R) for k in range(2)]
                w_lo = [sb(st, f"ew_lo{k}{tag}", [P, C, D], F32R) for k in range(2)]
                b_raw = sb(st, f"eb_raw{tag}", [2, E, D])
                b_hi = sb(st, f"eb_hi{tag}", [2, E, D], F32R)
                b_two = sb(st, f"eb_two{tag}", [2, E, D], F32R)
                row_neg = sb(st, f"row_neg{tag}", [2, 1])
                ones_raw = sb(st, f"ones_raw{tag}", [2, P])
                ones_two = sb(st, f"ones_two{tag}", [2, P], F32R)
                g_raw = sb(st, f"g_raw{tag}", [P, C, E])
                g_hi = sb(st, f"g_hi{tag}", [P, C, E], F32R)
                g_lo = sb(st, f"g_lo{tag}", [P, C, E], F32R)
                g_bias = sb(st, f"g_bias{tag}", [P, E])
                logitsT = sb(st, f"logitsT{tag}", [E, S])
                logits = sb(st, f"logits{tag}", [P, T * E])
                before = sb(st, f"before{tag}", [P, E, E])
                gt = sb(st, f"gt{tag}", [P, T * E * E])
                eq = sb(st, f"eq{tag}", [P, T * E * E])
                mask = sb(st, f"mask{tag}", [P, T * E])
                relu = sb(st, f"relu{tag}", [P, 2, D])
                small_loaded = sem(st, f"e_small_loaded{tag}")
                w_loaded = [sem(st, f"ew_loaded{k}{tag}") for k in range(2)]
                w_split = sem(st, f"ew_split{tag}")
                pool_step = sem(st, f"e_pool_step{tag}")
                hi_step = sem(st, f"ew_hi_step{tag}")
                consts_ready = sem(st, f"e_consts{tag}")
                dve_step = sem(st, f"e_dve_step{tag}")
                logitsT_ready = sem(st, f"logitsT_ready{tag}")
                logitsT_copied = sem(st, f"logitsT_copied{tag}")
                logits_turned = sem(st, f"logits_turned{tag}")
                mask_ready = sem(st, f"mask_ready{tag}")
                y_ready = sem(st, f"ey_ready{tag}")
                relu_done = sem(st, f"relu_done{tag}")
                added = sem(st, f"e_added{tag}")
                with nc.Block() as block:
                    @block.sync
                    def _(sp):
                        sp.dma_start(g_raw[:, :, :], w_gate.rearrange("(c p) e -> p c e", p=P)).then_inc(small_loaded, 16)
                        sp.dma_start(g_bias[:, :], b_gate.partition_broadcast(P)).then_inc(small_loaded, 16)
                        sp.dma_start(b_raw[:, :, :], b_e.partition_broadcast(2)).then_inc(small_loaded, 16)
                        with sp.Fori(0, E // 2) as i:
                            for k in range(2):
                                sp.wait_ge(w_split, i * 2 + (k + 1))
                                sp.dma_start(w_raw[:, k, :, :],
                                             w_e[bass.ds(i * 2 + k, 1)].rearrange("e (c p) h -> p (e c) h", p=P))\
                                  .then_inc(w_loaded[k], 16)

                    @block.gpsimd
                    def _(pool):
                        pool.sem_inc(w_split, 2)
                        pool.memset(before[:, :, :], 1.0).then_inc(pool_step, 1)
                        pool.memset(row_neg[:, :], 0.0).then_inc(pool_step, 1)
                        pool.memset(ones_raw[:, :], 1.0).then_inc(pool_step, 1)
                        pool.wait_ge(pool_step, 3)
                        pool.affine_select(out=before[:, :, :], in_=before[:, :, :], compare_op=ALU.is_gt, fill=0.0,
                                           base=0, pattern=[[1, E], [-1, E]], channel_multiplier=0)\
                            .then_inc(consts_ready, 1)
                        pool.affine_select(out=row_neg[:, :], in_=row_neg[:, :], compare_op=ALU.not_equal, fill=-1.0,
                                           base=-1, pattern=[[0, 1]], channel_multiplier=1).then_inc(consts_ready, 1)
                        pool.tensor_copy(ones_two[:, :], ones_raw[:, :]).then_inc(consts_ready, 1)
                        with pool.Fori(0, E // 2) as i:
                            for k in range(2):
                                pool.wait_ge(w_loaded[k], (i + 1) * 16)
                                pool.wait_ge(y_ready, i * 2 * T + (k + 1) * T)
                                pool.tensor_tensor(w_hi[k][:, :, :], w_raw[:, k, :, :],
                                                   zero_col[:, :].unsqueeze(2).to_broadcast([P, C, D]), ALU.add).then_inc(hi_step, 1)
                                pool.wait_ge(hi_step, i * 2 + (k + 1))
                                pool.tensor_tensor(w_lo[k][:, :, :], w_raw[:, k, :, :], w_hi[k][:, :, :].bitcast(F32),
                                                   ALU.subtract).then_inc(w_split, 1)

                    @block.tensor
                    def _(pe):
                        pe.sem_inc(y_ready, 2 * T)
                        pe.wait_ge(dve_step, 2)
                        for h in range(2):
                            for c in range(C):
                                rhs = xn_cols(c, h * HALF, (h + 1) * HALF)
                                last = mm3(pe, ps[0:E, h, :], (g_hi[:, c, :], g_lo[:, c, :]), rhs, c == 0, c == C - 1)
                        last.then_inc(logitsT_ready, 1)
                        pe.wait_ge(logitsT_copied, 1)
                        for t in range(T):
                            last = pe.transpose(ps[:, 2, t * E:(t + 1) * E], logitsT[:, t * P:(t + 1) * P],
                                                ident[0:E, 0:E])
                        last.then_inc(logits_turned, 1)
                        pe.wait_ge(dve_step, 4)
                        pe.wait_ge(consts_ready, 3)
                        with pe.Fori(0, E // 2) as i:
                            for k in range(2):
                                pe.wait_ge(w_split, i * 2 + (k + 3))
                                for t in range(T):
                                    n = k * T + t
                                    bank = ps[:, 4 + n % RING, :]
                                    pe.wait_ge(relu_done, i * 2 * T + (n + 1))
                                    for c in range(C):
                                        mm3(pe, bank, xn_cols(c, t * P, (t + 1) * P),
                                            (w_hi[k][:, c, :], w_lo[k][:, c, :]), c == 0, False)
                                    pe.matmul(bank, ones_two[:, :],
                                              b_two[:, bass.ds(i * 2 + k, 1), :].rearrange("p e d -> p (e d)"),
                                              start=False, stop=True, skip_group_check=True).then_inc(y_ready, 1)

                    @block.scalar
                    def _(act):
                        act.sem_inc(relu_done, RING)
                        act.wait_ge(logitsT_ready, 1)
                        act.activation(logitsT[:, :].rearrange("e (h n) -> e h n", h=2), ps[0:E, 0:2, :], ACT.Copy)\
                           .then_inc(logitsT_copied, 1)
                        act.wait_ge(mask_ready, 1)
                        with act.Fori(0, E // 2) as i:
                            for k in range(2):
                                for t in range(T):
                                    n = k * T + t
                                    act.wait_ge(y_ready, i * 2 * T + (n + 1 + 2 * T))
                                    act.wait_ge(added, i * 2 * T + (n + 1))
                                    act.activation(relu[:, n % 2, :], ps[:, 4 + n % RING, :], ACT.Relu,
                                                   scale=mask[:, bass.ds(i * 2 + (t * E + k), 1)])\
                                       .then_inc(relu_done, 1)

                    @block.vector
                    def _(dve):
                        dve.sem_inc(added, 2)
                        dve.wait_ge(small_loaded, 48)
                        dve.tensor_copy(g_hi[:, :, :], g_raw[:, :, :]).then_inc(dve_step, 1)
                        dve.wait_ge(dve_step, 1)
                        dve.tensor_tensor(g_lo[:, :, :], g_raw[:, :, :], g_hi[:, :, :].bitcast(F32), ALU.subtract)\
                           .then_inc(dve_step, 1)
                        dve.tensor_copy(b_hi[:, :, :], b_raw[:, :, :]).then_inc(dve_step, 1)
                        dve.wait_ge(dve_step, 3)
                        dve.wait_ge(consts_ready, 2)
                        dve.scalar_tensor_tensor(b_two[:, :, :], b_hi[:, :, :].bitcast(F32), row_neg[:, 0:1],
                                                 b_raw[:, :, :], ALU.mult, ALU.add).then_inc(dve_step, 1)
                        dve.wait_ge(logits_turned, 1)
                        dve.tensor_tensor(logits[:, :].rearrange("p (t e) -> p t e", e=E),
                                          ps[:, 2, 0:T * E].rearrange("p (t e) -> p t e", e=E),
                                          g_bias[:, :].unsqueeze(1).to_broadcast([P, T, E]), ALU.add)\
                           .then_inc(dve_step, 1)
                        n = rank_mask(dve, dve_step, 5, logits[:, :], mask[:, :], gt[:, :], eq[:, :],
                                      before[:, :, :], E, K, SCALE)
                        dve.wait_ge(dve_step, n)
                        dve.sem_inc(mask_ready, 1)
                        with dve.Fori(0, E // 2) as i:
                            for k in range(2):
                                for t in range(T):
                                    n = k * T + t
                                    dve.wait_ge(relu_done, i * 2 * T + (n + 1 + RING))
                                    dve.tensor_tensor(x_res[:, t, :], x_res[:, t, :], relu[:, n % 2, :], ALU.add)\
                                       .then_inc(added, 1)

        def attention(tag):
            H, DN, DQ, HP = 32, 128, 192, 2
            TURNS = H // HP
            SCALE = DQ ** -0.5
            RING = 4
            with ExitStack() as st:
                raw = {k: sb(st, f"a_raw_{k}", [P, 2 * D]) for k in ("q", "k", "v", "o")}
                w = {k: [sb(st, f"a_w{part}_{k}", [P, 2 * D], F32R) for part in ("hi", "lo")] for k in ("q", "k", "v", "o")}
                cols4 = "p (c n) -> p c n"
                wq2, wk2, wv2 = [[a[:, :].rearrange(cols4, c=C) for a in w[k]] for k in ("q", "k", "v")]
                wo2 = [a[:, :].rearrange("p (h n) -> p h n", h=HP) for a in w["o"]]
                qT = [sb(st, f"qT_{part}", [P, HP, S], F32R) for part in ("hi", "lo")]
                kT = [sb(st, f"kT_{part}", [P, HP, S], F32R) for part in ("hi", "lo")]
                V = [sb(st, f"V_{part}", [P, T, HP * DN], F32R) for part in ("hi", "lo")]
                prob = sb(st, "prob", [P, 2, S])
                PT = [sb(st, f"PT_{part}", [P, T, HALF], F32R) for part in ("hi", "lo")]
                oT = [sb(st, f"oT_{part}", [P, HP, S], F32R) for part in ("hi", "lo")]
                top = sb(st, "row_top", [P, 2])
                shift = sb(st, "row_shift", [P, 2])
                total = sb(st, "row_total", [P, 2])
                share = sb(st, "row_share", [P, 2])
                ident_bf = sb(st, "ident_bf", [P, P], BF16)
                later_f = sb(st, "later_f", [P, P])
                later = sb(st, "later_keys", [P, P], BF16)
                raw_loaded = {k: sem(st, f"a_loaded_{k}") for k in "qkvo"}
                split_done = {k: sem(st, f"a_split_{k}") for k in "qkvo"}
                hi_step = sem(st, "a_hi_step")
                pool_step = sem(st, "a_pool_step")
                consts = sem(st, "a_consts")
                zeroed = sem(st, "a_pt_zeroed")
                bank_full = sem(st, "a_bank_full")
                hi_done = sem(st, "a_hi_done")
                bank_free = sem(st, "a_bank_free")
                scores_full = sem(st, "scores_full")
                shift_ready = sem(st, "shift_ready")
                top_found = sem(st, "top_found")
                exp_done = sem(st, "exp_done")
                share_found = sem(st, "share_found")
                scaled = sem(st, "prob_scaled")

                steps = [("qk", 0, m, h) for m in "qk" for h in range(2)]
                steps += [("s", 0), ("v", 0), ("n", 0)]
                steps += [("qk", 1, m, h) for m in "qk" for h in range(2)] + [("v", k) for k in range(1, 4)]
                units = [(hh, qt) for hh in range(HP) for qt in range(T)]
                N_UNITS = len(units)
                pending = None
                for u, (hh, qt) in enumerate(units):
                    if u + 1 < N_UNITS:
                        steps.append(("s", u + 1))
                    for k0 in range(0, qt + 1, 4):
                        steps.append(("t", u, k0, min(k0 + 4, qt + 1)))
                    if u + 1 < N_UNITS:
                        steps.append(("n", u + 1))
                    if pending:
                        steps.append(pending)
                        pending = None
                    if qt % 4 == 3:
                        pending = ("pv", hh, qt // 4)
                steps.append(pending)
                steps += [("wo", t) for t in range(T)]
                ring_kinds = ("qk", "v", "t", "pv", "wo")
                USES = sum(s[0] in ring_kinds for s in steps)
                SPLITS = sum(s[0] in ("qk", "v", "t", "pv") for s in steps)

                assert USES % RING == 0

                def use_of(step):
                    return [s for s in steps if s[0] in ring_kinds].index(step)

                def split_of(step):
                    return [s for s in steps if s[0] in ring_kinds and s[0] != "wo"].index(step)

                last_pv = {(hh, c): split_of(("pv", hh, c)) for hh in range(HP) for c in range(2)}

                def pieces(qt):
                    n = max((qt + 1) * P, 256)
                    if n <= HALF:
                        return [(0, n)]
                    return [(0, HALF), (HALF, max(n, HALF + 256))]

                def split_views(step):
                    kind = step[0]
                    if kind == "qk":
                        _, hh, m, h = step
                        dst = qT if m == "q" else kT
                        return (lambda b: b[:, :]), [a[:, hh, h * HALF:(h + 1) * HALF] for a in dst]
                    if kind == "v":
                        k = step[1]
                        return (lambda b: b[:, :].rearrange("p (t n) -> p t n", t=2)), [a[:, 2 * k:2 * k + 2, :] for a in V]
                    if kind == "t":
                        _, u, k0, k1 = step
                        q0 = (units[u][1] % 4) * P
                        return (lambda b: b[:, 0:(k1 - k0) * P].rearrange("p (k n) -> p k n", n=P)), \
                            [a[:, k0:k1, q0:q0 + P] for a in PT]
                    _, hh, c = step
                    return (lambda b: b[:, :]), [a[:, hh, c * HALF:(c + 1) * HALF] for a in oT]

                with nc.Block() as block:
                    @block.sync
                    def _(sp):
                        sp.wait_ge(consts, 1)
                        wq_v = wq.rearrange("(c p) (h e) -> p c h e", p=P, e=DQ)
                        wk_v = wkv[:, 0:H * DN].rearrange("(c p) (h e) -> p c h e", p=P, e=DN)
                        wv_v = wkv[:, H * DN:2 * H * DN].rearrange("(c p) (h e) -> p c h e", p=P, e=DN)
                        wo_v = wo.rearrange("(h p) n -> p h n", p=DN)
                        with sp.Fori(0, TURNS) as i:
                            for key, src in (("q", wq_v), ("k", wk_v), ("v", wv_v)):
                                sp.wait_ge(split_done[key], i + 1)
                                dst = raw[key][:, :].rearrange("p (c h e) -> p c h e", c=C, h=HP)
                                for c in range(C):
                                    sp.dma_start(dst[:, c], src[:, c, bass.ds(i * HP, HP), 0:DN]).then_inc(raw_loaded[key], 16)
                            sp.wait_ge(split_done["o"], i + 1)
                            sp.dma_start(raw["o"][:, :].rearrange("p (h n) -> p h n", h=HP),
                                         wo_v[:, bass.ds(i * HP, HP), :]).then_inc(raw_loaded["o"], 16)

                    @block.gpsimd
                    def _(pool):
                        for key in "qkvo":
                            pool.sem_inc(split_done[key], 1)
                        pool.memset(later_f[:, :], 0.0).then_inc(pool_step, 1)
                        pool.tensor_copy(ident_bf[:, :], ident[:, :]).then_inc(consts, 1)
                        pool.wait_ge(pool_step, 1)
                        pool.affine_select(out=later_f[:, :], in_=later_f[:, :], compare_op=ALU.is_ge, fill=-1e30,
                                           base=0, pattern=[[-1, P]], channel_multiplier=1).then_inc(pool_step, 1)
                        pool.wait_ge(pool_step, 2)
                        pool.tensor_copy(later[:, :], later_f[:, :]).then_inc(consts, 1)
                        last_use = {"q": use_of(("qk", 1, "q", 1)), "k": use_of(("qk", 1, "k", 1)),
                                    "v": use_of(("v", 3)), "o": use_of(("wo", T - 1))}
                        with pool.Fori(0, TURNS) as i:
                            for n, key in enumerate("qkvo"):
                                pool.wait_ge(raw_loaded[key], (i + 1) * (16 if key == "o" else 16 * C))
                                pool.wait_ge(bank_full, i * USES + (last_use[key] + 1))
                                hi, lo = w[key]
                                pool.tensor_tensor(hi[:, :], raw[key][:, :], zero_col[:, :].to_broadcast([P, 2 * D]), ALU.add).then_inc(hi_step, 1)
                                pool.wait_ge(hi_step, i * 4 + (n + 1))
                                pool.tensor_tensor(lo[:, :], raw[key][:, :], hi[:, :].bitcast(F32), ALU.subtract)\
                                    .then_inc(split_done[key], 1)

                    @block.tensor
                    def _(pe):
                        pe.sem_inc(bank_full, USES)
                        pe.wait_ge(consts, 2)
                        with pe.Fori(0, TURNS) as i:
                            use = 0
                            for step in steps:
                                kind = step[0]
                                if kind in ring_kinds:
                                    pe.wait_ge(bank_free, i * USES + (use + 1))
                                    bank = ps[:, 4 + use % RING, :]
                                    use += 1
                                if kind == "qk":
                                    _, hh, m, h = step
                                    if hh == 0 and h == 0:
                                        pe.wait_ge(split_done[m], i + 2)
                                    wt = wq2 if m == "q" else wk2
                                    for c in range(C):
                                        last = mm3(pe, bank, [a[:, c, hh * DN:(hh + 1) * DN] for a in wt],
                                                   xn_cols(c, h * HALF, (h + 1) * HALF), c == 0, c == C - 1)
                                elif kind == "v":
                                    if step[1] == 0:
                                        pe.wait_ge(split_done["v"], i + 2)
                                    for k in range(2):
                                        t = 2 * step[1] + k
                                        for c in range(C):
                                            last = mm3(pe, bank[:, k * 256:(k + 1) * 256], xn_cols(c, t * P, (t + 1) * P),
                                                       [a[:, c, :] for a in wv2], c == 0, c == C - 1)
                                elif kind == "s":
                                    u = step[1]
                                    hh, qt = units[u]
                                    pe.wait_ge(exp_done, i * N_UNITS + (u + 1))
                                    if qt == 0:
                                        pe.wait_ge(bank_free, i * USES + (use_of(("qk", hh, "k", 1)) + 1 + RING))
                                    sbank = ps[:, 2 * (u % 2):2 * (u % 2) + 2, :].rearrange("p b n -> p (b n)")
                                    q0 = qt * P
                                    for a, b in pieces(qt):
                                        mm3(pe, sbank[:, a:b], [x[:, hh, q0:q0 + P] for x in qT],
                                            [x[:, hh, a:b] for x in kT], True, False)
                                    last = pe.matmul(sbank[:, q0:q0 + P], ident_bf[:, :], later[:, :],
                                                     start=False, stop=True, skip_group_check=True)
                                    last.then_inc(scores_full, 1)
                                elif kind == "t":
                                    _, u, k0, k1 = step
                                    if k0 == 0:
                                        pe.wait_ge(scaled, i * N_UNITS + (u + 1 + 2))
                                    for k in range(k0, k1):
                                        last = pe.transpose(bank[:, (k - k0) * P:(k - k0 + 1) * P],
                                                            prob[:, u % 2, k * P:(k + 1) * P], ident[:, :])
                                elif kind == "pv":
                                    _, hh, c = step
                                    tail_step = [s for s in steps if s[0] == "t" and units[s[1]] == (hh, 4 * c + 3)][-1]
                                    pe.wait_ge(bank_free, i * USES + (use_of(tail_step) + 1 + RING))
                                    if (hh, c) == (0, 0):
                                        pe.wait_ge(zeroed, 2)
                                    for k in range(4 * c + 4):
                                        q0 = max(0, k - 4 * c) * P
                                        if k == T - 1:
                                            q0 = 256
                                        last = mm3(pe, bank[:, q0:HALF], [x[:, k, hh * DN:(hh + 1) * DN] for x in V],
                                                   [x[:, k, q0:HALF] for x in PT], k == 0, k == 4 * c + 3)
                                elif kind == "wo":
                                    t = step[1]
                                    if t == 0:
                                        pe.wait_ge(split_done["o"], i + 2)
                                        pe.wait_ge(bank_free, i * USES + (use_of(("pv", HP - 1, 1)) + 1 + RING))
                                    for hh in range(HP):
                                        last = mm3(pe, bank, [x[:, hh, t * P:(t + 1) * P] for x in oT],
                                                   [x[:, hh, :] for x in wo2], hh == 0, hh == HP - 1)
                                if kind in ring_kinds:
                                    last.then_inc(bank_full, 1)

                    @block.scalar
                    def _(act):
                        act.sem_inc(exp_done, 2)
                        act.sem_inc(hi_done, SPLITS)
                        with act.Fori(0, TURNS) as i:
                            use = 0
                            for step in steps:
                                kind = step[0]
                                if kind == "s":
                                    u = step[1]
                                    n = (units[u][1] + 1) * P
                                    act.wait_ge(shift_ready, i * N_UNITS + (u + 1))
                                    prev = [s for s in steps if s[0] == "t" and s[1] == (u - 2) % N_UNITS][-1]
                                    turn_back = 1 if u < 2 else 0
                                    act.wait_ge(bank_full, i * USES + (use_of(prev) + 1 + (1 - turn_back) * USES))
                                    sbank = ps[:, 2 * (u % 2):2 * (u % 2) + 2, :].rearrange("p b n -> p (b n)")
                                    act.activation(prob[:, u % 2, 0:n], sbank[:, 0:n], ACT.Exp,
                                                   bias=shift[:, u % 2:u % 2 + 1], scale=SCALE,
                                                   accum_out=total[:, u % 2:u % 2 + 1]).then_inc(exp_done, 1)
                                elif kind in ring_kinds:
                                    bank = ps[:, 4 + use % RING, :]
                                    use += 1
                                    if kind == "wo":
                                        continue
                                    act.wait_ge(bank_full, i * USES + (use + USES))
                                    if kind == "t":
                                        _, u, k0, k1 = step
                                        hh, qt = units[u]
                                        if qt % 4 == 0 and k0 == 0:
                                            before = (hh, 0) if qt == 4 else (hh - 1, 1)
                                            if before[0] < 0:
                                                act.wait_ge(bank_full, i * USES + (use_of(("pv", HP - 1, 1)) + 1))
                                            else:
                                                act.wait_ge(bank_full, i * USES + (use_of(("pv", *before)) + 1 + USES))
                                    src, dst = split_views(step)
                                    act.activation(dst[0], src(bank), ACT.Copy).then_inc(hi_done, 1)

                    @block.vector
                    def _(dve):
                        dve.sem_inc(bank_free, RING)
                        dve.sem_inc(scaled, 2)
                        for part in PT:
                            dve.memset(part[:, T - 1, 256:384].bitcast(F32), 0.0).then_inc(zeroed, 1)
                        with dve.Fori(0, TURNS) as i:
                            use = split = 0
                            for step in steps:
                                kind = step[0]
                                if kind == "s":
                                    u = step[1]
                                    n = (units[u][1] + 1) * P
                                    dve.wait_ge(scores_full, i * N_UNITS + (u + 1))
                                    sbank = ps[:, 2 * (u % 2):2 * (u % 2) + 2, :].rearrange("p b n -> p (b n)")
                                    dve.tensor_reduce(top[:, u % 2:u % 2 + 1], sbank[:, 0:n], AX.X, ALU.max)\
                                       .then_inc(top_found, 1)
                                    dve.wait_ge(top_found, i * N_UNITS + (u + 1))
                                    dve.tensor_scalar(shift[:, u % 2:u % 2 + 1], top[:, u % 2:u % 2 + 1], -SCALE, None,
                                                      ALU.mult).then_inc(shift_ready, 1)
                                elif kind == "n":
                                    u = step[1]
                                    n = (units[u][1] + 1) * P
                                    dve.wait_ge(exp_done, i * N_UNITS + (u + 1 + 2))
                                    dve.reciprocal(share[:, u % 2:u % 2 + 1], total[:, u % 2:u % 2 + 1]).then_inc(share_found, 1)
                                    dve.wait_ge(share_found, i * N_UNITS + (u + 1))
                                    dve.tensor_scalar(prob[:, u % 2, 0:n], prob[:, u % 2, 0:n], share[:, u % 2:u % 2 + 1],
                                                      None, ALU.mult).then_inc(scaled, 1)
                                elif kind in ring_kinds:
                                    bank = ps[:, 4 + use % RING, :]
                                    use += 1
                                    if kind == "wo":
                                        t = step[1]
                                        dve.wait_ge(bank_full, i * USES + (use + USES))
                                        dve.tensor_tensor(x_res[:, t, :], x_res[:, t, :], bank, ALU.add).then_inc(bank_free, 1)
                                    else:
                                        split += 1
                                        dve.wait_ge(hi_done, i * SPLITS + (split + SPLITS))
                                        src, dst = split_views(step)
                                        dve.tensor_tensor(dst[1], src(bank), dst[0].bitcast(F32), ALU.subtract)\
                                           .then_inc(bank_free, 1)

        def lora_ffn(tag):
            E, R, SCALE = 4, 8, 1.0
            ER = E * R
            GA = E + ER
            RING = 4
            with ExitStack() as st:
                up_nat = sb(st, f"up_nat{tag}", [P, C, D])
                ga_nat = sb(st, f"ga_nat{tag}", [GA, D])
                lb_nat = sb(st, f"lb_nat{tag}", [P, C, E, R])
                e_bias = sb(st, f"e_bias{tag}", [P, E])
                upT = [sb(st, f"upT_{part}{tag}", [P, C, D], F32R) for part in ("hi", "lo")]
                gaT = [sb(st, f"gaT_{part}{tag}", [P, C, GA], F32R) for part in ("hi", "lo")]
                lbT = [sb(st, f"lbT_{part}{tag}", [ER, D], F32R) for part in ("hi", "lo")]
                lzT = sb(st, f"lzT{tag}", [GA, S])
                lz = sb(st, f"lz{tag}", [P, T, GA])
                logits = sb(st, f"logits{tag}", [P, T * E])
                z = sb(st, f"z{tag}", [P, T, ER])
                zT = [sb(st, f"zT_{part}{tag}", [ER, S], F32R) for part in ("hi", "lo")]
                before = sb(st, f"before{tag}", [P, E, E])
                gt = sb(st, f"gt{tag}", [P, T * E * E])
                eq = sb(st, f"eq{tag}", [P, T * E * E])
                mask = sb(st, f"mask{tag}", [P, T * E])
                loaded = sem(st, f"l_loaded{tag}")
                pool_step = sem(st, f"l_pool_step{tag}")
                full = sem(st, f"l_bank_full{tag}")
                hi_done = sem(st, f"l_hi_done{tag}")
                free = sem(st, f"l_bank_free{tag}")
                dve_step = sem(st, f"l_dve_step{tag}")
                lz_ready = sem(st, f"lz_ready{tag}")
                z_ready = sem(st, f"z_ready{tag}")
                uses = [("ga", 0), ("lb", 0)] + [("up", c) for c in range(C)] + [("lzT", 0), ("lzT", 1), ("lz", 0)] \
                    + [("z", 0), ("z", 1)] + [("y", t) for t in range(T)]
                at = {u: n for n, u in enumerate(uses)}
                SPLITS = [u for u in uses if u[0] in ("ga", "lb", "up", "z")]
                bank_of = {u: ps[:, n % RING, :] for u, n in at.items()}

                def split_of(u):
                    b = bank_of[u]
                    kind, k = u
                    if kind == "ga":
                        return b[:, 0:C * GA].rearrange("p (c n) -> p c n", c=C), [a[:, :, :] for a in gaT]
                    if kind == "lb":
                        return b[0:ER, :], [a[:, :] for a in lbT]
                    if kind == "up":
                        return b, [a[:, k, :] for a in upT]
                    return b[0:ER, :], [a[:, k * HALF:(k + 1) * HALF] for a in zT]

                with nc.Block() as block:
                    @block.sync
                    def _(sp):
                        sp.dma_start(ga_nat[0:E, :], gate_w).then_inc(loaded, 16)
                        sp.dma_start(ga_nat[E:GA, :], lora_a.rearrange("e r h -> (e r) h")).then_inc(loaded, 16)
                        for c in range(C):
                            sp.dma_start(lb_nat[:, c, :, :], lora_b[:, c * P:(c + 1) * P, :].rearrange("e p r -> p e r"))\
                              .then_inc(loaded, 16)
                        sp.dma_start(e_bias[:, :], expert_bias.partition_broadcast(P)).then_inc(loaded, 16)
                        sp.dma_start(up_nat[:, :, :], w_up.rearrange("(c p) h -> p c h", p=P)).then_inc(loaded, 16)

                    @block.gpsimd
                    def _(pool):
                        pool.memset(before[:, :, :], 1.0).then_inc(pool_step, 1)
                        pool.wait_ge(pool_step, 1)
                        pool.affine_select(out=before[:, :, :], in_=before[:, :, :], compare_op=ALU.is_gt, fill=0.0,
                                           base=0, pattern=[[1, E], [-1, E]], channel_multiplier=0)\
                            .then_inc(pool_step, 1)

                    @block.tensor
                    def _(pe):
                        pe.wait_ge(loaded, 16 * 8)
                        for n, u in enumerate(uses):
                            kind, k = u
                            b = bank_of[u]
                            if n >= RING:
                                pe.wait_ge(free, n - RING + 1)
                            if kind == "ga":
                                for c in range(C):
                                    last = pe.transpose(b[:, c * GA:(c + 1) * GA], ga_nat[:, c * P:(c + 1) * P],
                                                        ident[0:GA, 0:GA])
                            elif kind == "lb":
                                for c in range(C):
                                    last = pe.transpose(b[0:ER, c * P:(c + 1) * P],
                                                        lb_nat[:, c, :, :].rearrange("p e r -> p (e r)"), ident[:, :])
                            elif kind == "up":
                                for o in range(C):
                                    last = pe.transpose(b[:, o * P:(o + 1) * P], up_nat[:, o, k * P:(k + 1) * P],
                                                        ident[:, :])
                            elif kind == "lzT":
                                pe.wait_ge(free, at[("ga", 0)] + 1)
                                for c in range(C):
                                    last = mm3(pe, b[0:GA, :], [a[:, c, :] for a in gaT],
                                               xn_cols(c, k * HALF, (k + 1) * HALF), c == 0, c == C - 1)
                            elif kind == "lz":
                                pe.wait_ge(free, at[("lzT", 1)] + 1)
                                for t in range(T):
                                    last = pe.transpose(b[:, t * GA:(t + 1) * GA], lzT[:, t * P:(t + 1) * P],
                                                        ident[0:GA, 0:GA])
                            elif kind == "z":
                                pe.wait_ge(z_ready, 1)
                                for t in range(4):
                                    last = pe.transpose(b[0:ER, t * P:(t + 1) * P], z[:, 4 * k + t, :], ident[:, :])
                            elif kind == "y":
                                if k == 0:
                                    pe.wait_ge(free, at[("z", 1)] + 1)
                                for c in range(C):
                                    mm3(pe, b, xn_cols(c, k * P, (k + 1) * P), [a[:, c, :] for a in upT], c == 0, False)
                                last = mm3(pe, b, [a[:, k * P:(k + 1) * P] for a in zT], [a[:, :] for a in lbT],
                                           False, True)
                            last.then_inc(full, 1)

                    @block.scalar
                    def _(act):
                        for u in SPLITS:
                            act.wait_ge(full, at[u] + 1)
                            src, dst = split_of(u)
                            act.activation(dst[0], src, ACT.Copy).then_inc(hi_done, 1)

                    @block.vector
                    def _(dve):
                        for n, u in enumerate(uses):
                            kind, k = u
                            b = bank_of[u]
                            if u in SPLITS:
                                dve.wait_ge(hi_done, SPLITS.index(u) + 1)
                                src, dst = split_of(u)
                                dve.tensor_tensor(dst[1], src, dst[0].bitcast(F32), ALU.subtract).then_inc(free, 1)
                            elif kind == "lzT":
                                dve.wait_ge(full, n + 1)
                                dve.tensor_copy(lzT[:, k * HALF:(k + 1) * HALF], b[0:GA, :]).then_inc(free, 1)
                            elif kind == "lz":
                                dve.wait_ge(full, n + 1)
                                dve.tensor_copy(lz[:, :, :], b[:, 0:T * GA].rearrange("p (t n) -> p t n", n=GA))\
                                   .then_inc(free, 1)
                                dve.wait_ge(free, n + 1)
                                dve.wait_ge(loaded, 16 * 8)
                                dve.tensor_tensor(logits[:, :].rearrange("p (t e) -> p t e", e=E), lz[:, :, 0:E],
                                                  e_bias[:, :].unsqueeze(1).to_broadcast([P, T, E]), ALU.add)\
                                   .then_inc(dve_step, 1)
                                dve.wait_ge(pool_step, 2)
                                m = rank_mask(dve, dve_step, 1, logits[:, :], mask[:, :], gt[:, :], eq[:, :],
                                              before[:, :, :], E, 1, SCALE)
                                dve.wait_ge(dve_step, m)
                                dve.tensor_tensor(z[:, :, :].rearrange("p t (e r) -> p t e r", r=R),
                                                  lz[:, :, E:GA].rearrange("p t (e r) -> p t e r", r=R),
                                                  mask[:, :].rearrange("p (t e) -> p t e", e=E).unsqueeze(3)
                                                  .to_broadcast([P, T, E, R]), ALU.mult).then_inc(z_ready, 1)
                            elif kind == "y":
                                dve.wait_ge(full, n + 1)
                                dve.scalar_tensor_tensor(x_res[:, k, :], b, 0.5, x_res[:, k, :], ALU.mult, ALU.add)\
                                   .then_inc(free, 1)

        class Tally:

            def __init__(self, semaphore, per_turn, unit=1):
                self.sem, self.per, self.unit = semaphore, per_turn, unit

            def start(self, eng):
                eng.sem_inc(self.sem, self.per * self.unit)

            def wait(self, eng, turn, n):
                assert -self.per <= n < self.per, (n, self.per)
                eng.wait_ge(self.sem, turn * (self.per * self.unit) + (self.per + n + 1) * self.unit)

            def mark(self, instruction):
                return instruction.then_inc(self.sem, self.unit)

        def mamba(tag):
            H, PD, N, G, K = 64, 64, 128, 8, 4
            I = H * PD
            HG = H // G
            GW = HG * PD
            CT = (I + 2 * G * N) // P
            Q = S // P
            with ExitStack() as st:
                dt = sb(st, "dt", [P, Q, H])
                a = sb(st, "a", [P, Q, H])
                grown = sb(st, "grown", [P, Q, H])
                through = sb(st, "through", [P, Q, H])
                to_end = sb(st, "to_end", [P, Q, H])
                upto = sb(st, "upto", [P, P])
                after = sb(st, "after", [P, P])
                mean_row = sb(st, "mean_row", [P, P])
                conv_w = sb(st, "conv_w", [P, CT, K])
                conv_b = sb(st, "conv_b", [P, CT])
                d_col = sb(st, "d_col", [P, I // P])
                nw_col = sb(st, "nw_col", [P, I // P])

                with ExitStack() as pre:
                    wdt_nat = sb(pre, "wdt_nat", [H, D])
                    wdtT = [sb(pre, f"wdtT_{part}", [P, C, H], F32R) for part in ("hi", "lo")]
                    dtT = sb(pre, "dtT", [H, S])
                    dt_b = sb(pre, "dt_b", [P, H])
                    alog = sb(pre, "alog", [P, H])
                    rate = sb(pre, "rate", [P, H])
                    ones = sb(pre, "ones", [P, P])
                    v, mag, u, w, lnw, zero, dec = [sb(pre, f"sp_{n}", [P, Q * H]) for n in ("v", "mag", "u", "w", "lnw", "zero", "dec")]
                    loaded = sem(pre, "m_loaded")
                    pool_step = sem(pre, "m_pool_step")
                    consts = sem(pre, "m_consts")
                    pe_step = sem(pre, "m_pe_step")
                    act_step = sem(pre, "m_act_step")
                    dve_step = sem(pre, "m_dve_step")
                    flat = "p q h -> p (q h)"
                    with nc.Block() as block:
                        @block.sync
                        def _(sp):
                            sp.dma_start(wdt_nat[:, :], in_proj_w[2 * I + 2 * G * N:2 * I + 2 * G * N + H, :]).then_inc(loaded, 16)
                            sp.dma_start(dt_b[:, :], dt_bias.partition_broadcast(P)).then_inc(loaded, 16)
                            sp.dma_start(alog[:, :], a_log.partition_broadcast(P)).then_inc(loaded, 16)
                            with nc.allow_non_contiguous_dma("per-channel vectors, loaded once"):
                                sp.dma_start(conv_w[:, :, :], conv_weight.rearrange("(j p) k -> p j k", p=P)).then_inc(loaded, 16)
                                sp.dma_start(conv_b[:, :], conv_bias.rearrange("(j p) -> p j", p=P)).then_inc(loaded, 16)
                                sp.dma_start(nw_col[:, :], norm_weight.rearrange("(j p) -> p j", p=P)).then_inc(loaded, 16)
                                for k in range(P // PD):
                                    sp.dma_start(d_col[k * PD:(k + 1) * PD, :],
                                                 d_skip.rearrange("(j k) -> k j", k=P // PD)[k].partition_broadcast(PD))\
                                      .then_inc(loaded, 16)

                        @block.gpsimd
                        def _(pool):
                            for m in (upto, after, ones):
                                pool.memset(m[:, :], 1.0).then_inc(pool_step, 1)
                            pool.memset(mean_row[:, :], 1.0 / GW).then_inc(pool_step, 1)
                            pool.wait_ge(pool_step, 4)
                            pool.affine_select(out=upto[:, :], in_=upto[:, :], compare_op=ALU.is_ge, fill=0.0, base=0,
                                               pattern=[[1, P]], channel_multiplier=-1).then_inc(consts, 1)
                            pool.affine_select(out=after[:, :], in_=after[:, :], compare_op=ALU.is_gt, fill=0.0, base=0,
                                               pattern=[[-1, P]], channel_multiplier=1).then_inc(consts, 1)

                        @block.tensor
                        def _(pe):
                            pe.wait_ge(loaded, 16 * 8)
                            for c in range(C):
                                last = pe.transpose(ps[:, 0, c * H:(c + 1) * H], wdt_nat[:, c * P:(c + 1) * P],
                                                    ident[0:H, 0:H])
                            last.then_inc(pe_step, 1)
                            pe.wait_ge(dve_step, 1)
                            for h in range(2):
                                for c in range(C):
                                    last = mm3(pe, ps[0:H, 1 + h, :], [x[:, c, :] for x in wdtT],
                                               xn_cols(c, h * HALF, (h + 1) * HALF), c == 0, c == C - 1)
                            last.then_inc(pe_step, 1)
                            pe.wait_ge(act_step, 2)
                            for t in range(T):
                                last = pe.transpose(ps[:, 3, t * H:(t + 1) * H], dtT[:, t * P:(t + 1) * P],
                                                    ident[0:H, 0:H])
                            last.then_inc(pe_step, 1)
                            pe.wait_ge(consts, 2)
                            pe.wait_ge(dve_step, 13)
                            for b, m in ((4, upto), (5, ones), (6, after)):
                                last = pe.matmul(ps[:, b, :], m[:, :], a[:, :, :].rearrange(flat), start=True, stop=True)
                            last.then_inc(pe_step, 1)

                        @block.scalar
                        def _(act):
                            act.wait_ge(pe_step, 1)
                            act.activation(wdtT[0][:, :, :], ps[:, 0, 0:C * H].rearrange("p (c n) -> p c n", c=C), ACT.Copy)\
                               .then_inc(act_step, 1)
                            act.wait_ge(pe_step, 2)
                            act.activation(dtT[:, :].rearrange("p (h n) -> p h n", h=2), ps[0:H, 1:3, :], ACT.Copy)\
                               .then_inc(act_step, 1)
                            act.wait_ge(dve_step, 3)
                            act.activation(u[:, :], mag[:, :], ACT.Exp, scale=-1.0).then_inc(act_step, 1)
                            act.activation(rate[:, :], alog[:, :], ACT.Exp).then_inc(act_step, 1)
                            act.wait_ge(dve_step, 4)
                            act.activation(lnw[:, :], w[:, :], ACT.Ln).then_inc(act_step, 1)
                            act.wait_ge(pe_step, 4)
                            for b, dst in ((4, grown[:, :, :].rearrange(flat)), (5, through[:, :, :].rearrange(flat)), (6, dec[:, :])):
                                act.activation(dst, ps[:, b, :], ACT.Exp).then_inc(act_step, 1)

                        @block.vector
                        def _(dve):
                            dve.wait_ge(act_step, 1)
                            dve.tensor_tensor(wdtT[1][:, :, :], ps[:, 0, 0:C * H].rearrange("p (c n) -> p c n", c=C),
                                              wdtT[0][:, :, :].bitcast(F32), ALU.subtract).then_inc(dve_step, 1)
                            dve.wait_ge(pe_step, 3)
                            dve.wait_ge(loaded, 16 * 8)
                            vq = v[:, :].rearrange("p (q h) -> p q h", h=H)
                            dt_flat = dt[:, :, :].rearrange(flat)
                            n = 1

                            def then(instruction):
                                nonlocal n
                                instruction.then_inc(dve_step, 1)
                                n += 1
                                dve.wait_ge(dve_step, n)

                            then(dve.tensor_tensor(vq, ps[:, 3, :].rearrange("p (q h) -> p q h", h=H),
                                                   dt_b[:, :].unsqueeze(1).to_broadcast([P, Q, H]), ALU.add))
                            then(dve.scalar_tensor_tensor(mag[:, :], v[:, :], -1.0, v[:, :], ALU.mult, ALU.max))
                            dve.wait_ge(act_step, 4)
                            then(dve.tensor_scalar(w[:, :], u[:, :], 1.0, None, ALU.add))
                            then(dve.tensor_scalar(zero[:, :], w[:, :], 1.0, None, ALU.is_equal))
                            dve.wait_ge(act_step, 5)
                            then(dve.tensor_tensor(lnw[:, :], lnw[:, :], zero[:, :], ALU.add))
                            then(dve.tensor_tensor(lnw[:, :], lnw[:, :], u[:, :], ALU.mult))
                            then(dve.scalar_tensor_tensor(w[:, :], w[:, :], -1.0, zero[:, :], ALU.add, ALU.add))
                            then(dve.reciprocal(mag[:, :], w[:, :]))
                            then(dve.tensor_tensor(lnw[:, :], lnw[:, :], mag[:, :], ALU.mult))
                            then(dve.scalar_tensor_tensor(dt_flat, v[:, :], 0.0, lnw[:, :], ALU.max, ALU.add))
                            then(dve.scalar_tensor_tensor(a[:, :, :], dt[:, :, :], -1.0,
                                                          rate[:, :].unsqueeze(1).to_broadcast([P, Q, H]), ALU.mult, ALU.mult))
                            then(dve.tensor_scalar(a[:, :, :].rearrange(flat), a[:, :, :].rearrange(flat), -1e30, None, ALU.max))
                            dve.wait_ge(act_step, 8)
                            then(dve.tensor_tensor(to_end[:, :, :].rearrange(flat), dec[:, :], dt_flat, ALU.mult))

                NATS, NB, RING = 14, 4, 4
                nat = [sb(st, f"nat{k}", [P, D]) for k in range(NB)]
                WT = [[sb(st, f"WT{k}_{part}", [P, C, P], F32R) for part in ("hi", "lo")] for k in range(2)]
                WOT = [sb(st, f"WOT_{part}", [P, C, D], F32R) for part in ("hi", "lo")]
                gate = sb(st, "gate", [P, 4, S])
                XT = sb(st, "XT", [P, 6, S])
                raw = sb(st, "conv_raw", [P, K - 1 + S])
                acc = sb(st, "conv_acc", [P, S])
                X = sb(st, "X", [P, 2, GW])
                B = sb(st, "B", [P, 2, N])
                xdt = sb(st, "xdt", [P, GW])
                xend = sb(st, "xend", [P, GW])
                steps_a = sb(st, "steps_a", [P, HG, P])
                E = sb(st, "decay", [P, 2, HG, P])
                Gm = sb(st, "Gm", [P, 2, P])
                carried = sb(st, "carried", [P, GW])
                state = sb(st, "state", [P, GW])
                yT = sb(st, "yT", [P, 4, HALF])
                var = sb(st, "m_var", [P, HALF])
                rs = sb(st, "m_rs", [P, HALF])
                tmp = sb(st, "m_tmp", [P, HALF])
                yn = [sb(st, f"yn_{part}", [P, 4, HALF], F32R) for part in ("hi", "lo")]

                squares = [acc[:, 0:HALF], acc[:, HALF:S], raw[:, K - 1:K - 1 + HALF], raw[:, K - 1 + HALF:K - 1 + S]]

                steps = [("nat", 0)]
                for j in range(10):
                    steps.append(("nat", j + 1))
                    steps += [("proj", j, 0), ("proj", j, 1)]
                steps += [("nat", 11), ("nat", 12), ("nat", 13)]

                def prepare(c):
                    return [("xc", c), ("bc", c), ("dec", c, 0), ("dec", c, 1), ("g", c)]

                steps += prepare(0)
                for c in range(Q):
                    if c + 1 < Q:
                        steps += prepare(c + 1)
                    if c:
                        steps.append(("in", c))
                    if c + 1 < Q:
                        steps.append(("st", c))
                    if c == 4:
                        steps += [("out", 0, t) for t in range(4)]
                    steps.append(("y", c))
                    if c % 4 == 3:
                        steps.append(("ss", c // 4))
                steps += [("out", 1, t) for t in range(4)]
                ring_of = {"proj": "a", "xc": "a", "bc": "a", "dec": "a"}
                order = {"a": [s for s in steps if ring_of.get(s[0], "v") == "a"],
                         "v": [s for s in steps if ring_of.get(s[0], "v") == "v"]}
                at = {s: n for r in order.values() for n, s in enumerate(r)}

                def bank_of(s):
                    r = ring_of.get(s[0], "v")
                    return ps[:, (0 if r == "a" else 4) + at[s] % RING, :]

                def use_before(s):
                    n, per = at[s], len(order[ring_of.get(s[0], "v")])
                    return n - RING if n >= RING else max(m for m in range(per) if m % RING == n % RING) - per

                full = {r: Tally(sem(st, f"full_{r}"), len(order[r])) for r in "av"}
                free = {r: Tally(sem(st, f"free_{r}"), len(order[r])) for r in "av"}
                nat_loaded = [Tally(sem(st, f"nat_loaded{k}"), len(range(k, NATS, NB)), 16) for k in range(NB)]
                nat_hi = Tally(sem(st, "nat_hi"), NATS)
                taps = Tally(sem(st, "taps"), 6 * (K - 1))
                raw_copied = Tally(sem(st, "raw_copied"), 12)
                silu_done = Tally(sem(st, "silu_done"), 6)
                steps_a_ready = Tally(sem(st, "steps_a_ready"), Q)
                x_scaled = Tally(sem(st, "x_scaled"), 2 * Q)
                mixed = Tally(sem(st, "mixed"), Q)
                state_kept = Tally(sem(st, "state_kept"), Q - 2)
                squared = Tally(sem(st, "squared"), 8)
                log_done = Tally(sem(st, "m_log_done"), 2)
                root_done = Tally(sem(st, "m_root_done"), 2)
                rs_step = Tally(sem(st, "m_rs_step"), 6)
                gated = Tally(sem(st, "m_gated"), 8)
                scaled = Tally(sem(st, "m_scaled"), 2)
                yn_hi = Tally(sem(st, "yn_hi"), 2)
                yn_lo = Tally(sem(st, "yn_lo"), 2)
                zeroed = sem(st, "m_zeroed")
                tallies = {
                    "pe": [full["a"], full["v"]],
                    "act": [free["a"], nat_hi, raw_copied, silu_done, squared, log_done, root_done, yn_hi],
                    "dve": [free["v"], taps, mixed, state_kept, rs_step, gated, scaled],
                    "pool": [steps_a_ready, x_scaled, yn_lo],
                }
                bc8 = [P, HG, PD]

                def heads(t):
                    return t.rearrange("p (h d) -> p h d", h=HG)

                def of_group(t, i, c):
                    return t[:, c, bass.ds(i * HG, HG)]

                def nat_dst(n):
                    if n < 10:
                        return lambda b: b.rearrange("p (c n) -> p c n", c=C), [x[:, :, :] for x in WT[n % 2]]
                    k = n - 10
                    return lambda b: b.rearrange("p (c n) -> p c n", c=C), [x[:, :, k * P:(k + 1) * P] for x in WOT]

                with nc.Block() as block:
                    @block.sync
                    def _(sp):
                        with sp.Fori(0, G) as i:
                            for n in range(NATS):
                                for m in {9: (10,), 10: ()}.get(n, (n,)):
                                    full["v"].wait(sp, i, at[("nat", m - NB)] if m >= NB else
                                                   at[("nat", [x for x in range(NATS) if x % NB == m % NB][-1])] - len(order["v"]))
                                if n < 4:
                                    src = in_proj_w[bass.ds(i * GW + n * P, P), :]
                                elif n < 8:
                                    src = in_proj_w[bass.ds(i * GW + (I + (n - 4) * P), P), :]
                                elif n < 10:
                                    src = in_proj_w[bass.ds(i * N + (2 * I + (n - 8) * G * N), P), :]
                                else:
                                    src = out_proj_w[(n - 10) * P:(n - 9) * P, bass.ds(i * GW, GW)]
                                nat_loaded[n % NB].mark(sp.dma_start(nat[n % NB][:, :], src))

                    @block.tensor
                    def _(pe):
                        for x in tallies["pe"]:
                            x.start(pe)
                        with pe.Fori(0, G) as i:
                            for s in steps:
                                kind, k = s[0], s[1]
                                r = ring_of.get(kind, "v")
                                free[r].wait(pe, i, use_before(s))
                                b = bank_of(s)
                                if kind == "nat":
                                    pe.wait_ge(nat_loaded[k % NB].sem, i * (nat_loaded[k % NB].per * 16) + (k // NB + 1) * 16)
                                    for c in range(C):
                                        last = pe.transpose(b[:, c * P:(c + 1) * P], nat[k % NB][:, c * P:(c + 1) * P],
                                                            ident[:, :])
                                elif kind == "proj":
                                    free["v"].wait(pe, i, at[("nat", k)])
                                    for c in range(C):
                                        last = mm3(pe, b, [x[:, c, :] for x in WT[k % 2]],
                                                   xn_cols(c, s[2] * HALF, (s[2] + 1) * HALF), c == 0, c == C - 1)
                                elif kind == "xc":
                                    silu_done.wait(pe, i, 5)
                                    for j in range(4):
                                        last = pe.transpose(b[:, j * P:(j + 1) * P], XT[:, j, k * P:(k + 1) * P], ident[:, :])
                                elif kind == "bc":
                                    last = pe.transpose(b[:, 0:P], XT[:, 4, k * P:(k + 1) * P], ident[:, :])
                                elif kind == "dec":
                                    steps_a_ready.wait(pe, i, k)
                                    last = pe.matmul(b, after[:, :],
                                                     steps_a[:, 4 * s[2]:4 * s[2] + 4, :].rearrange("p h t -> p (h t)"),
                                                     start=True, stop=True, skip_group_check=True)
                                elif kind == "g":
                                    cols = slice(k * P, (k + 1) * P)
                                    last = pe.matmul(b[:, 0:P], XT[:, 4, cols], XT[:, 5, cols], start=True, stop=True,
                                                     skip_group_check=True)
                                elif kind == "in":
                                    free["v"].wait(pe, i, at[("st", k - 1)])
                                    last = pe.matmul(b, XT[:, 5, k * P:(k + 1) * P], state[:, :], start=True, stop=True,
                                                     skip_group_check=True)
                                elif kind == "st":
                                    x_scaled.wait(pe, i, 2 * k + 1)
                                    free["a"].wait(pe, i, at[("bc", k)])
                                    last = pe.matmul(b, B[:, k % 2, :], xend[:, :], start=True, stop=True,
                                                     skip_group_check=True)
                                elif kind == "y":
                                    mixed.wait(pe, i, k)
                                    x_scaled.wait(pe, i, 2 * k)
                                    if k:
                                        free["v"].wait(pe, i, at[("in", k)])
                                    for j in range(4):
                                        cols = b[:, j * P:(j + 1) * P]
                                        for m in range(2):
                                            h = 2 * j + m
                                            last = pe.matmul(cols[m * PD:(m + 1) * PD, :], xdt[:, h * PD:(h + 1) * PD],
                                                             E[:, k % 2, h, :], start=True, stop=(k == 0),
                                                             skip_group_check=True)
                                        if k:
                                            last = pe.matmul(cols, carried[:, j * P:(j + 1) * P], ident[:, :],
                                                             start=False, stop=True, skip_group_check=True)
                                elif kind == "ss":
                                    for j in range(4):
                                        squared.wait(pe, i, 4 * k + j)
                                        last = pe.matmul(b, mean_row[:, :], squares[j], start=(j == 0), stop=(j == 3),
                                                         skip_group_check=True)
                                elif kind == "out":
                                    yn_lo.wait(pe, i, k)
                                    t = s[2]
                                    for j in range(4):
                                        last = mm3(pe, b, [x[:, j, t * P:(t + 1) * P] for x in yn],
                                                   [x[:, j, :] for x in WOT], j == 0, j == 3)
                                full[r].mark(last)

                    @block.scalar
                    def _(act):
                        for x in tallies["act"]:
                            x.start(act)
                        with act.Fori(0, G) as i:
                            for s in steps:
                                kind, k = s[0], s[1]
                                b = bank_of(s)
                                if kind in ring_of:
                                    full["a"].wait(act, i, at[s])
                                if kind == "nat":
                                    full["v"].wait(act, i, at[s])
                                    if k < 10:
                                        if k >= 2:
                                            full["a"].wait(act, i, at[("proj", k - 2, 1)])
                                    elif k == 10:
                                        full["v"].wait(act, i, at[("out", 1, 3)] - len(order["v"]))
                                    src, dst = nat_dst(k)
                                    nat_hi.mark(act.activation(dst[0], src(b), ACT.Copy))
                                elif kind == "proj" and k < 4:
                                    free["a"].mark(act.activation(gate[:, k, s[2] * HALF:(s[2] + 1) * HALF], b, ACT.Silu))
                                elif kind == "proj":
                                    j, h = k - 4, s[2]
                                    ct = i * 4 + j if j < 4 else i + (I // P + (j - 4) * G)
                                    cols = slice(h * HALF, (h + 1) * HALF)
                                    if h == 0:
                                        taps.wait(act, i, (K - 1) * j - 1)
                                        silu_done.wait(act, i, j - 1)
                                        if j == 0:
                                            full["v"].wait(act, i, at[("ss", 1)] - len(order["v"]))
                                    raw_copied.mark(act.activation(raw[:, K - 1 + h * HALF:K - 1 + (h + 1) * HALF], b, ACT.Copy))
                                    free["a"].mark(act.activation(acc[:, cols], b, ACT.Identity,
                                                                  scale=conv_w[:, bass.ds(ct, 1), K - 1],
                                                                  bias=conv_b[:, bass.ds(ct, 1)]))
                                    if h == 1:
                                        taps.wait(act, i, (K - 1) * (j + 1) - 1)
                                        silu_done.mark(act.activation(XT[:, j, :], acc[:, :], ACT.Silu))
                                elif kind == "xc":
                                    x_scaled.wait(act, i, 2 * (k - 2) + 1)
                                    free["a"].mark(act.activation(X[:, k % 2, :], b, ACT.Copy))
                                elif kind == "bc":
                                    if k >= 2:
                                        full["v"].wait(act, i, at[("st", k - 2)])
                                    free["a"].mark(act.activation(B[:, k % 2, :], b[:, 0:P], ACT.Copy))
                                elif kind == "dec":
                                    if k >= 2 and s[2] == 0:
                                        full["v"].wait(act, i, at[("y", k - 2)])
                                    free["a"].mark(act.activation(
                                        E[:, k % 2, 4 * s[2]:4 * s[2] + 4, :].rearrange("p h t -> p (h t)"), b, ACT.Exp))
                                elif kind == "ss":
                                    free["v"].wait(act, i, at[("y", 4 * k + 3)])
                                    silu_done.wait(act, i, 5)
                                    if k:
                                        full["v"].wait(act, i, at[("ss", k - 1)])
                                    for j in range(4):
                                        squared.mark(act.activation(squares[j], yT[:, j, :], ACT.Square))
                                    free["v"].wait(act, i, at[("ss", k)])
                                    log_done.mark(act.activation(tmp[:, :], var[:, :], ACT.Ln))
                                    log_done.wait(act, i, k)
                                    root_done.mark(act.activation(rs[:, :], tmp[:, :], ACT.Exp, scale=-0.5))
                                    scaled.wait(act, i, k)
                                    full["v"].wait(act, i, at[("out", 0, 3)] if k else at[("out", 1, 3)] - len(order["v"]))
                                    yn_hi.mark(act.activation(yn[0][:, :, :], yT[:, :, :], ACT.Copy))

                    @block.gpsimd
                    def _(pool):
                        for x in tallies["pool"]:
                            x.start(pool)
                        pool.memset(raw[:, 0:K - 1], 0.0).then_inc(zeroed, 1)
                        with pool.Fori(0, G) as i:
                            for s in steps:
                                kind, k = s[0], s[1]
                                if kind == "dec" and s[2] == 0:
                                    full["a"].wait(pool, i, at[("dec", k - 1, 1)] if k else at[("dec", Q - 1, 1)] - len(order["a"]))
                                    steps_a_ready.mark(pool.tensor_tensor(
                                        steps_a[:, :, :], upto[:, :].unsqueeze(1).to_broadcast([P, HG, P]),
                                        of_group(a, i, k).unsqueeze(2).to_broadcast([P, HG, P]), ALU.mult))
                                elif kind == "g":
                                    c = k
                                    free["a"].wait(pool, i, at[("xc", c)])
                                    if c:
                                        full["v"].wait(pool, i, at[("y", c - 1)])
                                    else:
                                        full["v"].wait(pool, i, at[("y", Q - 1)] - len(order["v"]))
                                    x_scaled.mark(pool.tensor_tensor(heads(xdt[:, :]), heads(X[:, c % 2, :]),
                                                                     of_group(dt, i, c).unsqueeze(2).to_broadcast(bc8), ALU.mult))
                                    x_scaled.mark(pool.tensor_tensor(heads(xend[:, :]), heads(X[:, c % 2, :]),
                                                                     of_group(to_end, i, c).unsqueeze(2).to_broadcast(bc8), ALU.mult))
                                elif kind == "ss":
                                    yn_hi.wait(pool, i, k)
                                    yn_lo.mark(pool.tensor_tensor(yn[1][:, :, :], yT[:, :, :], yn[0][:, :, :].bitcast(F32),
                                                                  ALU.subtract))

                    @block.vector
                    def _(dve):
                        for x in tallies["dve"]:
                            x.start(dve)
                        dve.wait_ge(zeroed, 1)
                        with dve.Fori(0, G) as i:
                            for s in steps:
                                kind, k = s[0], s[1]
                                b = bank_of(s)
                                if kind not in ring_of and kind != "nat":
                                    full["v"].wait(dve, i, at[s])
                                if kind == "nat":
                                    nat_hi.wait(dve, i, k)
                                    src, dst = nat_dst(k)
                                    free["v"].mark(dve.tensor_tensor(dst[1], src(b), dst[0].bitcast(F32), ALU.subtract))
                                elif kind == "proj" and k >= 4 and s[2] == 1:
                                    j = k - 4
                                    ct = i * 4 + j if j < 4 else i + (I // P + (j - 4) * G)
                                    free["a"].wait(dve, i, at[s])
                                    for m in range(K - 1):
                                        if m:
                                            taps.wait(dve, i, (K - 1) * j + m - 1)
                                        taps.mark(dve.scalar_tensor_tensor(
                                            acc[:, :], raw[:, m:m + S], conv_w[:, bass.ds(ct, 1), m], acc[:, :],
                                            ALU.mult, ALU.add))
                                elif kind == "g":
                                    free["v"].mark(dve.tensor_tensor(Gm[:, k % 2, :], b[:, 0:P], upto[:, :], ALU.mult))
                                    free["v"].wait(dve, i, at[s])
                                    free["a"].wait(dve, i, at[("dec", k, 1)])
                                    mixed.mark(dve.tensor_tensor(E[:, k % 2, :, :], E[:, k % 2, :, :],
                                                                 Gm[:, k % 2, :].unsqueeze(1).to_broadcast([P, HG, P]), ALU.mult))
                                elif kind == "in":
                                    if k >= 2:
                                        full["v"].wait(dve, i, at[("y", k - 1)])
                                    free["v"].mark(dve.tensor_tensor(heads(carried[:, :]), heads(b),
                                                                     of_group(grown, i, k).unsqueeze(2).to_broadcast(bc8), ALU.mult))
                                elif kind == "st":
                                    if k == 0:
                                        free["v"].mark(dve.tensor_copy(state[:, :], b))
                                    else:
                                        state_kept.mark(dve.tensor_tensor(heads(state[:, :]), heads(state[:, :]),
                                                                          of_group(through, i, k).unsqueeze(2).to_broadcast(bc8), ALU.mult))
                                        state_kept.wait(dve, i, k - 1)
                                        free["v"].mark(dve.tensor_tensor(state[:, :], state[:, :], b, ALU.add))
                                elif kind == "y":
                                    c = k
                                    if c % 4 == 0:
                                        yn_lo.wait(dve, i, c // 4 - 1)
                                    for j in range(4):
                                        o = (c % 4) * P
                                        ins = dve.scalar_tensor_tensor(yT[:, j, o:o + P], XT[:, j, c * P:(c + 1) * P],
                                                                       d_col[:, bass.ds(i * 4 + j, 1)], b[:, j * P:(j + 1) * P],
                                                                       ALU.mult, ALU.add)
                                    free["v"].mark(ins)
                                elif kind == "ss":
                                    free["v"].mark(dve.tensor_scalar(var[:, :], b, EPS, None, ALU.add))
                                    for j in range(4):
                                        gated.mark(dve.scalar_tensor_tensor(yT[:, j, :], yT[:, j, :], nw_col[:, bass.ds(i * 4 + j, 1)],
                                                                            gate[:, j, k * HALF:(k + 1) * HALF], ALU.mult, ALU.mult))
                                    root_done.wait(dve, i, k)
                                    rs_step.mark(dve.tensor_tensor(tmp[:, :], rs[:, :], rs[:, :], ALU.mult))
                                    rs_step.wait(dve, i, 3 * k)
                                    rs_step.mark(dve.scalar_tensor_tensor(tmp[:, :], tmp[:, :], -0.5, var[:, :], ALU.mult, ALU.mult))
                                    rs_step.wait(dve, i, 3 * k + 1)
                                    rs_step.mark(dve.scalar_tensor_tensor(rs[:, :], tmp[:, :], 1.5, rs[:, :], ALU.add, ALU.mult))
                                    rs_step.wait(dve, i, 3 * k + 2)
                                    scaled.mark(dve.tensor_tensor(yT[:, :, :], yT[:, :, :],
                                                                  rs[:, :].unsqueeze(1).to_broadcast([P, 4, HALF]), ALU.mult))
                                elif kind == "out":
                                    t = 4 * k + s[2]
                                    free["v"].mark(dve.tensor_tensor(x_res[:, t, :], x_res[:, t, :], b, ALU.add))

        steps = [("f0a", experts_ffn), ("at0", attention), ("f0b", experts_ffn),
                 ("f1a", lora_ffn), ("ssm", mamba), ("f1b", lora_ffn)]
        for tag, stage in [steps[n] for n in stages]:
            layer_norm(tag)
            stage(tag)

        with ExitStack() as st:
            stored = sem(st, "out_stored")
            with nc.Block() as block:
                @block.sync
                def _(sp):
                    sp.dma_start(out.rearrange("a (t p) d -> p (a t) d", p=P), x_res[:, :, :]).then_inc(stored, 16)
                    sp.wait_ge(stored, 16)


_INS = ['L0_attn_hidden_states', 'L0_attn_wq', 'L0_attn_wkv', 'L0_attn_wo', 'L0_ffn_W_gate', 'L0_ffn_b_gate',
        'L0_ffn_W_e', 'L0_ffn_b_e', 'L1_attn_in_proj_w', 'L1_attn_conv_weight', 'L1_attn_conv_bias',
        'L1_attn_dt_bias', 'L1_attn_A_log', 'L1_attn_D', 'L1_attn_norm_weight', 'L1_attn_out_proj_w',
        'L1_ffn_W_up', 'L1_ffn_gate_w', 'L1_ffn_expert_bias', 'L1_ffn_lora_A', 'L1_ffn_lora_B']
_STAGES = range(6)


def kernel(**inputs):
    import numpy as _np
    import concourse.bacc as _bacc
    from concourse import mybir as _mybir
    from concourse.bass_utils import run_bass_kernel_spmd as _run

    nc = _bacc.Bacc("TRN2", target_bir_lowering=False, num_devices=1)
    arrays, args = {}, []
    for name in _INS:
        a = _np.ascontiguousarray(inputs[name])
        arrays[f"in_{name}_dram"] = a
        args.append(nc.dram_tensor(f"in_{name}_dram", a.shape, _mybir.dt.from_np(a.dtype), kind="ExternalInput").ap())
    out = nc.dram_tensor("out_0_dram", (1, S, D), _mybir.dt.float32, kind="ExternalOutput").ap()
    build(nc, _STAGES, *args, out)
    r = _run(nc, [arrays], core_ids=[0])
    return r.results[0]["out_0_dram"]
```

```python
import concourse.bass as bass
from concourse import mybir
from contextlib import ExitStack

F32 = mybir.dt.float32
F32R = mybir.dt.float32r
BF16 = mybir.dt.bfloat16
ALU = mybir.AluOpType
ACT = mybir.ActivationFunctionType
AX = mybir.AxisListType

P = 128
D = 512
S = 1024
T = S // P
C = D // P
HALF = 512
EPS = 1e-5


def build(nc, stages, hidden, wq, wkv, wo, w_gate, b_gate, w_e, b_e, in_proj_w, conv_weight, conv_bias,
          dt_bias, a_log, d_skip, norm_weight, out_proj_w, w_up, gate_w, expert_bias, lora_a, lora_b, out):
    whole = ExitStack()
    with whole:
        def sb(stack, name, shape, dtype=F32):
            return stack.enter_context(nc.sbuf_tensor(name, shape, dtype))

        def sem(stack, name):
            return stack.enter_context(nc.semaphore(name))

        x_res = sb(whole, "x_res", [P, T, D])
        xnT_hi = sb(whole, "xnT_hi", [P, C, S], F32R)
        xnT_lo = sb(whole, "xnT_lo", [P, C, S], F32R)
        ident = sb(whole, "ident", [P, P])
        zero_col = sb(whole, "zero_col", [P, 1])
        minus_half = sb(whole, "minus_half", [P, 1])
        ps = whole.enter_context(nc.psum_tensor("ps", [P, 8, HALF], F32))

        def mm3(pe, out, lhs, rhs, first, last):
            pe.matmul(out, lhs[0], rhs[0], start=first, stop=False, skip_group_check=True)
            pe.matmul(out, lhs[0], rhs[1], start=False, stop=False, skip_group_check=True)
            return pe.matmul(out, lhs[1], rhs[0], start=False, stop=last, skip_group_check=True)

        def xn_cols(c, a, b):
            return xnT_hi[:, c, a:b], xnT_lo[:, c, a:b]

        with ExitStack() as st:
            x_loaded = sem(st, "x_loaded")
            ident_zeroed = sem(st, "ident_zeroed")
            with nc.Block() as block:
                @block.sync
                def _(sp):
                    src = hidden.rearrange("a (t p) d -> p (a t) d", p=P)
                    sp.dma_start(x_res[:, :, :], src).then_inc(x_loaded, 16)
                    sp.wait_ge(x_loaded, 16)

                @block.gpsimd
                def _(pool):
                    pool.memset(zero_col[:, :], 0.0)
                    pool.memset(minus_half[:, :], -0.5)
                    pool.memset(ident[:, :], 0.0).then_inc(ident_zeroed, 1)
                    pool.wait_ge(ident_zeroed, 1)
                    pool.affine_select(out=ident[:, :], in_=ident[:, :], compare_op=ALU.not_equal, fill=1.0,
                                       base=0, pattern=[[-1, P]], channel_multiplier=1)

        def inverse_root(dve, step, n0, r, root, v, tmp):
            dve.reciprocal(r, root).then_inc(step, 1)
            dve.wait_ge(step, n0 + 1)
            dve.tensor_tensor(tmp, r, r, ALU.mult).then_inc(step, 1)
            dve.wait_ge(step, n0 + 2)
            dve.tensor_tensor(tmp, tmp, v, ALU.mult).then_inc(step, 1)
            dve.wait_ge(step, n0 + 3)
            dve.tensor_scalar(tmp, tmp, -0.5, 1.5, ALU.mult, ALU.add).then_inc(step, 1)
            dve.wait_ge(step, n0 + 4)
            dve.tensor_tensor(r, r, tmp, ALU.mult).then_inc(step, 1)

        def layer_norm(tag):
            with ExitStack() as st:
                stats = sb(st, f"stats{tag}", [P, T, 6])
                mean_var = sb(st, f"mean_var{tag}", [P, T, 2])
                rstd = sb(st, f"rstd{tag}", [P, T])
                xn = sb(st, f"xn{tag}", [P, T, D])
                dve_step = sem(st, f"ln_dve_step{tag}")
                xn_ready = sem(st, f"xn_ready{tag}")
                turned = sem(st, f"xn_turned{tag}")
                hi_done = sem(st, f"xn_hi_done{tag}")
                lo_done = sem(st, f"xn_lo_done{tag}")
                var = sb(st, f"var{tag}", [P, T])
                root = sb(st, f"root{tag}", [P, T])
                r2v = sb(st, f"r2v{tag}", [P, T])
                var_ready = sem(st, f"var_ready{tag}")
                root_ready = sem(st, f"root_ready{tag}")
                banks = 4
                with nc.Block() as block:
                    @block.vector
                    def _(dve):
                        for t in range(T):
                            dve.bn_stats(stats[:, t, :], x_res[:, t, :]).then_inc(dve_step, 1)
                        for t in range(T):
                            dve.wait_ge(dve_step, t + 1)
                            dve.bn_aggr(mean_var[:, t, :], stats[:, t, :]).then_inc(dve_step, 1)
                        dve.wait_ge(dve_step, 2 * T)
                        dve.tensor_scalar(var[:, :], mean_var[:, :, 1], EPS, None, ALU.add).then_inc(var_ready, 1)
                        dve.wait_ge(root_ready, 1)
                        inverse_root(dve, dve_step, 2 * T, rstd[:, :], root[:, :], var[:, :], r2v[:, :])
                        dve.wait_ge(dve_step, 2 * T + 5)
                        for t in range(T):
                            dve.tensor_scalar(xn[:, t, :], x_res[:, t, :], mean_var[:, t, 0:1],
                                              rstd[:, t:t + 1], ALU.subtract, ALU.mult).then_inc(xn_ready, 1)
                        for t in range(T):
                            dve.wait_ge(hi_done, t + 1)
                            cols = slice(t * P, (t + 1) * P)
                            dve.tensor_tensor(xnT_lo[:, :, cols],
                                              ps[:, t % banks, :].rearrange("p (c n) -> p c n", c=C),
                                              xnT_hi[:, :, cols].bitcast(F32), ALU.subtract).then_inc(lo_done, 1)

                    @block.tensor
                    def _(pe):
                        for t in range(T):
                            pe.wait_ge(xn_ready, t + 1)
                            if t >= banks:
                                pe.wait_ge(lo_done, t - banks + 1)
                            for c in range(C):
                                last = pe.transpose(ps[:, t % banks, c * P:(c + 1) * P],
                                                    xn[:, t, c * P:(c + 1) * P], ident[:, :])
                            last.then_inc(turned, 1)

                    @block.scalar
                    def _(act):
                        act.wait_ge(var_ready, 1)
                        act.activation(root[:, :], var[:, :], ACT.Sqrt).then_inc(root_ready, 1)
                        for t in range(T):
                            act.wait_ge(turned, t + 1)
                            act.activation(xnT_hi[:, :, t * P:(t + 1) * P],
                                           ps[:, t % banks, :].rearrange("p (c n) -> p c n", c=C),
                                           ACT.Copy).then_inc(hi_done, 1)

        def rank_mask(dve, step, n0, logits, mask, gt, eq, before, E, K, scale):
            shape = [P, T, E, E]
            rival = logits.rearrange("p (t j) -> p t j", j=E).unsqueeze(2).to_broadcast(shape)
            own = logits.rearrange("p (t e) -> p t e", e=E).unsqueeze(3).to_broadcast(shape)
            v = [a.rearrange("p (t e j) -> p t e j", e=E, j=E) for a in (gt, eq)]
            for k, ins in enumerate((
                lambda: dve.tensor_tensor(v[0], rival, own, ALU.is_gt),
                lambda: dve.tensor_tensor(v[1], rival, own, ALU.is_equal),
                lambda: dve.tensor_tensor(v[1], v[1], before.unsqueeze(1).to_broadcast(shape), ALU.mult),
                lambda: dve.tensor_tensor(v[0], v[0], v[1], ALU.add),
                lambda: dve.tensor_reduce(mask, v[0].rearrange("p t e j -> p (t e) j"), AX.X, ALU.add),
                lambda: dve.tensor_scalar(mask, mask, K - 0.5, scale, ALU.is_lt, ALU.mult),
            )):
                dve.wait_ge(step, n0 + k)
                ins().then_inc(step, 1)
            return n0 + 6

        def experts_ffn(tag):
            E, K, SCALE, RING = 8, 2, 0.25, 4
            with ExitStack() as st:
                w_raw = sb(st, f"ew_raw{tag}", [P, 2, C, D])
                w_hi = [sb(st, f"ew_hi{k}{tag}", [P, C, D], F32R) for k in range(2)]
                w_lo = [sb(st, f"ew_lo{k}{tag}", [P, C, D], F32R) for k in range(2)]
                b_raw = sb(st, f"eb_raw{tag}", [2, E, D])
                b_hi = sb(st, f"eb_hi{tag}", [2, E, D], F32R)
                b_two = sb(st, f"eb_two{tag}", [2, E, D], F32R)
                row_neg = sb(st, f"row_neg{tag}", [2, 1])
                ones_raw = sb(st, f"ones_raw{tag}", [2, P])
                ones_two = sb(st, f"ones_two{tag}", [2, P], F32R)
                g_raw = sb(st, f"g_raw{tag}", [P, C, E])
                g_hi = sb(st, f"g_hi{tag}", [P, C, E], F32R)
                g_lo = sb(st, f"g_lo{tag}", [P, C, E], F32R)
                g_bias = sb(st, f"g_bias{tag}", [P, E])
                logitsT = sb(st, f"logitsT{tag}", [E, S])
                logits = sb(st, f"logits{tag}", [P, T * E])
                before = sb(st, f"before{tag}", [P, E, E])
                gt = sb(st, f"gt{tag}", [P, T * E * E])
                eq = sb(st, f"eq{tag}", [P, T * E * E])
                mask = sb(st, f"mask{tag}", [P, T * E])
                relu = sb(st, f"relu{tag}", [P, 2, D])
                small_loaded = sem(st, f"e_small_loaded{tag}")
                w_loaded = [sem(st, f"ew_loaded{k}{tag}") for k in range(2)]
                w_split = sem(st, f"ew_split{tag}")
                pool_step = sem(st, f"e_pool_step{tag}")
                hi_step = sem(st, f"ew_hi_step{tag}")
                consts_ready = sem(st, f"e_consts{tag}")
                dve_step = sem(st, f"e_dve_step{tag}")
                logitsT_ready = sem(st, f"logitsT_ready{tag}")
                logitsT_copied = sem(st, f"logitsT_copied{tag}")
                logits_turned = sem(st, f"logits_turned{tag}")
                mask_ready = sem(st, f"mask_ready{tag}")
                y_ready = sem(st, f"ey_ready{tag}")
                relu_done = sem(st, f"relu_done{tag}")
                added = sem(st, f"e_added{tag}")
                with nc.Block() as block:
                    @block.sync
                    def _(sp):
                        sp.dma_start(g_raw[:, :, :], w_gate.rearrange("(c p) e -> p c e", p=P)).then_inc(small_loaded, 16)
                        sp.dma_start(g_bias[:, :], b_gate.partition_broadcast(P)).then_inc(small_loaded, 16)
                        sp.dma_start(b_raw[:, :, :], b_e.partition_broadcast(2)).then_inc(small_loaded, 16)
                        with sp.Fori(0, E // 2) as i:
                            for k in range(2):
                                sp.wait_ge(w_split, i * 2 + (k + 1))
                                sp.dma_start(w_raw[:, k, :, :],
                                             w_e[bass.ds(i * 2 + k, 1)].rearrange("e (c p) h -> p (e c) h", p=P))\
                                  .then_inc(w_loaded[k], 16)

                    @block.gpsimd
                    def _(pool):
                        pool.sem_inc(w_split, 2)
                        pool.memset(before[:, :, :], 1.0).then_inc(pool_step, 1)
                        pool.memset(row_neg[:, :], 0.0).then_inc(pool_step, 1)
                        pool.memset(ones_raw[:, :], 1.0).then_inc(pool_step, 1)
                        pool.wait_ge(pool_step, 3)
                        pool.affine_select(out=before[:, :, :], in_=before[:, :, :], compare_op=ALU.is_gt, fill=0.0,
                                           base=0, pattern=[[1, E], [-1, E]], channel_multiplier=0)\
                            .then_inc(consts_ready, 1)
                        pool.affine_select(out=row_neg[:, :], in_=row_neg[:, :], compare_op=ALU.not_equal, fill=-1.0,
                                           base=-1, pattern=[[0, 1]], channel_multiplier=1).then_inc(consts_ready, 1)
                        pool.tensor_copy(ones_two[:, :], ones_raw[:, :]).then_inc(consts_ready, 1)
                        with pool.Fori(0, E // 2) as i:
                            for k in range(2):
                                pool.wait_ge(w_loaded[k], (i + 1) * 16)
                                pool.wait_ge(y_ready, i * 2 * T + (k + 1) * T)
                                pool.tensor_tensor(w_hi[k][:, :, :], w_raw[:, k, :, :],
                                                   zero_col[:, :].unsqueeze(2).to_broadcast([P, C, D]), ALU.add).then_inc(hi_step, 1)
                                pool.wait_ge(hi_step, i * 2 + (k + 1))
                                pool.tensor_tensor(w_lo[k][:, :, :], w_raw[:, k, :, :], w_hi[k][:, :, :].bitcast(F32),
                                                   ALU.subtract).then_inc(w_split, 1)

                    @block.tensor
                    def _(pe):
                        pe.sem_inc(y_ready, 2 * T)
                        pe.wait_ge(dve_step, 2)
                        for h in range(2):
                            for c in range(C):
                                rhs = xn_cols(c, h * HALF, (h + 1) * HALF)
                                last = mm3(pe, ps[0:E, h, :], (g_hi[:, c, :], g_lo[:, c, :]), rhs, c == 0, c == C - 1)
                        last.then_inc(logitsT_ready, 1)
                        pe.wait_ge(logitsT_copied, 1)
                        for t in range(T):
                            last = pe.transpose(ps[:, 2, t * E:(t + 1) * E], logitsT[:, t * P:(t + 1) * P],
                                                ident[0:E, 0:E])
                        last.then_inc(logits_turned, 1)
                        pe.wait_ge(dve_step, 4)
                        pe.wait_ge(consts_ready, 3)
                        with pe.Fori(0, E // 2) as i:
                            for k in range(2):
                                pe.wait_ge(w_split, i * 2 + (k + 3))
                                for t in range(T):
                                    n = k * T + t
                                    bank = ps[:, 4 + n % RING, :]
                                    pe.wait_ge(relu_done, i * 2 * T + (n + 1))
                                    for c in range(C):
                                        mm3(pe, bank, xn_cols(c, t * P, (t + 1) * P),
                                            (w_hi[k][:, c, :], w_lo[k][:, c, :]), c == 0, False)
                                    pe.matmul(bank, ones_two[:, :],
                                              b_two[:, bass.ds(i * 2 + k, 1), :].rearrange("p e d -> p (e d)"),
                                              start=False, stop=True, skip_group_check=True).then_inc(y_ready, 1)

                    @block.scalar
                    def _(act):
                        act.sem_inc(relu_done, RING)
                        act.wait_ge(logitsT_ready, 1)
                        act.activation(logitsT[:, :].rearrange("e (h n) -> e h n", h=2), ps[0:E, 0:2, :], ACT.Copy)\
                           .then_inc(logitsT_copied, 1)
                        act.wait_ge(mask_ready, 1)
                        with act.Fori(0, E // 2) as i:
                            for k in range(2):
                                for t in range(T):
                                    n = k * T + t
                                    act.wait_ge(y_ready, i * 2 * T + (n + 1 + 2 * T))
                                    act.wait_ge(added, i * 2 * T + (n + 1))
                                    act.activation(relu[:, n % 2, :], ps[:, 4 + n % RING, :], ACT.Relu,
                                                   scale=mask[:, bass.ds(i * 2 + (t * E + k), 1)])\
                                       .then_inc(relu_done, 1)

                    @block.vector
                    def _(dve):
                        dve.sem_inc(added, 2)
                        dve.wait_ge(small_loaded, 48)
                        dve.tensor_copy(g_hi[:, :, :], g_raw[:, :, :]).then_inc(dve_step, 1)
                        dve.wait_ge(dve_step, 1)
                        dve.tensor_tensor(g_lo[:, :, :], g_raw[:, :, :], g_hi[:, :, :].bitcast(F32), ALU.subtract)\
                           .then_inc(dve_step, 1)
                        dve.tensor_copy(b_hi[:, :, :], b_raw[:, :, :]).then_inc(dve_step, 1)
                        dve.wait_ge(dve_step, 3)
                        dve.wait_ge(consts_ready, 2)
                        dve.scalar_tensor_tensor(b_two[:, :, :], b_hi[:, :, :].bitcast(F32), row_neg[:, 0:1],
                                                 b_raw[:, :, :], ALU.mult, ALU.add).then_inc(dve_step, 1)
                        dve.wait_ge(logits_turned, 1)
                        dve.tensor_tensor(logits[:, :].rearrange("p (t e) -> p t e", e=E),
                                          ps[:, 2, 0:T * E].rearrange("p (t e) -> p t e", e=E),
                                          g_bias[:, :].unsqueeze(1).to_broadcast([P, T, E]), ALU.add)\
                           .then_inc(dve_step, 1)
                        n = rank_mask(dve, dve_step, 5, logits[:, :], mask[:, :], gt[:, :], eq[:, :],
                                      before[:, :, :], E, K, SCALE)
                        dve.wait_ge(dve_step, n)
                        dve.sem_inc(mask_ready, 1)
                        with dve.Fori(0, E // 2) as i:
                            for k in range(2):
                                for t in range(T):
                                    n = k * T + t
                                    dve.wait_ge(relu_done, i * 2 * T + (n + 1 + RING))
                                    dve.tensor_tensor(x_res[:, t, :], x_res[:, t, :], relu[:, n % 2, :], ALU.add)\
                                       .then_inc(added, 1)

        def attention(tag):
            H, DN, DQ, HP = 32, 128, 192, 2
            TURNS = H // HP
            SCALE = DQ ** -0.5
            RING = 4
            with ExitStack() as st:
                raw = {k: sb(st, f"a_raw_{k}", [P, 2 * D]) for k in ("q", "k", "v", "o")}
                w = {k: [sb(st, f"a_w{part}_{k}", [P, 2 * D], F32R) for part in ("hi", "lo")] for k in ("q", "k", "v", "o")}
                cols4 = "p (c n) -> p c n"
                wq2, wk2, wv2 = [[a[:, :].rearrange(cols4, c=C) for a in w[k]] for k in ("q", "k", "v")]
                wo2 = [a[:, :].rearrange("p (h n) -> p h n", h=HP) for a in w["o"]]
                qT = [sb(st, f"qT_{part}", [P, HP, S], F32R) for part in ("hi", "lo")]
                kT = [sb(st, f"kT_{part}", [P, HP, S], F32R) for part in ("hi", "lo")]
                V = [sb(st, f"V_{part}", [P, T, HP * DN], F32R) for part in ("hi", "lo")]
                prob = sb(st, "prob", [P, 2, S])
                PT = [sb(st, f"PT_{part}", [P, T, HALF], F32R) for part in ("hi", "lo")]
                oT = [sb(st, f"oT_{part}", [P, HP, S], F32R) for part in ("hi", "lo")]
                top = sb(st, "row_top", [P, 2])
                shift = sb(st, "row_shift", [P, 2])
                total = sb(st, "row_total", [P, 4])
                share = sb(st, "row_share", [P, 4])
                share_row = sb(st, "share_row", [P, HALF])
                o_norm = sb(st, "o_norm", [P, HALF])
                ident_bf = sb(st, "ident_bf", [P, P], BF16)
                later_f = sb(st, "later_f", [P, P])
                later = sb(st, "later_keys", [P, P], BF16)
                raw_loaded = {k: sem(st, f"a_loaded_{k}") for k in "qkvo"}
                split_done = {k: sem(st, f"a_split_{k}") for k in "qkvo"}
                hi_step = sem(st, "a_hi_step")
                pool_step = sem(st, "a_pool_step")
                consts = sem(st, "a_consts")
                zeroed = sem(st, "a_pt_zeroed")
                bank_full = sem(st, "a_bank_full")
                hi_done = sem(st, "a_hi_done")
                bank_free = sem(st, "a_bank_free")
                scores_full = sem(st, "scores_full")
                shift_ready = sem(st, "shift_ready")
                top_found = sem(st, "top_found")
                exp_done = sem(st, "exp_done")
                share_found = sem(st, "share_found")
                o_hi_done = sem(st, "o_hi_done")
                o_lo_done = sem(st, "o_lo_done")

                units = [(hh, qt) for hh in range(HP) for qt in range(T)]
                N_UNITS = len(units)
                head0 = [("qk", 0, m, h) for m in "qk" for h in range(2)]
                head1 = [("qk", 1, m, h) for m in "qk" for h in range(2)]
                beside = {0: [("v", 1)], 1: [("v", 2)], 2: [("v", 3)], 3: head1[0:2], 4: head1[2:3], 5: head1[3:],
                          N_UNITS - 1: [("wo", t) for t in range(3)]}
                steps = head0 + [("v", 0), ("s", 0), ("e", 0), ("s", 1), ("e", 1)]
                pending = []
                for u, (hh, qt) in enumerate(units):
                    steps += beside.get(u, [])
                    if u + 2 < N_UNITS:
                        steps.append(("s", u + 2))
                    for k0 in range(0, qt + 1, 4):
                        steps.append(("t", u, k0, min(k0 + 4, qt + 1)))
                    if u + 2 < N_UNITS:
                        steps.append(("e", u + 2))
                    steps += pending
                    pending = [("ol", *pending[1][1:])] if len(pending) == 2 else []
                    if qt % 4 == 3:
                        pending = [("sh", hh, qt // 4), ("pv", hh, qt // 4)]
                steps += pending + [("wo", 3), ("ol", HP - 1, 1)] + [("wo", t) for t in range(4, T)]
                ring_kinds = ("qk", "v", "t", "sh", "pv", "wo")
                USES = sum(s[0] in ring_kinds for s in steps)
                SPLITS = sum(s[0] in ("qk", "v", "t") for s in steps)

                assert USES % RING == 0

                def use_of(step):
                    return [s for s in steps if s[0] in ring_kinds].index(step)

                def split_of(step):
                    return [s for s in steps if s[0] in ("qk", "v", "t")].index(step)

                def pieces(qt):
                    n = max((qt + 1) * P, 256)
                    if n <= HALF:
                        return [(0, n)]
                    return [(0, HALF), (HALF, max(n, HALF + 256))]

                def split_views(step):
                    kind = step[0]
                    if kind == "qk":
                        _, hh, m, h = step
                        dst = qT if m == "q" else kT
                        return (lambda b: b[:, :]), [a[:, hh, h * HALF:(h + 1) * HALF] for a in dst]
                    if kind == "v":
                        k = step[1]
                        return (lambda b: b[:, :].rearrange("p (t n) -> p t n", t=2)), [a[:, 2 * k:2 * k + 2, :] for a in V]
                    _, u, k0, k1 = step
                    q0 = (units[u][1] % 4) * P
                    return (lambda b: b[:, 0:(k1 - k0) * P].rearrange("p (k n) -> p k n", n=P)), \
                        [a[:, k0:k1, q0:q0 + P] for a in PT]

                with nc.Block() as block:
                    @block.sync
                    def _(sp):
                        sp.wait_ge(consts, 1)
                        wq_v = wq.rearrange("(c p) (h e) -> p c h e", p=P, e=DQ)
                        wk_v = wkv[:, 0:H * DN].rearrange("(c p) (h e) -> p c h e", p=P, e=DN)
                        wv_v = wkv[:, H * DN:2 * H * DN].rearrange("(c p) (h e) -> p c h e", p=P, e=DN)
                        wo_v = wo.rearrange("(h p) n -> p h n", p=DN)
                        with sp.Fori(0, TURNS) as i:
                            for key, src in (("q", wq_v), ("k", wk_v), ("v", wv_v)):
                                sp.wait_ge(split_done[key], i + 1)
                                dst = raw[key][:, :].rearrange("p (c h e) -> p c h e", c=C, h=HP)
                                for c in range(C):
                                    sp.dma_start(dst[:, c], src[:, c, bass.ds(i * HP, HP), 0:DN]).then_inc(raw_loaded[key], 16)
                            sp.wait_ge(split_done["o"], i + 1)
                            sp.dma_start(raw["o"][:, :].rearrange("p (h n) -> p h n", h=HP),
                                         wo_v[:, bass.ds(i * HP, HP), :]).then_inc(raw_loaded["o"], 16)

                    @block.gpsimd
                    def _(pool):
                        for key in "qkvo":
                            pool.sem_inc(split_done[key], 1)
                        pool.memset(later_f[:, :], 0.0).then_inc(pool_step, 1)
                        pool.tensor_copy(ident_bf[:, :], ident[:, :]).then_inc(consts, 1)
                        pool.wait_ge(pool_step, 1)
                        pool.affine_select(out=later_f[:, :], in_=later_f[:, :], compare_op=ALU.is_ge, fill=-1e30,
                                           base=0, pattern=[[-1, P]], channel_multiplier=1).then_inc(pool_step, 1)
                        pool.wait_ge(pool_step, 2)
                        pool.tensor_copy(later[:, :], later_f[:, :]).then_inc(consts, 1)
                        last_use = {"q": use_of(("qk", 1, "q", 1)), "k": use_of(("qk", 1, "k", 1)),
                                    "v": use_of(("v", 3)), "o": use_of(("wo", T - 1))}
                        with pool.Fori(0, TURNS) as i:
                            for n, key in enumerate("qkvo"):
                                pool.wait_ge(raw_loaded[key], (i + 1) * (16 if key == "o" else 16 * C))
                                pool.wait_ge(bank_full, i * USES + (last_use[key] + 1))
                                hi, lo = w[key]
                                pool.tensor_tensor(hi[:, :], raw[key][:, :], zero_col[:, :].to_broadcast([P, 2 * D]), ALU.add).then_inc(hi_step, 1)
                                pool.wait_ge(hi_step, i * 4 + (n + 1))
                                pool.tensor_tensor(lo[:, :], raw[key][:, :], hi[:, :].bitcast(F32), ALU.subtract)\
                                    .then_inc(split_done[key], 1)

                    @block.tensor
                    def _(pe):
                        pe.sem_inc(bank_full, USES)
                        pe.wait_ge(consts, 2)
                        with pe.Fori(0, TURNS) as i:
                            use = 0
                            for step in steps:
                                kind = step[0]
                                if kind in ring_kinds:
                                    pe.wait_ge(bank_free, i * USES + (use + 1))
                                    bank = ps[:, 4 + use % RING, :]
                                    use += 1
                                if kind == "qk":
                                    _, hh, m, h = step
                                    if hh == 0 and h == 0:
                                        pe.wait_ge(split_done[m], i + 2)
                                    wt = wq2 if m == "q" else wk2
                                    for c in range(C):
                                        last = mm3(pe, bank, [a[:, c, hh * DN:(hh + 1) * DN] for a in wt],
                                                   xn_cols(c, h * HALF, (h + 1) * HALF), c == 0, c == C - 1)
                                elif kind == "v":
                                    if step[1] == 0:
                                        pe.wait_ge(split_done["v"], i + 2)
                                    for k in range(2):
                                        t = 2 * step[1] + k
                                        for c in range(C):
                                            last = mm3(pe, bank[:, k * 256:(k + 1) * 256], xn_cols(c, t * P, (t + 1) * P),
                                                       [a[:, c, :] for a in wv2], c == 0, c == C - 1)
                                elif kind == "s":
                                    u = step[1]
                                    hh, qt = units[u]
                                    pe.wait_ge(exp_done, i * N_UNITS + (u + 1))
                                    if qt == 0:
                                        pe.wait_ge(bank_free, i * USES + (use_of(("qk", hh, "k", 1)) + 1 + RING))
                                    sbank = ps[:, 2 * (u % 2):2 * (u % 2) + 2, :].rearrange("p b n -> p (b n)")
                                    q0 = qt * P
                                    for a, b in pieces(qt):
                                        mm3(pe, sbank[:, a:b], [x[:, hh, q0:q0 + P] for x in qT],
                                            [x[:, hh, a:b] for x in kT], True, False)
                                    last = pe.matmul(sbank[:, q0:q0 + P], ident_bf[:, :], later[:, :],
                                                     start=False, stop=True, skip_group_check=True)
                                    last.then_inc(scores_full, 1)
                                elif kind == "t":
                                    _, u, k0, k1 = step
                                    if k0 == 0:
                                        pe.wait_ge(exp_done, i * N_UNITS + (u + 1 + 2))
                                    for k in range(k0, k1):
                                        last = pe.transpose(bank[:, (k - k0) * P:(k - k0 + 1) * P],
                                                            prob[:, u % 2, k * P:(k + 1) * P], ident[:, :])
                                elif kind == "sh":
                                    _, hh, c = step
                                    pe.wait_ge(share_found, i * N_UNITS + (8 * hh + 4 * c + 4))
                                    for m in range(4):
                                        last = pe.transpose(bank[:, m * P:(m + 1) * P],
                                                            share[:, m:m + 1].to_broadcast([P, P]), ident[:, :])
                                elif kind == "pv":
                                    _, hh, c = step
                                    tail_step = [s for s in steps if s[0] == "t" and units[s[1]] == (hh, 4 * c + 3)][-1]
                                    pe.wait_ge(bank_free, i * USES + (use_of(tail_step) + 1 + RING))
                                    if (hh, c) == (0, 0):
                                        pe.wait_ge(zeroed, 2)
                                    for k in range(4 * c + 4):
                                        q0 = max(0, k - 4 * c) * P
                                        if k == T - 1:
                                            q0 = 256
                                        last = mm3(pe, bank[:, q0:HALF], [x[:, k, hh * DN:(hh + 1) * DN] for x in V],
                                                   [x[:, k, q0:HALF] for x in PT], k == 0, k == 4 * c + 3)
                                elif kind == "wo":
                                    t = step[1]
                                    if t == 0:
                                        pe.wait_ge(split_done["o"], i + 2)
                                    if t % 4 == 0:
                                        pe.wait_ge(o_lo_done, i * 4 + (3 + t // 4))
                                    for hh in range(HP):
                                        last = mm3(pe, bank, [x[:, hh, t * P:(t + 1) * P] for x in oT],
                                                   [x[:, hh, :] for x in wo2], hh == 0, hh == HP - 1)
                                if kind in ring_kinds:
                                    last.then_inc(bank_full, 1)

                    @block.scalar
                    def _(act):
                        act.sem_inc(exp_done, 2)
                        act.sem_inc(hi_done, SPLITS)
                        with act.Fori(0, TURNS) as i:
                            use = 0
                            for step in steps:
                                kind = step[0]
                                if kind == "e":
                                    u = step[1]
                                    n = (units[u][1] + 1) * P
                                    act.wait_ge(shift_ready, i * N_UNITS + (u + 1))
                                    prev = [s for s in steps if s[0] == "t" and s[1] == (u - 2) % N_UNITS][-1]
                                    turn_back = 1 if u < 2 else 0
                                    act.wait_ge(bank_full, i * USES + (use_of(prev) + 1 + (1 - turn_back) * USES))
                                    sbank = ps[:, 2 * (u % 2):2 * (u % 2) + 2, :].rearrange("p b n -> p (b n)")
                                    act.activation(prob[:, u % 2, 0:n], sbank[:, 0:n], ACT.Exp,
                                                   bias=shift[:, u % 2:u % 2 + 1], scale=SCALE,
                                                   accum_out=total[:, u % 4:u % 4 + 1]).then_inc(exp_done, 1)
                                elif kind in ring_kinds:
                                    bank = ps[:, 4 + use % RING, :]
                                    use += 1
                                    if kind == "pv":
                                        _, hh, c = step
                                        act.wait_ge(bank_free, i * USES + (use_of(step) + 1 + RING))
                                        if (hh, c) in ((0, 0), (0, 1)):
                                            act.wait_ge(bank_full, i * USES + (use_of(("wo", 4 * c + 3)) + 1))
                                        act.activation(oT[0][:, hh, c * HALF:(c + 1) * HALF], o_norm[:, :], ACT.Copy)\
                                           .then_inc(o_hi_done, 1)
                                    if kind not in ("qk", "v", "t"):
                                        continue
                                    act.wait_ge(bank_full, i * USES + (use + USES))
                                    if kind == "t":
                                        _, u, k0, k1 = step
                                        hh, qt = units[u]
                                        if qt % 4 == 0 and k0 == 0:
                                            before = (hh, 0) if qt == 4 else (hh - 1, 1)
                                            if before[0] < 0:
                                                act.wait_ge(bank_full, i * USES + (use_of(("pv", HP - 1, 1)) + 1))
                                            else:
                                                act.wait_ge(bank_full, i * USES + (use_of(("pv", *before)) + 1 + USES))
                                    src, dst = split_views(step)
                                    act.activation(dst[0], src(bank), ACT.Copy).then_inc(hi_done, 1)

                    @block.vector
                    def _(dve):
                        dve.sem_inc(bank_free, RING)
                        for part in PT:
                            dve.memset(part[:, T - 1, 256:384].bitcast(F32), 0.0).then_inc(zeroed, 1)
                        with dve.Fori(0, TURNS) as i:
                            use = split = 0
                            for step in steps:
                                kind = step[0]
                                if kind == "s":
                                    u = step[1]
                                    n = (units[u][1] + 1) * P
                                    dve.wait_ge(scores_full, i * N_UNITS + (u + 1))
                                    sbank = ps[:, 2 * (u % 2):2 * (u % 2) + 2, :].rearrange("p b n -> p (b n)")
                                    dve.tensor_reduce(top[:, u % 2:u % 2 + 1], sbank[:, 0:n], AX.X, ALU.max)\
                                       .then_inc(top_found, 1)
                                    dve.wait_ge(top_found, i * N_UNITS + (u + 1))
                                    dve.tensor_scalar(shift[:, u % 2:u % 2 + 1], top[:, u % 2:u % 2 + 1], -SCALE, None,
                                                      ALU.mult).then_inc(shift_ready, 1)
                                elif kind == "ol":
                                    _, hh, c = step
                                    dve.wait_ge(o_hi_done, i * 4 + (2 * hh + c + 1))
                                    cols = slice(c * HALF, (c + 1) * HALF)
                                    dve.tensor_tensor(oT[1][:, hh, cols], o_norm[:, :], oT[0][:, hh, cols].bitcast(F32),
                                                      ALU.subtract).then_inc(o_lo_done, 1)
                                elif kind in ring_kinds:
                                    bank = ps[:, 4 + use % RING, :]
                                    use += 1
                                    if kind == "wo":
                                        t = step[1]
                                        dve.wait_ge(bank_full, i * USES + (use + USES))
                                        dve.tensor_tensor(x_res[:, t, :], x_res[:, t, :], bank, ALU.add).then_inc(bank_free, 1)
                                    elif kind == "sh":
                                        dve.wait_ge(bank_full, i * USES + (use + USES))
                                        dve.tensor_copy(share_row[:, :], bank).then_inc(bank_free, 1)
                                    elif kind == "pv":
                                        _, hh, c = step
                                        dve.wait_ge(bank_full, i * USES + (use + USES))
                                        dve.wait_ge(bank_free, i * USES + (use_of(("sh", hh, c)) + 1 + RING))
                                        dve.tensor_tensor(o_norm[:, :], bank, share_row[:, :], ALU.mult).then_inc(bank_free, 1)
                                    else:
                                        if kind == "t" and step[2] == 0:
                                            _, u, k0, k1 = step
                                            dve.wait_ge(exp_done, i * N_UNITS + (u + 1 + 2))
                                            if units[u][1] % 4 == 0:
                                                before = [x for x in steps if x[0] == "sh" and 8 * x[1] + 4 * x[2] < u]
                                                dve.wait_ge(bank_full, i * USES + (use_of(before[-1]) + 1 + USES) if before
                                                            else i * USES + (use_of(("sh", HP - 1, 1)) + 1))
                                            dve.reciprocal(share[:, units[u][1] % 4:units[u][1] % 4 + 1],
                                                           total[:, u % 4:u % 4 + 1]).then_inc(share_found, 1)
                                        split += 1
                                        dve.wait_ge(hi_done, i * SPLITS + (split + SPLITS))
                                        src, dst = split_views(step)
                                        dve.tensor_tensor(dst[1], src(bank), dst[0].bitcast(F32), ALU.subtract)\
                                           .then_inc(bank_free, 1)

        def lora_ffn(tag):
            E, R, SCALE = 4, 8, 1.0
            ER = E * R
            GA = E + ER
            RING = 4
            with ExitStack() as st:
                up_nat = sb(st, f"up_nat{tag}", [P, C, D])
                ga_nat = sb(st, f"ga_nat{tag}", [GA, D])
                lb_nat = sb(st, f"lb_nat{tag}", [P, C, E, R])
                e_bias = sb(st, f"e_bias{tag}", [P, E])
                upT = [sb(st, f"upT_{part}{tag}", [P, C, D], F32R) for part in ("hi", "lo")]
                gaT = [sb(st, f"gaT_{part}{tag}", [P, C, GA], F32R) for part in ("hi", "lo")]
                lbT = [sb(st, f"lbT_{part}{tag}", [ER, D], F32R) for part in ("hi", "lo")]
                lzT = sb(st, f"lzT{tag}", [GA, S])
                lz = sb(st, f"lz{tag}", [P, T, GA])
                logits = sb(st, f"logits{tag}", [P, T * E])
                z = sb(st, f"z{tag}", [P, T, ER])
                zT = [sb(st, f"zT_{part}{tag}", [ER, S], F32R) for part in ("hi", "lo")]
                before = sb(st, f"before{tag}", [P, E, E])
                gt = sb(st, f"gt{tag}", [P, T * E * E])
                eq = sb(st, f"eq{tag}", [P, T * E * E])
                mask = sb(st, f"mask{tag}", [P, T * E])
                loaded = sem(st, f"l_loaded{tag}")
                pool_step = sem(st, f"l_pool_step{tag}")
                full = sem(st, f"l_bank_full{tag}")
                hi_done = sem(st, f"l_hi_done{tag}")
                free = sem(st, f"l_bank_free{tag}")
                dve_step = sem(st, f"l_dve_step{tag}")
                lz_ready = sem(st, f"lz_ready{tag}")
                z_ready = sem(st, f"z_ready{tag}")
                uses = [("ga", 0), ("lb", 0)] + [("up", c) for c in range(C)] + [("lzT", 0), ("lzT", 1), ("lz", 0)] \
                    + [("z", 0), ("z", 1)] + [("y", t) for t in range(T)]
                at = {u: n for n, u in enumerate(uses)}
                SPLITS = [u for u in uses if u[0] in ("ga", "lb", "up", "z")]
                bank_of = {u: ps[:, n % RING, :] for u, n in at.items()}

                def split_of(u):
                    b = bank_of[u]
                    kind, k = u
                    if kind == "ga":
                        return b[:, 0:C * GA].rearrange("p (c n) -> p c n", c=C), [a[:, :, :] for a in gaT]
                    if kind == "lb":
                        return b[0:ER, :], [a[:, :] for a in lbT]
                    if kind == "up":
                        return b, [a[:, k, :] for a in upT]
                    return b[0:ER, :], [a[:, k * HALF:(k + 1) * HALF] for a in zT]

                with nc.Block() as block:
                    @block.sync
                    def _(sp):
                        sp.dma_start(ga_nat[0:E, :], gate_w).then_inc(loaded, 16)
                        sp.dma_start(ga_nat[E:GA, :], lora_a.rearrange("e r h -> (e r) h")).then_inc(loaded, 16)
                        for c in range(C):
                            sp.dma_start(lb_nat[:, c, :, :], lora_b[:, c * P:(c + 1) * P, :].rearrange("e p r -> p e r"))\
                              .then_inc(loaded, 16)
                        sp.dma_start(e_bias[:, :], expert_bias.partition_broadcast(P)).then_inc(loaded, 16)
                        sp.dma_start(up_nat[:, :, :], w_up.rearrange("(c p) h -> p c h", p=P)).then_inc(loaded, 16)

                    @block.gpsimd
                    def _(pool):
                        pool.memset(before[:, :, :], 1.0).then_inc(pool_step, 1)
                        pool.wait_ge(pool_step, 1)
                        pool.affine_select(out=before[:, :, :], in_=before[:, :, :], compare_op=ALU.is_gt, fill=0.0,
                                           base=0, pattern=[[1, E], [-1, E]], channel_multiplier=0)\
                            .then_inc(pool_step, 1)

                    @block.tensor
                    def _(pe):
                        pe.wait_ge(loaded, 16 * 8)
                        for n, u in enumerate(uses):
                            kind, k = u
                            b = bank_of[u]
                            if n >= RING:
                                pe.wait_ge(free, n - RING + 1)
                            if kind == "ga":
                                for c in range(C):
                                    last = pe.transpose(b[:, c * GA:(c + 1) * GA], ga_nat[:, c * P:(c + 1) * P],
                                                        ident[0:GA, 0:GA])
                            elif kind == "lb":
                                for c in range(C):
                                    last = pe.transpose(b[0:ER, c * P:(c + 1) * P],
                                                        lb_nat[:, c, :, :].rearrange("p e r -> p (e r)"), ident[:, :])
                            elif kind == "up":
                                for o in range(C):
                                    last = pe.transpose(b[:, o * P:(o + 1) * P], up_nat[:, o, k * P:(k + 1) * P],
                                                        ident[:, :])
                            elif kind == "lzT":
                                pe.wait_ge(free, at[("ga", 0)] + 1)
                                for c in range(C):
                                    last = mm3(pe, b[0:GA, :], [a[:, c, :] for a in gaT],
                                               xn_cols(c, k * HALF, (k + 1) * HALF), c == 0, c == C - 1)
                            elif kind == "lz":
                                pe.wait_ge(free, at[("lzT", 1)] + 1)
                                for t in range(T):
                                    last = pe.transpose(b[:, t * GA:(t + 1) * GA], lzT[:, t * P:(t + 1) * P],
                                                        ident[0:GA, 0:GA])
                            elif kind == "z":
                                pe.wait_ge(z_ready, 1)
                                for t in range(4):
                                    last = pe.transpose(b[0:ER, t * P:(t + 1) * P], z[:, 4 * k + t, :], ident[:, :])
                            elif kind == "y":
                                if k == 0:
                                    pe.wait_ge(free, at[("z", 1)] + 1)
                                for c in range(C):
                                    mm3(pe, b, xn_cols(c, k * P, (k + 1) * P), [a[:, c, :] for a in upT], c == 0, False)
                                last = mm3(pe, b, [a[:, k * P:(k + 1) * P] for a in zT], [a[:, :] for a in lbT],
                                           False, True)
                            last.then_inc(full, 1)

                    @block.scalar
                    def _(act):
                        for u in SPLITS:
                            act.wait_ge(full, at[u] + 1)
                            src, dst = split_of(u)
                            act.activation(dst[0], src, ACT.Copy).then_inc(hi_done, 1)

                    @block.vector
                    def _(dve):
                        for n, u in enumerate(uses):
                            kind, k = u
                            b = bank_of[u]
                            if u in SPLITS:
                                dve.wait_ge(hi_done, SPLITS.index(u) + 1)
                                src, dst = split_of(u)
                                dve.tensor_tensor(dst[1], src, dst[0].bitcast(F32), ALU.subtract).then_inc(free, 1)
                            elif kind == "lzT":
                                dve.wait_ge(full, n + 1)
                                dve.tensor_copy(lzT[:, k * HALF:(k + 1) * HALF], b[0:GA, :]).then_inc(free, 1)
                            elif kind == "lz":
                                dve.wait_ge(full, n + 1)
                                dve.tensor_copy(lz[:, :, :], b[:, 0:T * GA].rearrange("p (t n) -> p t n", n=GA))\
                                   .then_inc(free, 1)
                                dve.wait_ge(free, n + 1)
                                dve.wait_ge(loaded, 16 * 8)
                                dve.tensor_tensor(logits[:, :].rearrange("p (t e) -> p t e", e=E), lz[:, :, 0:E],
                                                  e_bias[:, :].unsqueeze(1).to_broadcast([P, T, E]), ALU.add)\
                                   .then_inc(dve_step, 1)
                                dve.wait_ge(pool_step, 2)
                                m = rank_mask(dve, dve_step, 1, logits[:, :], mask[:, :], gt[:, :], eq[:, :],
                                              before[:, :, :], E, 1, SCALE)
                                dve.wait_ge(dve_step, m)
                                dve.tensor_tensor(z[:, :, :].rearrange("p t (e r) -> p t e r", r=R),
                                                  lz[:, :, E:GA].rearrange("p t (e r) -> p t e r", r=R),
                                                  mask[:, :].rearrange("p (t e) -> p t e", e=E).unsqueeze(3)
                                                  .to_broadcast([P, T, E, R]), ALU.mult).then_inc(z_ready, 1)
                            elif kind == "y":
                                dve.wait_ge(full, n + 1)
                                dve.scalar_tensor_tensor(x_res[:, k, :], b, 0.5, x_res[:, k, :], ALU.mult, ALU.add)\
                                   .then_inc(free, 1)

        class Tally:

            def __init__(self, semaphore, per_turn, unit=1):
                self.sem, self.per, self.unit = semaphore, per_turn, unit

            def start(self, eng):
                eng.sem_inc(self.sem, self.per * self.unit)

            def wait(self, eng, turn, n):
                assert -self.per <= n < self.per, (n, self.per)
                eng.wait_ge(self.sem, turn * (self.per * self.unit) + (self.per + n + 1) * self.unit)

            def mark(self, instruction):
                return instruction.then_inc(self.sem, self.unit)

        def mamba(tag):
            H, PD, N, G, K = 64, 64, 128, 8, 4
            I = H * PD
            HG = H // G
            GW = HG * PD
            CT = (I + 2 * G * N) // P
            Q = S // P
            with ExitStack() as st:
                dt = sb(st, "dt", [P, Q, H])
                a = sb(st, "a", [P, Q, H])
                grown = sb(st, "grown", [P, Q, H])
                through = sb(st, "through", [P, Q, H])
                to_end = sb(st, "to_end", [P, Q, H])
                upto = sb(st, "upto", [P, P])
                after = sb(st, "after", [P, P])
                after_r = sb(st, "after_r", [P, P], F32R)
                a_hi = sb(st, "a_hi", [P, Q, H], F32R)
                a_lo = sb(st, "a_lo", [P, Q, H], F32R)
                mean_col = sb(st, "mean_col", [P, 1])
                conv_w = sb(st, "conv_w", [P, CT, K])
                conv_b = sb(st, "conv_b", [P, CT])
                d_col = sb(st, "d_col", [P, I // P])
                nw_col = sb(st, "nw_col", [P, 4 + I // P])

                with ExitStack() as pre:
                    wdt_nat = sb(pre, "wdt_nat", [H, D])
                    wdtT = [sb(pre, f"wdtT_{part}", [P, C, H], F32R) for part in ("hi", "lo")]
                    dtT = sb(pre, "dtT", [H, S])
                    dt_b = sb(pre, "dt_b", [P, H])
                    alog = sb(pre, "alog", [P, H])
                    rate = sb(pre, "rate", [P, H])
                    ones = sb(pre, "ones", [P, P])
                    v, mag, u, w, lnw, zero, dec = [sb(pre, f"sp_{n}", [P, Q * H]) for n in ("v", "mag", "u", "w", "lnw", "zero", "dec")]
                    loaded = sem(pre, "m_loaded")
                    pool_step = sem(pre, "m_pool_step")
                    consts = sem(pre, "m_consts")
                    pe_step = sem(pre, "m_pe_step")
                    act_step = sem(pre, "m_act_step")
                    dve_step = sem(pre, "m_dve_step")
                    flat = "p q h -> p (q h)"
                    with nc.Block() as block:
                        @block.sync
                        def _(sp):
                            sp.dma_start(wdt_nat[:, :], in_proj_w[2 * I + 2 * G * N:2 * I + 2 * G * N + H, :]).then_inc(loaded, 16)
                            sp.dma_start(dt_b[:, :], dt_bias.partition_broadcast(P)).then_inc(loaded, 16)
                            sp.dma_start(alog[:, :], a_log.partition_broadcast(P)).then_inc(loaded, 16)
                            with nc.allow_non_contiguous_dma("per-channel vectors, loaded once"):
                                sp.dma_start(conv_w[:, :, :], conv_weight.rearrange("(j p) k -> p j k", p=P)).then_inc(loaded, 16)
                                sp.dma_start(conv_b[:, :], conv_bias.rearrange("(j p) -> p j", p=P)).then_inc(loaded, 16)
                                sp.dma_start(nw_col[:, 4:4 + I // P], norm_weight.rearrange("(j p) -> p j", p=P)).then_inc(loaded, 16)
                                for k in range(P // PD):
                                    sp.dma_start(d_col[k * PD:(k + 1) * PD, :],
                                                 d_skip.rearrange("(j k) -> k j", k=P // PD)[k].partition_broadcast(PD))\
                                      .then_inc(loaded, 16)

                        @block.gpsimd
                        def _(pool):
                            for m in (upto, after, ones):
                                pool.memset(m[:, :], 1.0).then_inc(pool_step, 1)
                            pool.memset(mean_col[:, :], 1.0 / GW).then_inc(pool_step, 1)
                            pool.memset(nw_col[:, 0:4], 0.0).then_inc(pool_step, 1)
                            pool.wait_ge(pool_step, 5)
                            pool.affine_select(out=upto[:, :], in_=upto[:, :], compare_op=ALU.is_ge, fill=0.0, base=0,
                                               pattern=[[1, P]], channel_multiplier=-1).then_inc(consts, 1)
                            pool.affine_select(out=after[:, :], in_=after[:, :], compare_op=ALU.is_gt, fill=0.0, base=0,
                                               pattern=[[-1, P]], channel_multiplier=1).then_inc(consts, 1)

                        @block.tensor
                        def _(pe):
                            pe.wait_ge(loaded, 16 * 8)
                            for c in range(C):
                                last = pe.transpose(ps[:, 0, c * H:(c + 1) * H], wdt_nat[:, c * P:(c + 1) * P],
                                                    ident[0:H, 0:H])
                            last.then_inc(pe_step, 1)
                            pe.wait_ge(dve_step, 1)
                            for h in range(2):
                                for c in range(C):
                                    last = mm3(pe, ps[0:H, 1 + h, :], [x[:, c, :] for x in wdtT],
                                               xn_cols(c, h * HALF, (h + 1) * HALF), c == 0, c == C - 1)
                            last.then_inc(pe_step, 1)
                            pe.wait_ge(act_step, 2)
                            for t in range(T):
                                last = pe.transpose(ps[:, 3, t * H:(t + 1) * H], dtT[:, t * P:(t + 1) * P],
                                                    ident[0:H, 0:H])
                            last.then_inc(pe_step, 1)
                            pe.wait_ge(consts, 2)
                            pe.wait_ge(dve_step, 13)
                            for b, m in ((4, upto), (5, ones), (6, after)):
                                last = pe.matmul(ps[:, b, :], m[:, :], a[:, :, :].rearrange(flat), start=True, stop=True)
                            last.then_inc(pe_step, 1)

                        @block.scalar
                        def _(act):
                            act.wait_ge(pe_step, 1)
                            act.activation(wdtT[0][:, :, :], ps[:, 0, 0:C * H].rearrange("p (c n) -> p c n", c=C), ACT.Copy)\
                               .then_inc(act_step, 1)
                            act.wait_ge(pe_step, 2)
                            act.activation(dtT[:, :].rearrange("p (h n) -> p h n", h=2), ps[0:H, 1:3, :], ACT.Copy)\
                               .then_inc(act_step, 1)
                            act.wait_ge(dve_step, 3)
                            act.activation(u[:, :], mag[:, :], ACT.Exp, scale=-1.0).then_inc(act_step, 1)
                            act.activation(rate[:, :], alog[:, :], ACT.Exp).then_inc(act_step, 1)
                            act.wait_ge(dve_step, 4)
                            act.activation(lnw[:, :], w[:, :], ACT.Ln).then_inc(act_step, 1)
                            act.wait_ge(pe_step, 4)
                            for b, dst in ((4, grown[:, :, :].rearrange(flat)), (5, through[:, :, :].rearrange(flat)), (6, dec[:, :])):
                                act.activation(dst, ps[:, b, :], ACT.Exp).then_inc(act_step, 1)

                        @block.vector
                        def _(dve):
                            dve.wait_ge(act_step, 1)
                            dve.tensor_tensor(wdtT[1][:, :, :], ps[:, 0, 0:C * H].rearrange("p (c n) -> p c n", c=C),
                                              wdtT[0][:, :, :].bitcast(F32), ALU.subtract).then_inc(dve_step, 1)
                            dve.wait_ge(pe_step, 3)
                            dve.wait_ge(loaded, 16 * 8)
                            vq = v[:, :].rearrange("p (q h) -> p q h", h=H)
                            dt_flat = dt[:, :, :].rearrange(flat)
                            n = 1

                            def then(instruction):
                                nonlocal n
                                instruction.then_inc(dve_step, 1)
                                n += 1
                                dve.wait_ge(dve_step, n)

                            then(dve.tensor_tensor(vq, ps[:, 3, :].rearrange("p (q h) -> p q h", h=H),
                                                   dt_b[:, :].unsqueeze(1).to_broadcast([P, Q, H]), ALU.add))
                            then(dve.scalar_tensor_tensor(mag[:, :], v[:, :], -1.0, v[:, :], ALU.mult, ALU.max))
                            dve.wait_ge(act_step, 4)
                            then(dve.tensor_scalar(w[:, :], u[:, :], 1.0, None, ALU.add))
                            then(dve.tensor_scalar(zero[:, :], w[:, :], 1.0, None, ALU.is_equal))
                            dve.wait_ge(act_step, 5)
                            then(dve.tensor_tensor(lnw[:, :], lnw[:, :], zero[:, :], ALU.add))
                            then(dve.tensor_tensor(lnw[:, :], lnw[:, :], u[:, :], ALU.mult))
                            then(dve.scalar_tensor_tensor(w[:, :], w[:, :], -1.0, zero[:, :], ALU.add, ALU.add))
                            then(dve.reciprocal(mag[:, :], w[:, :]))
                            then(dve.tensor_tensor(lnw[:, :], lnw[:, :], mag[:, :], ALU.mult))
                            then(dve.scalar_tensor_tensor(dt_flat, v[:, :], 0.0, lnw[:, :], ALU.max, ALU.add))
                            then(dve.scalar_tensor_tensor(a[:, :, :], dt[:, :, :], -1.0,
                                                          rate[:, :].unsqueeze(1).to_broadcast([P, Q, H]), ALU.mult, ALU.mult))
                            then(dve.tensor_scalar(a[:, :, :].rearrange(flat), a[:, :, :].rearrange(flat), -1e30, None, ALU.max))
                            then(dve.tensor_copy(a_hi[:, :, :], a[:, :, :]))
                            dve.tensor_tensor(a_lo[:, :, :], a[:, :, :], a_hi[:, :, :].bitcast(F32), ALU.subtract)
                            dve.wait_ge(consts, 2)
                            dve.tensor_copy(after_r[:, :], after[:, :])
                            dve.wait_ge(act_step, 8)
                            then(dve.tensor_tensor(to_end[:, :, :].rearrange(flat), dec[:, :], dt_flat, ALU.mult))

                NATS, NB, RING = 14, 4, 4
                nat = [sb(st, f"nat{k}", [P, D]) for k in range(NB)]
                WT = [[sb(st, f"WT{k}_{part}", [P, C, P], F32R) for part in ("hi", "lo")] for k in range(2)]
                WOT = [sb(st, f"WOT_{part}", [P, C, D], F32R) for part in ("hi", "lo")]
                gate = sb(st, "gate", [P, 4, S])
                XT = sb(st, "XT", [P, 6, S])
                raw = sb(st, "conv_raw", [P, K - 1 + S])
                acc = sb(st, "conv_acc", [P, S])
                X = sb(st, "X", [P, 2, GW])
                B = sb(st, "B", [P, 2, N])
                xdt = sb(st, "xdt", [P, GW])
                xend = sb(st, "xend", [P, GW])
                steps_a = [sb(st, f"steps_a_{part}", [P, HG, P], F32R) for part in ("hi", "lo")]
                E = sb(st, "decay", [P, 2, HG, P])
                Gm = sb(st, "Gm", [P, 2, P])
                carried = sb(st, "carried", [P, GW])
                state = sb(st, "state", [P, GW])
                yT = sb(st, "yT", [P, 4, HALF])
                var = sb(st, "m_var", [P, 4])
                rs = sb(st, "m_rs", [P, 2, 4])
                yn = [sb(st, f"yn_{part}", [P, 4, HALF], F32R) for part in ("hi", "lo")]

                def squares(j, k):
                    return XT[:, j, k * HALF:(k + 1) * HALF]

                steps = [("nat", 0), ("sa", 0), ("nat", 1), ("sq", 1)]
                for k in range(6):
                    steps.append(("proj", k, 0))
                    steps += {0: [], 1: [("ss", 1), ("yn", 1)]}.get(k, [("out", 1, k - 2)])
                    steps += [("proj", k, 1), ("nat", k + 2)]
                steps += [("proj", 6, 0), ("silu", 5), ("proj", 6, 1)]

                def prepare(c):
                    return [("xc", c), ("bc", c), ("dec", c, 0), ("dec", c, 1)] + [("sa", c + 1)] * (c + 1 < Q) + [("g", c)]

                steps += prepare(0)
                early = {0: [("nat", 8), ("proj", 7, 0)]}
                beside = {0: [("proj", 7, 1), ("nat", 9)], 1: [("proj", 8, 0)], 2: [("proj", 8, 1), ("proj", 9, 0)],
                          3: [("proj", 9, 1)], 4: [("nat", 10), ("nat", 11)], 5: [("nat", 12), ("nat", 13), ("ss", 0)],
                          6: [("out", 0, 0), ("out", 0, 1)], 7: [("out", 0, 2), ("out", 0, 3)]}
                for c in range(Q):
                    steps += early.get(c, [])
                    if c + 1 < Q:
                        steps += prepare(c + 1)
                    if c:
                        steps.append(("in", c))
                    steps += beside[c]
                    if c + 1 < Q:
                        steps.append(("st", c))
                    if c % 4 == 3:
                        steps.append(("sg", c // 4))
                    steps.append(("y", c))
                    if c == 3:
                        steps.append(("sq", 0))
                    if c == 4:
                        steps.append(("yn", 0))
                ON_PE = ("nat", "proj", "xc", "bc", "dec", "g", "in", "st", "y", "ss", "out")
                ring_of = {"proj": "a", "xc": "a", "bc": "a", "dec": "a"}
                order = {r: [s for s in steps if s[0] in ON_PE and ring_of.get(s[0], "v") == r] for r in "av"}
                at = {s: n for r in order.values() for n, s in enumerate(r)}

                def bank_of(s):
                    r = ring_of.get(s[0], "v")
                    return ps[:, (0 if r == "a" else 4) + at[s] % RING, :]

                def use_before(s):
                    n, per = at[s], len(order[ring_of.get(s[0], "v")])
                    return n - RING if n >= RING else max(m for m in range(per) if m % RING == n % RING) - per

                def yn_cols(t):
                    return [x[:, :, t * P:(t + 1) * P] for x in yn]

                full = {r: Tally(sem(st, f"full_{r}"), len(order[r])) for r in "av"}
                free = {r: Tally(sem(st, f"free_{r}"), len(order[r])) for r in "av"}
                nat_loaded = [Tally(sem(st, f"nat_loaded{k}"), len(range(k, NATS, NB)), 16) for k in range(NB)]
                nat_hi = Tally(sem(st, "nat_hi"), NATS)
                taps = Tally(sem(st, "taps"), 6 * (K - 1))
                raw_copied = Tally(sem(st, "raw_copied"), 12)
                silu_done = Tally(sem(st, "silu_done"), 6)
                steps_a_ready = Tally(sem(st, "steps_a_ready"), Q)
                x_scaled = Tally(sem(st, "x_scaled"), 2 * Q)
                mixed = Tally(sem(st, "mixed"), Q)
                state_kept = Tally(sem(st, "state_kept"), Q - 2)
                squared = Tally(sem(st, "squared"), 8)
                gate_done = Tally(sem(st, "m_gate_done"), 2)
                rs_ready = Tally(sem(st, "m_rs_ready"), 2)
                gated = Tally(sem(st, "m_gated"), 8)
                yn_hi = Tally(sem(st, "yn_hi"), 2)
                yn_lo = Tally(sem(st, "yn_lo"), 2)
                zeroed = sem(st, "m_zeroed")
                tail_full = sem(st, "m_tail_full")
                tail_var = sem(st, "m_tail_var")
                tallies = {
                    "pe": [full["a"], full["v"]],
                    "act": [free["a"], nat_hi, raw_copied, silu_done, squared, gate_done, yn_hi],
                    "dve": [free["v"], taps, mixed, state_kept, gated, yn_lo],
                    "pool": [steps_a_ready, x_scaled, rs_ready],
                }
                bc8 = [P, HG, PD]

                def heads(t):
                    return t.rearrange("p (h d) -> p h d", h=HG)

                def of_group(t, i, c):
                    return t[:, c, bass.ds(i * HG, HG)]

                def nat_dst(n):
                    if n < 10:
                        return lambda b: b.rearrange("p (c n) -> p c n", c=C), [x[:, :, :] for x in WT[n % 2]]
                    k = n - 10
                    return lambda b: b.rearrange("p (c n) -> p c n", c=C), [x[:, :, k * P:(k + 1) * P] for x in WOT]

                with nc.Block() as block:
                    @block.sync
                    def _(sp):
                        with sp.Fori(0, G) as i:
                            for n in range(NATS):
                                for m in {9: (10,), 10: ()}.get(n, (n,)):
                                    full["v"].wait(sp, i, at[("nat", m - NB)] if m >= NB else
                                                   at[("nat", [x for x in range(NATS) if x % NB == m % NB][-1])] - len(order["v"]))
                                if n < 4:
                                    src = in_proj_w[bass.ds(i * GW + (I + n * P), P), :]
                                elif n < 6:
                                    src = in_proj_w[bass.ds(i * N + (2 * I + (n - 4) * G * N), P), :]
                                elif n < 10:
                                    src = in_proj_w[bass.ds(i * GW + (n - 6) * P, P), :]
                                else:
                                    src = out_proj_w[(n - 10) * P:(n - 9) * P, bass.ds(i * GW, GW)]
                                nat_loaded[n % NB].mark(sp.dma_start(nat[n % NB][:, :], src))

                    @block.tensor
                    def _(pe):
                        for x in tallies["pe"]:
                            x.start(pe)
                        pe.wait_ge(zeroed, 2)
                        with pe.Fori(0, G) as i:
                            for s in steps:
                                kind, k = s[0], s[1]
                                if kind not in ON_PE:
                                    continue
                                r = ring_of.get(kind, "v")
                                free[r].wait(pe, i, use_before(s))
                                b = bank_of(s)
                                if kind == "nat":
                                    pe.wait_ge(nat_loaded[k % NB].sem, i * (nat_loaded[k % NB].per * 16) + (k // NB + 1) * 16)
                                    for c in range(C):
                                        last = pe.transpose(b[:, c * P:(c + 1) * P], nat[k % NB][:, c * P:(c + 1) * P],
                                                            ident[:, :])
                                elif kind == "proj":
                                    free["v"].wait(pe, i, at[("nat", k)])
                                    for c in range(C):
                                        last = mm3(pe, b, [x[:, c, :] for x in WT[k % 2]],
                                                   xn_cols(c, s[2] * HALF, (s[2] + 1) * HALF), c == 0, c == C - 1)
                                elif kind == "xc":
                                    silu_done.wait(pe, i, 3)
                                    for j in range(4):
                                        last = pe.transpose(b[:, j * P:(j + 1) * P], XT[:, j, k * P:(k + 1) * P], ident[:, :])
                                elif kind == "bc":
                                    silu_done.wait(pe, i, 4)
                                    last = pe.transpose(b[:, 0:P], XT[:, 4, k * P:(k + 1) * P], ident[:, :])
                                elif kind == "dec":
                                    steps_a_ready.wait(pe, i, k)
                                    for m in range(2):
                                        last = pe.matmul(b, after_r[:, :],
                                                         steps_a[m][:, 4 * s[2]:4 * s[2] + 4, :].rearrange("p h t -> p (h t)"),
                                                         start=(m == 0), stop=(m == 1), skip_group_check=True)
                                elif kind == "g":
                                    silu_done.wait(pe, i, 5)
                                    cols = slice(k * P, (k + 1) * P)
                                    last = pe.matmul(b[:, 0:P], XT[:, 4, cols], XT[:, 5, cols], start=True, stop=True,
                                                     skip_group_check=True)
                                elif kind == "in":
                                    free["v"].wait(pe, i, at[("st", k - 1)])
                                    last = pe.matmul(b, XT[:, 5, k * P:(k + 1) * P], state[:, :], start=True, stop=True,
                                                     skip_group_check=True)
                                elif kind == "st":
                                    x_scaled.wait(pe, i, 2 * k)
                                    free["a"].wait(pe, i, at[("bc", k)])
                                    last = pe.matmul(b, B[:, k % 2, :], xend[:, :], start=True, stop=True,
                                                     skip_group_check=True)
                                elif kind == "y":
                                    mixed.wait(pe, i, k)
                                    x_scaled.wait(pe, i, 2 * k + 1)
                                    if k:
                                        free["v"].wait(pe, i, at[("in", k)])
                                    for j in range(4):
                                        cols = b[:, j * P:(j + 1) * P]
                                        for m in range(2):
                                            h = 2 * j + m
                                            last = pe.matmul(cols[m * PD:(m + 1) * PD, :], xdt[:, h * PD:(h + 1) * PD],
                                                             E[:, k % 2, h, :], start=True, stop=(k == 0),
                                                             skip_group_check=True)
                                        if k:
                                            last = pe.matmul(cols, carried[:, j * P:(j + 1) * P], ident[:, :],
                                                             start=False, stop=True, skip_group_check=True)
                                elif kind == "ss":
                                    squared.wait(pe, i, 4 * (1 - k) + 3)
                                    for t in range(4):
                                        for j in range(4):
                                            last = pe.matmul(b[:, t:t + 1], squares(j, k)[:, t * P:(t + 1) * P], mean_col[:, :],
                                                             start=(j == 0), stop=(j == 3), skip_group_check=True)
                                elif kind == "out":
                                    yn_lo.wait(pe, i, 1 - k)
                                    for j in range(4):
                                        last = mm3(pe, b, [x[:, j, :] for x in yn_cols(s[2])],
                                                   [x[:, j, :] for x in WOT], j == 0, j == 3)
                                full[r].mark(last)
                        free["a"].wait(pe, G, -1)
                        free["v"].wait(pe, G, -1)
                        squared.wait(pe, G, 3)
                        for t in range(4):
                            for j in range(4):
                                last = pe.matmul(ps[:, 4, t:t + 1], squares(j, 1)[:, t * P:(t + 1) * P], mean_col[:, :],
                                                 start=(j == 0), stop=(j == 3), skip_group_check=True)
                        last.then_inc(tail_full, 1)
                        yn_lo.wait(pe, G, 0)
                        for t in range(4):
                            for j in range(4):
                                last = mm3(pe, ps[:, t, :], [x[:, j, :] for x in yn_cols(t)],
                                           [x[:, j, :] for x in WOT], j == 0, j == 3)
                            last.then_inc(tail_full, 1)

                    @block.scalar
                    def _(act):
                        for x in tallies["act"]:
                            x.start(act)
                        act.wait_ge(zeroed, 2)
                        with act.Fori(0, G) as i:
                            for s in steps:
                                kind, k = s[0], s[1]
                                b = bank_of(s) if s in at else None
                                if kind in ring_of:
                                    full["a"].wait(act, i, at[s])
                                if kind == "nat":
                                    full["v"].wait(act, i, at[s])
                                    if k < 10:
                                        if k >= 2:
                                            full["a"].wait(act, i, at[("proj", k - 2, 1)])
                                    elif k == 10:
                                        full["v"].wait(act, i, at[("out", 1, 3)])
                                    src, dst = nat_dst(k)
                                    nat_hi.mark(act.activation(dst[0], src(b), ACT.Copy))
                                elif kind == "proj" and k >= 6:
                                    yn_lo.wait(act, i, 0)
                                    free["a"].mark(act.activation(gate[:, k - 6, s[2] * HALF:(s[2] + 1) * HALF], b, ACT.Copy))
                                elif kind == "sg":
                                    half = gate[:, :, k * HALF:(k + 1) * HALF]
                                    free["a"].wait(act, i, at[("proj", 9, 1)])
                                    gate_done.mark(act.activation(half, half, ACT.Silu))
                                elif kind == "proj":
                                    j, h = k, s[2]
                                    ct = i * 4 + j if j < 4 else i + (I // P + (j - 4) * G)
                                    cols = slice(h * HALF, (h + 1) * HALF)
                                    if h == 0:
                                        taps.wait(act, i, (K - 1) * j - 1)
                                        silu_done.wait(act, i, j - 1)
                                    raw_copied.mark(act.activation(raw[:, K - 1 + h * HALF:K - 1 + (h + 1) * HALF], b, ACT.Copy))
                                    free["a"].mark(act.activation(acc[:, cols], b, ACT.Identity,
                                                                  scale=conv_w[:, bass.ds(ct, 1), K - 1],
                                                                  bias=conv_b[:, bass.ds(ct, 1)]))
                                    if h == 1 and j < 5:
                                        taps.wait(act, i, (K - 1) * (j + 1) - 1)
                                        if j == 0:
                                            full["v"].wait(act, i, at[("ss", 1)])
                                        silu_done.mark(act.activation(XT[:, j, :], acc[:, :], ACT.Silu))
                                elif kind == "silu":
                                    taps.wait(act, i, (K - 1) * (k + 1) - 1)
                                    silu_done.mark(act.activation(XT[:, k, :], acc[:, :], ACT.Silu))
                                elif kind == "xc":
                                    x_scaled.wait(act, i, 2 * (k - 2) + 1)
                                    free["a"].mark(act.activation(X[:, k % 2, :], b, ACT.Copy))
                                elif kind == "bc":
                                    if k >= 2:
                                        full["v"].wait(act, i, at[("st", k - 2)])
                                    free["a"].mark(act.activation(B[:, k % 2, :], b[:, 0:P], ACT.Copy))
                                elif kind == "dec":
                                    if k >= 2 and s[2] == 0:
                                        full["v"].wait(act, i, at[("y", k - 2)])
                                    free["a"].mark(act.activation(
                                        E[:, k % 2, 4 * s[2]:4 * s[2] + 4, :].rearrange("p h t -> p (h t)"), b, ACT.Exp))
                                elif kind == "sq":
                                    free["v"].wait(act, i, at[("y", 3)] if k == 0 else at[("y", Q - 1)] - len(order["v"]))
                                    for j in range(4):
                                        squared.mark(act.activation(squares(j, k), yT[:, j, :], ACT.Square))
                                elif kind == "yn":
                                    gated.wait(act, i, 4 * (1 - k) + 3)
                                    full["v"].wait(act, i, at[("out", 1, 3)] if k == 0 else at[("out", 0, 3)] - len(order["v"]))
                                    yn_hi.mark(act.activation(yn[0][:, :, :], gate[:, :, k * HALF:(k + 1) * HALF], ACT.Copy))

                        free["v"].wait(act, G, -1)
                        for j in range(4):
                            squared.mark(act.activation(squares(j, 1), yT[:, j, :], ACT.Square))
                        gated.wait(act, G, 3)
                        yn_hi.mark(act.activation(yn[0][:, :, :], gate[:, :, HALF:S], ACT.Copy))

                    @block.gpsimd
                    def _(pool):
                        for x in tallies["pool"]:
                            x.start(pool)
                        pool.memset(raw[:, 0:K - 1], 0.0).then_inc(zeroed, 1)
                        with pool.Fori(0, G) as i:
                            for s in steps:
                                kind, k = s[0], s[1]
                                if kind == "sa":
                                    full["a"].wait(pool, i, at[("dec", k - 1, 1)] if k else
                                                   at[("dec", Q - 1, 1)] - len(order["a"]))
                                    for dst, part in zip(steps_a, (a_hi, a_lo)):
                                        last = pool.tensor_tensor(
                                            dst[:, :, :], upto[:, :].unsqueeze(1).to_broadcast([P, HG, P]),
                                            of_group(part, i, k).bitcast(F32).unsqueeze(2).to_broadcast([P, HG, P]), ALU.mult)
                                    steps_a_ready.mark(last)
                                elif kind == "g":
                                    c = k
                                    free["a"].wait(pool, i, at[("xc", c)])
                                    if c:
                                        full["v"].wait(pool, i, at[("y", c - 1)])
                                    else:
                                        full["v"].wait(pool, i, at[("y", Q - 1)] - len(order["v"]))
                                    x_scaled.mark(pool.tensor_tensor(heads(xend[:, :]), heads(X[:, c % 2, :]),
                                                                     of_group(to_end, i, c).unsqueeze(2).to_broadcast(bc8), ALU.mult))
                                    x_scaled.mark(pool.tensor_tensor(heads(xdt[:, :]), heads(X[:, c % 2, :]),
                                                                     of_group(dt, i, c).unsqueeze(2).to_broadcast(bc8), ALU.mult))
                                elif kind == "ss":
                                    free["v"].wait(pool, i, at[s])
                                    rs_ready.mark(pool.tensor_tensor(rs[:, k, :], var[:, :], minus_half[:, :].to_broadcast([P, 4]),
                                                                     ALU.pow))
                        pool.wait_ge(tail_var, 1)
                        rs_ready.mark(pool.tensor_tensor(rs[:, 1, :], var[:, :], minus_half[:, :].to_broadcast([P, 4]), ALU.pow))

                    @block.vector
                    def _(dve):
                        for x in tallies["dve"]:
                            x.start(dve)
                        for m in (yT[:, :, :], gate[:, :, HALF:S], WOT[0][:, :, :].bitcast(F32), WOT[1][:, :, :].bitcast(F32)):
                            last = dve.memset(m, 0.0)
                        last.then_inc(zeroed, 1)
                        dve.wait_ge(zeroed, 2)
                        with dve.Fori(0, G) as i:
                            for s in steps:
                                kind, k = s[0], s[1]
                                b = bank_of(s) if s in at else None
                                if kind in ON_PE and kind not in ring_of and kind != "nat":
                                    full["v"].wait(dve, i, at[s])
                                if kind == "nat":
                                    nat_hi.wait(dve, i, k)
                                    src, dst = nat_dst(k)
                                    free["v"].mark(dve.tensor_tensor(dst[1], src(b), dst[0].bitcast(F32), ALU.subtract))
                                elif kind == "proj" and k < 6 and s[2] == 1:
                                    j = k
                                    ct = i * 4 + j if j < 4 else i + (I // P + (j - 4) * G)
                                    free["a"].wait(dve, i, at[s])
                                    for m in range(K - 1):
                                        if m:
                                            taps.wait(dve, i, (K - 1) * j + m - 1)
                                        taps.mark(dve.scalar_tensor_tensor(
                                            acc[:, :], raw[:, m:m + S], conv_w[:, bass.ds(ct, 1), m], acc[:, :],
                                            ALU.mult, ALU.add))
                                elif kind == "g":
                                    free["v"].mark(dve.tensor_tensor(Gm[:, k % 2, :], b[:, 0:P], upto[:, :], ALU.mult))
                                    free["v"].wait(dve, i, at[s])
                                    free["a"].wait(dve, i, at[("dec", k, 1)])
                                    mixed.mark(dve.tensor_tensor(E[:, k % 2, :, :], E[:, k % 2, :, :],
                                                                 Gm[:, k % 2, :].unsqueeze(1).to_broadcast([P, HG, P]), ALU.mult))
                                elif kind == "in":
                                    if k >= 2:
                                        full["v"].wait(dve, i, at[("y", k - 1)])
                                    free["v"].mark(dve.tensor_tensor(heads(carried[:, :]), heads(b),
                                                                     of_group(grown, i, k).unsqueeze(2).to_broadcast(bc8), ALU.mult))
                                elif kind == "st":
                                    if k == 0:
                                        free["v"].mark(dve.tensor_copy(state[:, :], b))
                                    else:
                                        state_kept.mark(dve.tensor_tensor(heads(state[:, :]), heads(state[:, :]),
                                                                          of_group(through, i, k).unsqueeze(2).to_broadcast(bc8), ALU.mult))
                                        state_kept.wait(dve, i, k - 1)
                                        free["v"].mark(dve.tensor_tensor(state[:, :], state[:, :], b, ALU.add))
                                elif kind == "y":
                                    c = k
                                    if c % 4 == 0:
                                        squared.wait(dve, i, c + 3)
                                    for j in range(4):
                                        o = (c % 4) * P
                                        ins = dve.scalar_tensor_tensor(yT[:, j, o:o + P], XT[:, j, c * P:(c + 1) * P],
                                                                       d_col[:, bass.ds(i * 4 + j, 1)], b[:, j * P:(j + 1) * P],
                                                                       ALU.mult, ALU.add)
                                    free["v"].mark(ins)
                                elif kind == "ss":
                                    rs_ready.wait(dve, i, -k)
                                    free["v"].mark(dve.tensor_scalar(var[:, :], b[:, 0:4], EPS, None, ALU.add))
                                elif kind == "sq":
                                    gate_done.wait(dve, i, -k)
                                    free["v"].wait(dve, i, at[("y", 3)] if k == 0 else at[("y", Q - 1)] - len(order["v"]))
                                    for j in range(4):
                                        half = gate[:, j, k * HALF:(k + 1) * HALF]
                                        gated.mark(dve.scalar_tensor_tensor(half, yT[:, j, :], nw_col[:, bass.ds(i * 4 + (j + 4 * (1 - k)), 1)],
                                                                            half, ALU.mult, ALU.mult))
                                elif kind == "yn":
                                    yn_hi.wait(dve, i, 1 - k)
                                    yn_lo.mark(dve.tensor_tensor(yn[1][:, :, :], gate[:, :, k * HALF:(k + 1) * HALF],
                                                                 yn[0][:, :, :].bitcast(F32), ALU.subtract))
                                elif kind == "out":
                                    t = 4 * k + s[2]
                                    if s[2] == 0:
                                        rs_ready.wait(dve, i, 1 - k)
                                    free["v"].mark(dve.scalar_tensor_tensor(x_res[:, t, :], b, rs[:, k, s[2]:s[2] + 1],
                                                                            x_res[:, t, :], ALU.mult, ALU.add))
                        gate_done.wait(dve, G, -1)
                        free["v"].wait(dve, G, -1)
                        for j in range(4):
                            half = gate[:, j, HALF:S]
                            gated.mark(dve.scalar_tensor_tensor(half, yT[:, j, :], nw_col[:, G * 4 + j:G * 4 + j + 1],
                                                                half, ALU.mult, ALU.mult))
                        yn_hi.wait(dve, G, 0)
                        yn_lo.mark(dve.tensor_tensor(yn[1][:, :, :], gate[:, :, HALF:S], yn[0][:, :, :].bitcast(F32), ALU.subtract))
                        dve.wait_ge(tail_full, 1)
                        dve.tensor_scalar(var[:, :], ps[:, 4, 0:4], EPS, None, ALU.add).then_inc(tail_var, 1)
                        rs_ready.wait(dve, G, 0)
                        for t in range(4):
                            dve.wait_ge(tail_full, t + 2)
                            dve.scalar_tensor_tensor(x_res[:, 4 + t, :], ps[:, t, :], rs[:, 1, t:t + 1], x_res[:, 4 + t, :],
                                                     ALU.mult, ALU.add)

        steps = [("f0a", experts_ffn), ("at0", attention), ("f0b", experts_ffn),
                 ("f1a", lora_ffn), ("ssm", mamba), ("f1b", lora_ffn)]
        for tag, stage in [steps[n] for n in stages]:
            layer_norm(tag)
            stage(tag)

        with ExitStack() as st:
            stored = sem(st, "out_stored")
            with nc.Block() as block:
                @block.sync
                def _(sp):
                    sp.dma_start(out.rearrange("a (t p) d -> p (a t) d", p=P), x_res[:, :, :]).then_inc(stored, 16)
                    sp.wait_ge(stored, 16)


_INS = ['L0_attn_hidden_states', 'L0_attn_wq', 'L0_attn_wkv', 'L0_attn_wo', 'L0_ffn_W_gate', 'L0_ffn_b_gate',
        'L0_ffn_W_e', 'L0_ffn_b_e', 'L1_attn_in_proj_w', 'L1_attn_conv_weight', 'L1_attn_conv_bias',
        'L1_attn_dt_bias', 'L1_attn_A_log', 'L1_attn_D', 'L1_attn_norm_weight', 'L1_attn_out_proj_w',
        'L1_ffn_W_up', 'L1_ffn_gate_w', 'L1_ffn_expert_bias', 'L1_ffn_lora_A', 'L1_ffn_lora_B']
_STAGES = range(6)


def kernel(**inputs):
    import numpy as _np
    import concourse.bacc as _bacc
    from concourse import mybir as _mybir
    from concourse.bass_utils import run_bass_kernel_spmd as _run

    nc = _bacc.Bacc("TRN2", target_bir_lowering=False, num_devices=1)
    arrays, args = {}, []
    for name in _INS:
        a = _np.ascontiguousarray(inputs[name])
        arrays[f"in_{name}_dram"] = a
        args.append(nc.dram_tensor(f"in_{name}_dram", a.shape, _mybir.dt.from_np(a.dtype), kind="ExternalInput").ap())
    out = nc.dram_tensor("out_0_dram", (1, S, D), _mybir.dt.float32, kind="ExternalOutput").ap()
    build(nc, _STAGES, *args, out)
    r = _run(nc, [arrays], core_ids=[0])
    return r.results[0]["out_0_dram"]
```

```python
import concourse.bass as bass
from concourse import mybir
from contextlib import ExitStack

F32 = mybir.dt.float32
F32R = mybir.dt.float32r
BF16 = mybir.dt.bfloat16
ALU = mybir.AluOpType
ACT = mybir.ActivationFunctionType
AX = mybir.AxisListType

P = 128
D = 512
S = 1024
T = S // P
C = D // P
HALF = 512
EPS = 1e-5


def build(nc, stages, hidden, wq, wkv, wo, w_gate, b_gate, w_e, b_e, in_proj_w, conv_weight, conv_bias,
          dt_bias, a_log, d_skip, norm_weight, out_proj_w, w_up, gate_w, expert_bias, lora_a, lora_b, out):
    TAGS = ("f0a", "at0", "f0b", "f1a", "ssm", "f1b")
    FIRST, LAST = TAGS[stages[0]], TAGS[stages[-1]]
    whole = ExitStack()
    with whole:
        def sb(stack, name, shape, dtype=F32):
            return stack.enter_context(nc.sbuf_tensor(name, shape, dtype))

        def sem(stack, name):
            return stack.enter_context(nc.semaphore(name))

        x_res = sb(whole, "x_res", [P, T, D])
        xnT_hi = sb(whole, "xnT_hi", [P, C, S], F32R)
        xnT_lo = sb(whole, "xnT_lo", [P, C, S], F32R)
        ident = sb(whole, "ident", [P, P])
        zero_col = sb(whole, "zero_col", [P, 1])
        minus_half = sb(whole, "minus_half", [P, 1])
        ps = whole.enter_context(nc.psum_tensor("ps", [P, 8, HALF], F32))

        def mm3(pe, out, lhs, rhs, first, last):
            pe.matmul(out, lhs[0], rhs[0], start=first, stop=False, skip_group_check=True)
            pe.matmul(out, lhs[0], rhs[1], start=False, stop=False, skip_group_check=True)
            return pe.matmul(out, lhs[1], rhs[0], start=False, stop=last, skip_group_check=True)

        def xn_cols(c, a, b):
            return xnT_hi[:, c, a:b], xnT_lo[:, c, a:b]

        x_loaded = [sem(whole, f"x_loaded{h}") for h in range(2)]
        with ExitStack() as st:
            ident_zeroed = sem(st, "ident_zeroed")
            with nc.Block() as block:
                @block.sync
                def _(sp):
                    src = hidden.rearrange("a (t p) d -> p (a t) d", p=P)
                    for h in range(2):
                        half = slice(h * T // 2, (h + 1) * T // 2)
                        sp.dma_start(x_res[:, half, :], src[:, half, :]).then_inc(x_loaded[h], 16)

                @block.gpsimd
                def _(pool):
                    pool.memset(zero_col[:, :], 0.0)
                    pool.memset(minus_half[:, :], -0.5)
                    pool.memset(ident[:, :], 0.0).then_inc(ident_zeroed, 1)
                    pool.wait_ge(ident_zeroed, 1)
                    pool.affine_select(out=ident[:, :], in_=ident[:, :], compare_op=ALU.not_equal, fill=1.0,
                                       base=0, pattern=[[-1, P]], channel_multiplier=1)

        def layer_norm(st, tag, xn, bank0=0):
            HT, BANKS = T // 2, 4
            stats = sb(st, f"stats{tag}", [P, T, 6])
            mean_var = sb(st, f"mean_var{tag}", [P, T, 2])
            var = sb(st, f"var{tag}", [P, T])
            rstd = sb(st, f"rstd{tag}", [P, T])
            dve_step = sem(st, f"ln_dve_step{tag}")
            var_ready = sem(st, f"var_ready{tag}")
            rstd_ready = sem(st, f"rstd_ready{tag}")
            xn_ready = sem(st, f"xn_ready{tag}")
            turned = sem(st, f"xn_turned{tag}")
            hi_done = sem(st, f"xn_hi_done{tag}")
            lo_done = sem(st, f"xn_lo_done{tag}")

            def bank(t):
                return ps[:, bank0 + t % BANKS, :]

            def vector(dve):
                for h in range(2):
                    if tag == FIRST:
                        dve.wait_ge(x_loaded[h], 16)
                    for t in range(h * HT, (h + 1) * HT):
                        dve.bn_stats(stats[:, t, :], x_res[:, t, :]).then_inc(dve_step, 1)
                    for t in range(h * HT, (h + 1) * HT):
                        dve.wait_ge(dve_step, h * HT + t + 1)
                        dve.bn_aggr(mean_var[:, t, :], stats[:, t, :]).then_inc(dve_step, 1)
                    dve.wait_ge(dve_step, 2 * (h + 1) * HT)
                    half = slice(h * HT, (h + 1) * HT)
                    dve.tensor_scalar(var[:, half], mean_var[:, half, 1], EPS, None, ALU.add).then_inc(var_ready, 1)
                for t in range(T + 2):
                    if t < T:
                        if t % HT == 0:
                            dve.wait_ge(rstd_ready, t // HT + 1)
                        if t >= BANKS:
                            dve.wait_ge(turned, t - BANKS + 1)
                        dve.tensor_scalar(xn[:, t % BANKS, :], x_res[:, t, :], mean_var[:, t, 0:1],
                                          rstd[:, t:t + 1], ALU.subtract, ALU.mult).then_inc(xn_ready, 1)
                    if t >= 2:
                        k = t - 2
                        dve.wait_ge(hi_done, k + 1)
                        cols = slice(k * P, (k + 1) * P)
                        dve.tensor_tensor(xnT_lo[:, :, cols], bank(k).rearrange("p (c n) -> p c n", c=C),
                                          xnT_hi[:, :, cols].bitcast(F32), ALU.subtract).then_inc(lo_done, 1)

            def tensor(pe):
                for t in range(T):
                    pe.wait_ge(xn_ready, t + 1)
                    if t >= BANKS:
                        pe.wait_ge(lo_done, t - BANKS + 1)
                    for c in range(C):
                        last = pe.transpose(bank(t)[:, c * P:(c + 1) * P], xn[:, t % BANKS, c * P:(c + 1) * P],
                                            ident[:, :])
                    last.then_inc(turned, 1)
                pe.wait_ge(lo_done, T)

            def scalar(act):
                for t in range(T):
                    act.wait_ge(turned, t + 1)
                    act.activation(xnT_hi[:, :, t * P:(t + 1) * P], bank(t).rearrange("p (c n) -> p c n", c=C),
                                   ACT.Copy).then_inc(hi_done, 1)

            def gpsimd(pool):
                for h in range(2):
                    half = slice(h * HT, (h + 1) * HT)
                    pool.wait_ge(var_ready, h + 1)
                    pool.tensor_tensor(rstd[:, half], var[:, half], minus_half[:, :].to_broadcast([P, HT]), ALU.pow)\
                        .then_inc(rstd_ready, 1)

            return vector, tensor, scalar, gpsimd

        def rank_mask(dve, step, n0, logits, mask, gt, eq, before, E, K, scale):
            shape = [P, T, E, E]
            rival = logits.rearrange("p (t j) -> p t j", j=E).unsqueeze(2).to_broadcast(shape)
            own = logits.rearrange("p (t e) -> p t e", e=E).unsqueeze(3).to_broadcast(shape)
            v = [a.rearrange("p (t e j) -> p t e j", e=E, j=E) for a in (gt, eq)]
            for k, ins in enumerate((
                lambda: dve.tensor_tensor(v[0], rival, own, ALU.is_gt),
                lambda: dve.tensor_tensor(v[1], rival, own, ALU.is_equal),
                lambda: dve.tensor_tensor(v[1], v[1], before.unsqueeze(1).to_broadcast(shape), ALU.mult),
                lambda: dve.tensor_tensor(v[0], v[0], v[1], ALU.add),
                lambda: dve.tensor_reduce(mask, v[0].rearrange("p t e j -> p (t e) j"), AX.X, ALU.add),
                lambda: dve.tensor_scalar(mask, mask, K - 0.5, scale, ALU.is_lt, ALU.mult),
            )):
                dve.wait_ge(step, n0 + k)
                ins().then_inc(step, 1)
            return n0 + 6

        def experts_ffn(tag):
            E, K, SCALE, RING = 8, 2, 0.25, 4
            with ExitStack() as st:
                w_raw = sb(st, f"ew_raw{tag}", [P, 2, C, D])
                w_hi = [sb(st, f"ew_hi{k}{tag}", [P, C, D], F32R) for k in range(2)]
                w_lo = [sb(st, f"ew_lo{k}{tag}", [P, C, D], F32R) for k in range(2)]
                bias = sb(st, f"e_bias_all{tag}", [P, E, D])
                biased = sb(st, f"e_biased{tag}", [P, 2, D])
                g_raw = sb(st, f"g_raw{tag}", [P, C, E])
                g_hi = sb(st, f"g_hi{tag}", [P, C, E], F32R)
                g_lo = sb(st, f"g_lo{tag}", [P, C, E], F32R)
                g_bias = sb(st, f"g_bias{tag}", [P, E])
                logitsT = sb(st, f"logitsT{tag}", [E, S])
                logits = sb(st, f"logits{tag}", [P, T * E])
                before = sb(st, f"before{tag}", [P, E, E])
                gt = sb(st, f"gt{tag}", [P, T * E * E])
                eq = sb(st, f"eq{tag}", [P, T * E * E])
                mask = sb(st, f"mask{tag}", [P, T * E])
                relu = sb(st, f"relu{tag}", [P, 2, D])
                small_loaded = sem(st, f"e_small_loaded{tag}")
                bias_loaded = sem(st, f"e_bias_loaded{tag}")
                w_loaded = [sem(st, f"ew_loaded{k}{tag}") for k in range(2)]
                w_split = sem(st, f"ew_split{tag}")
                pool_step = sem(st, f"e_pool_step{tag}")
                hi_step = sem(st, f"ew_hi_step{tag}")
                consts_ready = sem(st, f"e_consts{tag}")
                dve_step = sem(st, f"e_dve_step{tag}")
                logitsT_ready = sem(st, f"logitsT_ready{tag}")
                logitsT_copied = sem(st, f"logitsT_copied{tag}")
                logits_turned = sem(st, f"logits_turned{tag}")
                mask_ready = sem(st, f"mask_ready{tag}")
                y_ready = sem(st, f"ey_ready{tag}")
                biased_ready = sem(st, f"e_biased_ready{tag}")
                relu_done = sem(st, f"relu_done{tag}")
                added = sem(st, f"e_added{tag}")
                ln_vector, ln_tensor, ln_scalar, ln_gpsimd = layer_norm(st, tag, sb(st, f"xn{tag}", [P, 4, D]))
                with nc.Block() as block:
                    @block.sync
                    def _(sp):
                        sp.dma_start(g_raw[:, :, :], w_gate.rearrange("(c p) e -> p c e", p=P)).then_inc(small_loaded, 16)
                        sp.dma_start(g_bias[:, :], b_gate.partition_broadcast(P)).then_inc(small_loaded, 16)
                        sp.dma_start(bias[:, :, :], b_e.partition_broadcast(P)).then_inc(bias_loaded, 16)
                        with sp.Fori(0, E // 2) as i:
                            for k in range(2):
                                sp.wait_ge(w_split, i * 2 + (k + 1))
                                sp.dma_start(w_raw[:, k, :, :],
                                             w_e[bass.ds(i * 2 + k, 1)].rearrange("e (c p) h -> p (e c) h", p=P))\
                                  .then_inc(w_loaded[k], 16)

                    @block.gpsimd
                    def _(pool):
                        pool.sem_inc(w_split, 2)
                        pool.memset(before[:, :, :], 1.0).then_inc(pool_step, 1)
                        pool.wait_ge(pool_step, 1)
                        pool.affine_select(out=before[:, :, :], in_=before[:, :, :], compare_op=ALU.is_gt, fill=0.0,
                                           base=0, pattern=[[1, E], [-1, E]], channel_multiplier=0)\
                            .then_inc(consts_ready, 1)
                        ln_gpsimd(pool)
                        with pool.Fori(0, E // 2) as i:
                            for k in range(2):
                                pool.wait_ge(w_loaded[k], (i + 1) * 16)
                                pool.wait_ge(y_ready, i * 2 * T + (k + 1) * T)
                                pool.tensor_tensor(w_hi[k][:, :, :], w_raw[:, k, :, :],
                                                   zero_col[:, :].unsqueeze(2).to_broadcast([P, C, D]), ALU.add).then_inc(hi_step, 1)
                                pool.wait_ge(hi_step, i * 2 + (k + 1))
                                pool.tensor_tensor(w_lo[k][:, :, :], w_raw[:, k, :, :], w_hi[k][:, :, :].bitcast(F32),
                                                   ALU.subtract).then_inc(w_split, 1)

                    @block.tensor
                    def _(pe):
                        ln_tensor(pe)
                        pe.sem_inc(y_ready, 2 * T)
                        pe.wait_ge(dve_step, 2)
                        for h in range(2):
                            for c in range(C):
                                rhs = xn_cols(c, h * HALF, (h + 1) * HALF)
                                last = mm3(pe, ps[0:E, h, :], (g_hi[:, c, :], g_lo[:, c, :]), rhs, c == 0, c == C - 1)
                        last.then_inc(logitsT_ready, 1)
                        pe.wait_ge(logitsT_copied, 1)
                        for t in range(T):
                            last = pe.transpose(ps[:, 2, t * E:(t + 1) * E], logitsT[:, t * P:(t + 1) * P],
                                                ident[0:E, 0:E])
                        last.then_inc(logits_turned, 1)
                        with pe.Fori(0, E // 2) as i:
                            for k in range(2):
                                pe.wait_ge(w_split, i * 2 + (k + 3))
                                for t in range(T):
                                    n = k * T + t
                                    bank = ps[:, 4 + n % RING, :]
                                    pe.wait_ge(biased_ready, i * 2 * T + (n + 1))
                                    for c in range(C):
                                        last = mm3(pe, bank, xn_cols(c, t * P, (t + 1) * P),
                                                   (w_hi[k][:, c, :], w_lo[k][:, c, :]), c == 0, c == C - 1)
                                    last.then_inc(y_ready, 1)

                    @block.scalar
                    def _(act):
                        ln_scalar(act)
                        act.sem_inc(relu_done, 2)
                        act.wait_ge(logitsT_ready, 1)
                        act.activation(logitsT[:, :].rearrange("e (h n) -> e h n", h=2), ps[0:E, 0:2, :], ACT.Copy)\
                           .then_inc(logitsT_copied, 1)
                        act.wait_ge(mask_ready, 1)
                        with act.Fori(0, E // 2) as i:
                            for k in range(2):
                                for t in range(T):
                                    n = k * T + t
                                    act.wait_ge(biased_ready, i * 2 * T + (n + 1 + RING))
                                    act.wait_ge(added, i * 2 * T + (n + 1))
                                    act.activation(relu[:, n % 2, :], biased[:, n % 2, :], ACT.Relu,
                                                   scale=mask[:, bass.ds(i * 2 + (t * E + k), 1)])\
                                       .then_inc(relu_done, 1)

                    @block.vector
                    def _(dve):
                        ln_vector(dve)
                        dve.sem_inc(added, 2)
                        dve.sem_inc(biased_ready, RING)
                        dve.wait_ge(small_loaded, 32)
                        dve.tensor_copy(g_hi[:, :, :], g_raw[:, :, :]).then_inc(dve_step, 1)
                        dve.wait_ge(dve_step, 1)
                        dve.tensor_tensor(g_lo[:, :, :], g_raw[:, :, :], g_hi[:, :, :].bitcast(F32), ALU.subtract)\
                           .then_inc(dve_step, 1)
                        dve.wait_ge(logits_turned, 1)
                        dve.tensor_tensor(logits[:, :].rearrange("p (t e) -> p t e", e=E),
                                          ps[:, 2, 0:T * E].rearrange("p (t e) -> p t e", e=E),
                                          g_bias[:, :].unsqueeze(1).to_broadcast([P, T, E]), ALU.add)\
                           .then_inc(dve_step, 1)
                        dve.wait_ge(consts_ready, 1)
                        n = rank_mask(dve, dve_step, 3, logits[:, :], mask[:, :], gt[:, :], eq[:, :],
                                      before[:, :, :], E, K, SCALE)
                        dve.wait_ge(dve_step, n)
                        dve.sem_inc(mask_ready, 1)
                        dve.wait_ge(bias_loaded, 16)
                        with dve.Fori(0, E // 2) as i:
                            for k in range(2):
                                for t in range(T):
                                    n = k * T + t
                                    dve.wait_ge(y_ready, i * 2 * T + (n + 1 + 2 * T))
                                    dve.wait_ge(relu_done, i * 2 * T + (n + 1))
                                    dve.tensor_tensor(biased[:, n % 2, :], ps[:, 4 + n % RING, :],
                                                      bias[:, bass.ds(i * 2 + k, 1), :].rearrange("p e d -> p (e d)"),
                                                      ALU.add).then_inc(biased_ready, 1)
                                    dve.wait_ge(relu_done, i * 2 * T + (n + 1 + 2))
                                    dve.tensor_tensor(x_res[:, t, :], x_res[:, t, :], relu[:, n % 2, :], ALU.add)\
                                       .then_inc(added, 1)

        def attention(tag):
            H, DN, DQ, HP = 32, 128, 192, 2
            TURNS = H // HP
            SCALE = DQ ** -0.5
            RING = 4
            with ExitStack() as st:
                raw = {k: sb(st, f"a_raw_{k}", [P, 2 * D]) for k in ("q", "k", "v", "o")}
                w = {k: [sb(st, f"a_w{part}_{k}", [P, 2 * D], F32R) for part in ("hi", "lo")] for k in ("q", "k", "v", "o")}
                cols4 = "p (c n) -> p c n"
                wq2, wk2, wv2 = [[a[:, :].rearrange(cols4, c=C) for a in w[k]] for k in ("q", "k", "v")]
                wo2 = [a[:, :].rearrange("p (h n) -> p h n", h=HP) for a in w["o"]]
                qT = [sb(st, f"qT_{part}", [P, HP, S], F32R) for part in ("hi", "lo")]
                kT = [sb(st, f"kT_{part}", [P, HP, S], F32R) for part in ("hi", "lo")]
                V = [sb(st, f"V_{part}", [P, T, HP * DN], F32R) for part in ("hi", "lo")]
                prob = sb(st, "prob", [P, 2, S])
                PT = [sb(st, f"PT_{part}", [P, T, HALF], F32R) for part in ("hi", "lo")]
                oT = [sb(st, f"oT_{part}", [P, HP, S], F32R) for part in ("hi", "lo")]
                top = sb(st, "row_top", [P, 2])
                shift = sb(st, "row_shift", [P, 2])
                total = sb(st, "row_total", [P, 4])
                share = sb(st, "row_share", [P, 4])
                share_row = sb(st, "share_row", [P, HALF])
                o_norm = sb(st, "o_norm", [P, HALF])
                ident_bf = sb(st, "ident_bf", [P, P], BF16)
                later_f = sb(st, "later_f", [P, P])
                later = sb(st, "later_keys", [P, P], BF16)
                raw_loaded = {k: sem(st, f"a_loaded_{k}") for k in "qkvo"}
                split_done = {k: sem(st, f"a_split_{k}") for k in "qkvo"}
                hi_step = sem(st, "a_hi_step")
                pool_step = sem(st, "a_pool_step")
                consts = sem(st, "a_consts")
                zeroed = sem(st, "a_pt_zeroed")
                bank_full = sem(st, "a_bank_full")
                hi_done = sem(st, "a_hi_done")
                bank_free = sem(st, "a_bank_free")
                scores_full = sem(st, "scores_full")
                shift_ready = sem(st, "shift_ready")
                top_found = sem(st, "top_found")
                exp_done = sem(st, "exp_done")
                share_found = sem(st, "share_found")
                o_hi_done = sem(st, "o_hi_done")
                o_lo_done = sem(st, "o_lo_done")
                ln_vector, ln_tensor, ln_scalar, ln_gpsimd = layer_norm(
                    st, tag, prob[:, :, :].rearrange("p a (b n) -> p (a b) n", n=D))
                first_full = sem(st, "a_first_full")
                first_hi = sem(st, "a_first_hi")
                first_lo = sem(st, "a_first_lo")

                units = [(hh, qt) for hh in range(HP) for qt in range(T)]
                N_UNITS = len(units)
                head0 = [("qk", 0, m, h) for m in "qk" for h in range(2)]
                head1 = [("qk", 1, m, h) for m in "qk" for h in range(2)]
                beside = {0: [("v", 1)], 1: [("v", 2)], 2: [("v", 3)], 3: head1[0:2], 4: head1[2:3], 5: head1[3:],
                          6: head0[0:1], 8: head0[1:2], 10: head0[2:3], 13: head0[3:],
                          14: [("wo", 0)], 15: [("wo", 1)]}
                steps = [("s", 0), ("e", 0), ("s", 1), ("e", 1), ("v", 0)] + [("wo", t) for t in range(T // 2, T)]
                for u, (hh, qt) in enumerate(units):
                    steps += beside.get(u, [])
                    if u + 2 < N_UNITS:
                        steps.append(("s", u + 2))
                    if qt % 4 == 0 and u:
                        steps += pending[0:2]
                    for k0 in range(0, qt + 1, 4):
                        steps.append(("t", u, k0, min(k0 + 4, qt + 1)))
                    if u + 2 < N_UNITS:
                        steps.append(("e", u + 2))
                    if qt % 4 == 0 and u:
                        steps += pending[2:]
                    if qt % 4 == 3:
                        pending = [("sh", hh, qt // 4), ("pv", hh, qt // 4), ("ol", hh, qt // 4)]
                steps += [("wo", 2)] + pending[0:2] + [("wo", 3)] + pending[2:]
                ring_kinds = ("qk", "v", "t", "sh", "pv", "wo")
                USES = sum(s[0] in ring_kinds for s in steps)
                SPLITS = sum(s[0] in ("qk", "v", "t") for s in steps)

                assert USES % RING == 0

                def use_of(step):
                    return [s for s in steps if s[0] in ring_kinds].index(step)

                def split_of(step):
                    return [s for s in steps if s[0] in ("qk", "v", "t")].index(step)

                def pieces(qt):
                    n = max((qt + 1) * P, 256)
                    if n <= HALF:
                        return [(0, n)]
                    return [(0, HALF), (HALF, max(n, HALF + 256))]

                def split_views(step):
                    kind = step[0]
                    if kind == "qk":
                        _, hh, m, h = step
                        dst = qT if m == "q" else kT
                        return (lambda b: b[:, :]), [a[:, hh, h * HALF:(h + 1) * HALF] for a in dst]
                    if kind == "v":
                        k = step[1]
                        return (lambda b: b[:, :].rearrange("p (t n) -> p t n", t=2)), [a[:, 2 * k:2 * k + 2, :] for a in V]
                    _, u, k0, k1 = step
                    q0 = (units[u][1] % 4) * P
                    return (lambda b: b[:, 0:(k1 - k0) * P].rearrange("p (k n) -> p k n", n=P)), \
                        [a[:, k0:k1, q0:q0 + P] for a in PT]

                with nc.Block() as block:
                    @block.sync
                    def _(sp):
                        sp.wait_ge(consts, 1)
                        wq_v = wq.rearrange("(c p) (h e) -> p c h e", p=P, e=DQ)
                        wk_v = wkv[:, 0:H * DN].rearrange("(c p) (h e) -> p c h e", p=P, e=DN)
                        wv_v = wkv[:, H * DN:2 * H * DN].rearrange("(c p) (h e) -> p c h e", p=P, e=DN)
                        wo_v = wo.rearrange("(h p) n -> p h n", p=DN)
                        with sp.Fori(0, TURNS) as i:
                            for key, src in (("q", wq_v), ("k", wk_v), ("v", wv_v)):
                                sp.wait_ge(split_done[key], i + 1)
                                dst = raw[key][:, :].rearrange("p (c h e) -> p c h e", c=C, h=HP)
                                for c in range(C):
                                    sp.dma_start(dst[:, c], src[:, c, bass.ds(i * HP, HP), 0:DN]).then_inc(raw_loaded[key], 16)
                            sp.wait_ge(split_done["o"], i + 1)
                            sp.dma_start(raw["o"][:, :].rearrange("p (h n) -> p h n", h=HP),
                                         wo_v[:, bass.ds(i * HP, HP), :]).then_inc(raw_loaded["o"], 16)

                    @block.gpsimd
                    def _(pool):
                        for key in "qkvo":
                            pool.sem_inc(split_done[key], 1)
                        pool.memset(later_f[:, :], 0.0).then_inc(pool_step, 1)
                        pool.tensor_copy(ident_bf[:, :], ident[:, :]).then_inc(consts, 1)
                        pool.wait_ge(pool_step, 1)
                        pool.affine_select(out=later_f[:, :], in_=later_f[:, :], compare_op=ALU.is_ge, fill=-1e30,
                                           base=0, pattern=[[-1, P]], channel_multiplier=1).then_inc(pool_step, 1)
                        pool.wait_ge(pool_step, 2)
                        pool.tensor_copy(later[:, :], later_f[:, :]).then_inc(consts, 1)
                        ln_gpsimd(pool)
                        last_use = {"q": use_of(("qk", 1, "q", 1)), "k": use_of(("qk", 1, "k", 1)),
                                    "v": use_of(("v", 3)), "o": use_of(("wo", T - 1))}
                        with pool.Fori(0, TURNS) as i:
                            for n, key in enumerate("qkvo"):
                                pool.wait_ge(raw_loaded[key], (i + 1) * (16 if key == "o" else 16 * C))
                                pool.wait_ge(bank_full, i * USES + (last_use[key] + 1 + (USES if key == "o" else 0)))
                                hi, lo = w[key]
                                pool.tensor_tensor(hi[:, :], raw[key][:, :], zero_col[:, :].to_broadcast([P, 2 * D]), ALU.add).then_inc(hi_step, 1)
                                pool.wait_ge(hi_step, i * 4 + (n + 1))
                                pool.tensor_tensor(lo[:, :], raw[key][:, :], hi[:, :].bitcast(F32), ALU.subtract)\
                                    .then_inc(split_done[key], 1)
                        for key in "qk":
                            pool.sem_inc(split_done[key], 1)

                    @block.tensor
                    def _(pe):
                        pe.sem_inc(bank_full, USES)
                        ln_tensor(pe)
                        pe.wait_ge(consts, 2)
                        for n, (_, _, m, h) in enumerate(head0):
                            if h == 0:
                                pe.wait_ge(split_done[m], 2)
                            wt = wq2 if m == "q" else wk2
                            for c in range(C):
                                last = mm3(pe, ps[:, n, :], [a[:, c, 0:DN] for a in wt],
                                           xn_cols(c, h * HALF, (h + 1) * HALF), c == 0, c == C - 1)
                            last.then_inc(first_full, 1)
                        pe.wait_ge(zeroed, 6)
                        pe.wait_ge(first_lo, len(head0))
                        with pe.Fori(0, TURNS) as i:
                            use = 0
                            for step in steps:
                                kind = step[0]
                                if kind in ring_kinds:
                                    pe.wait_ge(bank_free, i * USES + (use + 1))
                                    bank = ps[:, 4 + use % RING, :]
                                    use += 1
                                if kind == "qk":
                                    _, hh, m, h = step
                                    if hh == 0 and h == 0:
                                        pe.wait_ge(split_done[m], i + 3)
                                    wt = wq2 if m == "q" else wk2
                                    for c in range(C):
                                        last = mm3(pe, bank, [a[:, c, hh * DN:(hh + 1) * DN] for a in wt],
                                                   xn_cols(c, h * HALF, (h + 1) * HALF), c == 0, c == C - 1)
                                elif kind == "v":
                                    if step[1] == 0:
                                        pe.wait_ge(split_done["v"], i + 2)
                                    for k in range(2):
                                        t = 2 * step[1] + k
                                        for c in range(C):
                                            last = mm3(pe, bank[:, k * 256:(k + 1) * 256], xn_cols(c, t * P, (t + 1) * P),
                                                       [a[:, c, :] for a in wv2], c == 0, c == C - 1)
                                elif kind == "s":
                                    u = step[1]
                                    hh, qt = units[u]
                                    pe.wait_ge(exp_done, i * N_UNITS + (u + 1))
                                    if qt == 0:
                                        if hh:
                                            pe.wait_ge(bank_free, i * USES + (use_of(("qk", hh, "k", 1)) + 1 + RING))
                                    sbank = ps[:, 2 * (u % 2):2 * (u % 2) + 2, :].rearrange("p b n -> p (b n)")
                                    q0 = qt * P
                                    for a, b in pieces(qt):
                                        mm3(pe, sbank[:, a:b], [x[:, hh, q0:q0 + P] for x in qT],
                                            [x[:, hh, a:b] for x in kT], True, False)
                                    last = pe.matmul(sbank[:, q0:q0 + P], ident_bf[:, :], later[:, :],
                                                     start=False, stop=True, skip_group_check=True)
                                    last.then_inc(scores_full, 1)
                                elif kind == "t":
                                    _, u, k0, k1 = step
                                    if k0 == 0:
                                        pe.wait_ge(exp_done, i * N_UNITS + (u + 1 + 2))
                                    for k in range(k0, k1):
                                        last = pe.transpose(bank[:, (k - k0) * P:(k - k0 + 1) * P],
                                                            prob[:, u % 2, k * P:(k + 1) * P], ident[:, :])
                                elif kind == "sh":
                                    _, hh, c = step
                                    pe.wait_ge(share_found, i * N_UNITS + (8 * hh + 4 * c + 4))
                                    for m in range(4):
                                        last = pe.transpose(bank[:, m * P:(m + 1) * P],
                                                            share[:, m:m + 1].to_broadcast([P, P]), ident[:, :])
                                elif kind == "pv":
                                    _, hh, c = step
                                    tail_step = [s for s in steps if s[0] == "t" and units[s[1]] == (hh, 4 * c + 3)][-1]
                                    pe.wait_ge(bank_free, i * USES + (use_of(tail_step) + 1 + RING))
                                    for k in range(4 * c + 4):
                                        q0 = max(0, k - 4 * c) * P
                                        if k == T - 1:
                                            q0 = 256
                                        last = mm3(pe, bank[:, q0:HALF], [x[:, k, hh * DN:(hh + 1) * DN] for x in V],
                                                   [x[:, k, q0:HALF] for x in PT], k == 0, k == 4 * c + 3)
                                elif kind == "wo":
                                    t = step[1]
                                    if t == 0:
                                        pe.wait_ge(split_done["o"], i + 2)
                                    if t % 4 == 0:
                                        pe.wait_ge(o_lo_done, i * 4 + (3 + 4 if t == 0 else 4))
                                    for hh in range(HP):
                                        last = mm3(pe, bank, [x[:, hh, t * P:(t + 1) * P] for x in oT],
                                                   [x[:, hh, :] for x in wo2], hh == 0, hh == HP - 1)
                                if kind in ring_kinds:
                                    last.then_inc(bank_full, 1)
                        pe.wait_ge(o_lo_done, TURNS * 4 + 4)
                        for t in range(T // 2, T):
                            pe.wait_ge(bank_free, TURNS * USES + (t - T // 2 + 1))
                            for hh in range(HP):
                                last = mm3(pe, ps[:, 4 + (t - T // 2) % RING, :], [x[:, hh, t * P:(t + 1) * P] for x in oT],
                                           [x[:, hh, :] for x in wo2], hh == 0, hh == HP - 1)
                            last.then_inc(bank_full, 1)

                    @block.scalar
                    def _(act):
                        ln_scalar(act)
                        act.sem_inc(exp_done, 2)
                        act.sem_inc(hi_done, SPLITS)
                        for n, step in enumerate(head0):
                            act.wait_ge(first_full, n + 1)
                            src, dst = split_views(step)
                            act.activation(dst[0], src(ps[:, n, :]), ACT.Copy).then_inc(first_hi, 1)
                        with act.Fori(0, TURNS) as i:
                            use = 0
                            for step in steps:
                                kind = step[0]
                                if kind == "e":
                                    u = step[1]
                                    n = (units[u][1] + 1) * P
                                    act.wait_ge(shift_ready, i * N_UNITS + (u + 1))
                                    prev = [s for s in steps if s[0] == "t" and s[1] == (u - 2) % N_UNITS][-1]
                                    turn_back = 1 if u < 2 else 0
                                    act.wait_ge(bank_full, i * USES + (use_of(prev) + 1 + (1 - turn_back) * USES))
                                    sbank = ps[:, 2 * (u % 2):2 * (u % 2) + 2, :].rearrange("p b n -> p (b n)")
                                    act.activation(prob[:, u % 2, 0:n], sbank[:, 0:n], ACT.Exp,
                                                   bias=shift[:, u % 2:u % 2 + 1], scale=SCALE,
                                                   accum_out=total[:, u % 4:u % 4 + 1]).then_inc(exp_done, 1)
                                elif kind in ring_kinds:
                                    bank = ps[:, 4 + use % RING, :]
                                    use += 1
                                    if kind == "pv":
                                        _, hh, c = step
                                        act.wait_ge(bank_free, i * USES + (use_of(step) + 1 + RING))
                                        if hh == 0:
                                            act.wait_ge(bank_full, i * USES + (use_of(("wo", 4 * c + 3)) + 1 + c * USES))
                                        act.activation(oT[0][:, hh, c * HALF:(c + 1) * HALF], o_norm[:, :], ACT.Copy)\
                                           .then_inc(o_hi_done, 1)
                                    if kind not in ("qk", "v", "t"):
                                        continue
                                    act.wait_ge(bank_full, i * USES + (use + USES))
                                    if kind == "t":
                                        _, u, k0, k1 = step
                                        hh, qt = units[u]
                                        if qt % 4 == 0 and k0 == 0:
                                            before = (hh, 0) if qt == 4 else (hh - 1, 1)
                                            if before[0] < 0:
                                                act.wait_ge(bank_full, i * USES + (use_of(("pv", HP - 1, 1)) + 1))
                                            else:
                                                act.wait_ge(bank_full, i * USES + (use_of(("pv", *before)) + 1 + USES))
                                    src, dst = split_views(step)
                                    act.activation(dst[0], src(bank), ACT.Copy).then_inc(hi_done, 1)

                    @block.vector
                    def _(dve):
                        dve.sem_inc(bank_free, RING)
                        dve.sem_inc(o_lo_done, 4)
                        ln_vector(dve)
                        for m in (w["o"][0][:, :], w["o"][1][:, :], oT[0][:, :, HALF:S], oT[1][:, :, HALF:S]):
                            dve.memset(m.bitcast(F32), 0.0).then_inc(zeroed, 1)
                        for part in PT:
                            dve.memset(part[:, T - 1, 256:384].bitcast(F32), 0.0).then_inc(zeroed, 1)
                        for n, step in enumerate(head0):
                            dve.wait_ge(first_hi, n + 1)
                            src, dst = split_views(step)
                            dve.tensor_tensor(dst[1], src(ps[:, n, :]), dst[0].bitcast(F32), ALU.subtract).then_inc(first_lo, 1)
                        with dve.Fori(0, TURNS) as i:
                            use = split = 0
                            for step in steps:
                                kind = step[0]
                                if kind == "s":
                                    u = step[1]
                                    n = (units[u][1] + 1) * P
                                    dve.wait_ge(scores_full, i * N_UNITS + (u + 1))
                                    sbank = ps[:, 2 * (u % 2):2 * (u % 2) + 2, :].rearrange("p b n -> p (b n)")
                                    dve.tensor_reduce(top[:, u % 2:u % 2 + 1], sbank[:, 0:n], AX.X, ALU.max)\
                                       .then_inc(top_found, 1)
                                    dve.wait_ge(top_found, i * N_UNITS + (u + 1))
                                    dve.tensor_scalar(shift[:, u % 2:u % 2 + 1], top[:, u % 2:u % 2 + 1], -SCALE, None,
                                                      ALU.mult).then_inc(shift_ready, 1)
                                elif kind == "ol":
                                    _, hh, c = step
                                    dve.wait_ge(o_hi_done, i * 4 + (2 * hh + c + 1))
                                    cols = slice(c * HALF, (c + 1) * HALF)
                                    dve.tensor_tensor(oT[1][:, hh, cols], o_norm[:, :], oT[0][:, hh, cols].bitcast(F32),
                                                      ALU.subtract).then_inc(o_lo_done, 1)
                                elif kind in ring_kinds:
                                    bank = ps[:, 4 + use % RING, :]
                                    use += 1
                                    if kind == "wo":
                                        t = step[1]
                                        dve.wait_ge(bank_full, i * USES + (use + USES))
                                        dve.tensor_tensor(x_res[:, t, :], x_res[:, t, :], bank, ALU.add).then_inc(bank_free, 1)
                                    elif kind == "sh":
                                        dve.wait_ge(bank_full, i * USES + (use + USES))
                                        dve.tensor_copy(share_row[:, :], bank).then_inc(bank_free, 1)
                                    elif kind == "pv":
                                        _, hh, c = step
                                        dve.wait_ge(bank_full, i * USES + (use + USES))
                                        dve.wait_ge(bank_free, i * USES + (use_of(("sh", hh, c)) + 1 + RING))
                                        dve.tensor_tensor(o_norm[:, :], bank, share_row[:, :], ALU.mult).then_inc(bank_free, 1)
                                    else:
                                        if kind == "t" and step[2] == 0:
                                            _, u, k0, k1 = step
                                            dve.wait_ge(exp_done, i * N_UNITS + (u + 1 + 2))
                                            if units[u][1] % 4 == 0:
                                                before = [x for x in steps if x[0] == "sh" and 8 * x[1] + 4 * x[2] < u]
                                                dve.wait_ge(bank_full, i * USES + (use_of(before[-1]) + 1 + USES) if before
                                                            else i * USES + (use_of(("sh", HP - 1, 1)) + 1))
                                            dve.reciprocal(share[:, units[u][1] % 4:units[u][1] % 4 + 1],
                                                           total[:, u % 4:u % 4 + 1]).then_inc(share_found, 1)
                                        split += 1
                                        dve.wait_ge(hi_done, i * SPLITS + (split + SPLITS))
                                        src, dst = split_views(step)
                                        dve.tensor_tensor(dst[1], src(bank), dst[0].bitcast(F32), ALU.subtract)\
                                           .then_inc(bank_free, 1)
                        for t in range(T // 2, T):
                            dve.wait_ge(bank_full, (TURNS + 1) * USES + (t - T // 2 + 1))
                            dve.tensor_tensor(x_res[:, t, :], x_res[:, t, :], ps[:, 4 + (t - T // 2) % RING, :], ALU.add)

        def lora_ffn(tag):
            E, R, SCALE = 4, 8, 1.0
            ER = E * R
            GA = E + ER
            RING, EARLY = 8, 4
            with ExitStack() as st:
                up_nat = sb(st, f"up_nat{tag}", [P, C, D])
                ga_nat = sb(st, f"ga_nat{tag}", [GA, D])
                lb_nat = sb(st, f"lb_nat{tag}", [P, C, E, R])
                e_bias = sb(st, f"e_bias{tag}", [P, E])
                upT = [sb(st, f"upT_{part}{tag}", [P, C, D], F32R) for part in ("hi", "lo")]
                gaT = [sb(st, f"gaT_{part}{tag}", [P, C, GA], F32R) for part in ("hi", "lo")]
                lbT = [sb(st, f"lbT_{part}{tag}", [ER, D], F32R) for part in ("hi", "lo")]
                lzT = sb(st, f"lzT{tag}", [GA, S])
                lz = sb(st, f"lz{tag}", [P, T, GA])
                logits = sb(st, f"logits{tag}", [P, T * E])
                z = sb(st, f"z{tag}", [P, T, ER])
                zT = [sb(st, f"zT_{part}{tag}", [ER, S], F32R) for part in ("hi", "lo")]
                before = sb(st, f"before{tag}", [P, E, E])
                gt = sb(st, f"gt{tag}", [P, T * E * E])
                eq = sb(st, f"eq{tag}", [P, T * E * E])
                mask = sb(st, f"mask{tag}", [P, T * E])
                loaded = sem(st, f"l_loaded{tag}")
                pool_step = sem(st, f"l_pool_step{tag}")
                full = sem(st, f"l_bank_full{tag}")
                hi_done = sem(st, f"l_hi_done{tag}")
                free = sem(st, f"l_bank_free{tag}")
                dve_step = sem(st, f"l_dve_step{tag}")
                lz_ready = sem(st, f"lz_ready{tag}")
                z_ready = sem(st, f"z_ready{tag}")
                stored = sem(st, f"out_stored{tag}")
                ln_vector, ln_tensor, ln_scalar, ln_gpsimd = layer_norm(st, tag, sb(st, f"xn{tag}", [P, 4, D]), bank0=4)
                uses = [("ga", 0), ("lb", 0)] + [("up", c) for c in range(C)] + [("lzT", 0), ("lzT", 1), ("lz", 0)] \
                    + [("z", 0), ("z", 1)] + [("y", t) for t in range(T)]
                at = {u: n for n, u in enumerate(uses)}
                SPLITS = [u for u in uses if u[0] in ("ga", "lb", "up", "z")]
                bank_of = {u: ps[:, n % RING, :] for u, n in at.items()}

                def split_of(u):
                    b = bank_of[u]
                    kind, k = u
                    if kind == "ga":
                        return b[:, 0:C * GA].rearrange("p (c n) -> p c n", c=C), [a[:, :, :] for a in gaT]
                    if kind == "lb":
                        return b[0:ER, :], [a[:, :] for a in lbT]
                    if kind == "up":
                        return b, [a[:, k, :] for a in upT]
                    return b[0:ER, :], [a[:, k * HALF:(k + 1) * HALF] for a in zT]

                with nc.Block() as block:
                    @block.sync
                    def _(sp):
                        sp.dma_start(ga_nat[0:E, :], gate_w).then_inc(loaded, 16)
                        sp.dma_start(ga_nat[E:GA, :], lora_a.rearrange("e r h -> (e r) h")).then_inc(loaded, 16)
                        for c in range(C):
                            sp.dma_start(lb_nat[:, c, :, :], lora_b[:, c * P:(c + 1) * P, :].rearrange("e p r -> p e r"))\
                              .then_inc(loaded, 16)
                        sp.dma_start(e_bias[:, :], expert_bias.partition_broadcast(P)).then_inc(loaded, 16)
                        sp.dma_start(up_nat[:, :, :], w_up.rearrange("(c p) h -> p c h", p=P)).then_inc(loaded, 16)
                        if tag == LAST:
                            for t in range(T):
                                sp.wait_ge(free, at[("y", t)] + 1)
                                sp.dma_start(out.rearrange("a (t p) d -> p (a t) d", p=P)[:, t, :], x_res[:, t, :])\
                                  .then_inc(stored, 16)
                            sp.wait_ge(stored, 16 * T)

                    @block.gpsimd
                    def _(pool):
                        pool.memset(before[:, :, :], 1.0).then_inc(pool_step, 1)
                        pool.wait_ge(pool_step, 1)
                        pool.affine_select(out=before[:, :, :], in_=before[:, :, :], compare_op=ALU.is_gt, fill=0.0,
                                           base=0, pattern=[[1, E], [-1, E]], channel_multiplier=0)\
                            .then_inc(pool_step, 1)
                        ln_gpsimd(pool)

                    def dense(pe, t):
                        for c in range(C):
                            mm3(pe, bank_of[("y", t)], xn_cols(c, t * P, (t + 1) * P), [a[:, c, :] for a in upT], c == 0, False)

                    @block.tensor
                    def _(pe):
                        ln_tensor(pe)
                        pe.wait_ge(loaded, 16 * 8)
                        for n, u in enumerate(uses):
                            kind, k = u
                            b = bank_of[u]
                            if n >= RING:
                                pe.wait_ge(free, n - RING + 1)
                            if kind == "ga":
                                for c in range(C):
                                    last = pe.transpose(b[:, c * GA:(c + 1) * GA], ga_nat[:, c * P:(c + 1) * P],
                                                        ident[0:GA, 0:GA])
                            elif kind == "lb":
                                for c in range(C):
                                    last = pe.transpose(b[0:ER, c * P:(c + 1) * P],
                                                        lb_nat[:, c, :, :].rearrange("p e r -> p (e r)"), ident[:, :])
                            elif kind == "up":
                                for o in range(C):
                                    last = pe.transpose(b[:, o * P:(o + 1) * P], up_nat[:, o, k * P:(k + 1) * P],
                                                        ident[:, :])
                            elif kind == "lzT":
                                pe.wait_ge(free, at[("ga", 0)] + 1)
                                for c in range(C):
                                    last = mm3(pe, b[0:GA, :], [a[:, c, :] for a in gaT],
                                               xn_cols(c, k * HALF, (k + 1) * HALF), c == 0, c == C - 1)
                            elif kind == "lz":
                                pe.wait_ge(free, at[("lzT", 1)] + 1)
                                for t in range(T):
                                    last = pe.transpose(b[:, t * GA:(t + 1) * GA], lzT[:, t * P:(t + 1) * P],
                                                        ident[0:GA, 0:GA])
                            elif kind == "z":
                                if k == 0:
                                    pe.wait_ge(free, max(at[("up", C - 1)], at[("y", EARLY - 1)] - RING) + 1)
                                    for t in range(EARLY):
                                        dense(pe, t)
                                pe.wait_ge(z_ready, 1)
                                for t in range(4):
                                    last = pe.transpose(b[0:ER, t * P:(t + 1) * P], z[:, 4 * k + t, :], ident[:, :])
                            elif kind == "y":
                                if k == 0:
                                    pe.wait_ge(free, at[("z", 1)] + 1)
                                if k >= EARLY:
                                    dense(pe, k)
                                last = mm3(pe, b, [a[:, k * P:(k + 1) * P] for a in zT], [a[:, :] for a in lbT],
                                           False, True)
                            last.then_inc(full, 1)

                    @block.scalar
                    def _(act):
                        ln_scalar(act)
                        for u in SPLITS:
                            act.wait_ge(full, at[u] + 1)
                            src, dst = split_of(u)
                            act.activation(dst[0], src, ACT.Copy).then_inc(hi_done, 1)

                    @block.vector
                    def _(dve):
                        ln_vector(dve)
                        for n, u in enumerate(uses):
                            kind, k = u
                            b = bank_of[u]
                            if u in SPLITS:
                                dve.wait_ge(hi_done, SPLITS.index(u) + 1)
                                src, dst = split_of(u)
                                dve.tensor_tensor(dst[1], src, dst[0].bitcast(F32), ALU.subtract).then_inc(free, 1)
                            elif kind == "lzT":
                                dve.wait_ge(full, n + 1)
                                dve.tensor_copy(lzT[:, k * HALF:(k + 1) * HALF], b[0:GA, :]).then_inc(free, 1)
                            elif kind == "lz":
                                dve.wait_ge(full, n + 1)
                                dve.tensor_copy(lz[:, :, :], b[:, 0:T * GA].rearrange("p (t n) -> p t n", n=GA))\
                                   .then_inc(free, 1)
                                dve.wait_ge(free, n + 1)
                                dve.wait_ge(loaded, 16 * 8)
                                dve.tensor_tensor(logits[:, :].rearrange("p (t e) -> p t e", e=E), lz[:, :, 0:E],
                                                  e_bias[:, :].unsqueeze(1).to_broadcast([P, T, E]), ALU.add)\
                                   .then_inc(dve_step, 1)
                                dve.wait_ge(pool_step, 2)
                                m = rank_mask(dve, dve_step, 1, logits[:, :], mask[:, :], gt[:, :], eq[:, :],
                                              before[:, :, :], E, 1, SCALE)
                                dve.wait_ge(dve_step, m)
                                dve.tensor_tensor(z[:, :, :].rearrange("p t (e r) -> p t e r", r=R),
                                                  lz[:, :, E:GA].rearrange("p t (e r) -> p t e r", r=R),
                                                  mask[:, :].rearrange("p (t e) -> p t e", e=E).unsqueeze(3)
                                                  .to_broadcast([P, T, E, R]), ALU.mult).then_inc(z_ready, 1)
                            elif kind == "y":
                                dve.wait_ge(full, n + 1)
                                dve.scalar_tensor_tensor(x_res[:, k, :], b, 0.5, x_res[:, k, :], ALU.mult, ALU.add)\
                                   .then_inc(free, 1)

        class Tally:

            def __init__(self, semaphore, per_turn, unit=1):
                self.sem, self.per, self.unit = semaphore, per_turn, unit

            def start(self, eng):
                eng.sem_inc(self.sem, self.per * self.unit)

            def wait(self, eng, turn, n):
                assert -self.per <= n < self.per, (n, self.per)
                eng.wait_ge(self.sem, turn * (self.per * self.unit) + (self.per + n + 1) * self.unit)

            def mark(self, instruction):
                return instruction.then_inc(self.sem, self.unit)

        def mamba(tag):
            H, PD, N, G, K = 64, 64, 128, 8, 4
            I = H * PD
            HG = H // G
            GW = HG * PD
            CT = (I + 2 * G * N) // P
            Q = S // P
            with ExitStack() as st:
                dt = sb(st, "dt", [P, Q, H])
                a = sb(st, "a", [P, Q, H])
                grown = sb(st, "grown", [P, Q, H])
                through = sb(st, "through", [P, Q, H])
                to_end = sb(st, "to_end", [P, Q, H])
                upto = sb(st, "upto", [P, P])
                after = sb(st, "after", [P, P])
                after_r = sb(st, "after_r", [P, P], F32R)
                a_hi = sb(st, "a_hi", [P, Q, H], F32R)
                a_lo = sb(st, "a_lo", [P, Q, H], F32R)
                mean_col = sb(st, "mean_col", [P, 1])
                conv_w = sb(st, "conv_w", [P, CT, K])
                conv_b = sb(st, "conv_b", [P, CT])
                d_col = sb(st, "d_col", [P, I // P])
                nw_col = sb(st, "nw_col", [P, I // P])

                NATS, NB = 14, 4
                nat = [sb(st, f"nat{k}", [P, D]) for k in range(NB)]
                WOT = [sb(st, f"WOT_{part}", [P, C, D], F32R) for part in ("hi", "lo")]
                yn = [sb(st, f"yn_{part}", [P, 2, 4, P], F32R) for part in ("hi", "lo")]
                square_sum = sb(st, "square_sum", [P, 2, P])
                rs = sb(st, "m_rs", [P, Q])
                nat_loaded = [Tally(sem(st, f"nat_loaded{k}"), len(range(k, NATS, NB)), 16) for k in range(NB)]
                zeroed = sem(st, "m_zeroed")

                def load_tile(sp, i, n):
                    if n < 4:
                        src = in_proj_w[bass.ds(i * GW + (I + n * P), P), :]
                    elif n < 6:
                        src = in_proj_w[bass.ds(i * N + (2 * I + (n - 4) * G * N), P), :]
                    elif n < 10:
                        src = in_proj_w[bass.ds(i * GW + (n - 6) * P, P), :]
                    else:
                        src = out_proj_w[(n - 10) * P:(n - 9) * P, bass.ds(i * GW, GW)]
                    nat_loaded[n % NB].mark(sp.dma_start(nat[n % NB][:, :], src))

                with ExitStack() as pre:
                    wdt_nat = sb(pre, "wdt_nat", [H, D])
                    wdtT = [sb(pre, f"wdtT_{part}", [P, C, H], F32R) for part in ("hi", "lo")]
                    dtT = sb(pre, "dtT", [H, S])
                    dt_b = sb(pre, "dt_b", [P, H])
                    alog = sb(pre, "alog", [P, H])
                    rate = sb(pre, "rate", [P, H])
                    ones = sb(pre, "ones", [P, P])
                    v, mag, u, w, lnw, zero, dec = [sb(pre, f"sp_{n}", [P, Q * H]) for n in ("v", "mag", "u", "w", "lnw", "zero", "dec")]
                    loaded = sem(pre, "m_loaded")
                    pool_step = sem(pre, "m_pool_step")
                    consts = sem(pre, "m_consts")
                    pe_step = sem(pre, "m_pe_step")
                    act_step = sem(pre, "m_act_step")
                    dve_step = sem(pre, "m_dve_step")
                    ln_vector, ln_tensor, ln_scalar, ln_gpsimd = layer_norm(pre, tag, sb(pre, f"xn{tag}", [P, 4, D]))
                    flat = "p q h -> p (q h)"
                    with nc.Block() as block:
                        @block.sync
                        def _(sp):
                            sp.dma_start(wdt_nat[:, :], in_proj_w[2 * I + 2 * G * N:2 * I + 2 * G * N + H, :]).then_inc(loaded, 16)
                            sp.dma_start(dt_b[:, :], dt_bias.partition_broadcast(P)).then_inc(loaded, 16)
                            sp.dma_start(alog[:, :], a_log.partition_broadcast(P)).then_inc(loaded, 16)
                            with nc.allow_non_contiguous_dma("per-channel vectors, loaded once"):
                                sp.dma_start(conv_w[:, :, :], conv_weight.rearrange("(j p) k -> p j k", p=P)).then_inc(loaded, 16)
                                sp.dma_start(conv_b[:, :], conv_bias.rearrange("(j p) -> p j", p=P)).then_inc(loaded, 16)
                                sp.dma_start(nw_col[:, :], norm_weight.rearrange("(j p) -> p j", p=P)).then_inc(loaded, 16)
                                for k in range(P // PD):
                                    sp.dma_start(d_col[k * PD:(k + 1) * PD, :],
                                                 d_skip.rearrange("(j k) -> k j", k=P // PD)[k].partition_broadcast(PD))\
                                      .then_inc(loaded, 16)
                            for n in range(NB):
                                load_tile(sp, 0, n)

                        @block.gpsimd
                        def _(pool):
                            for m in (upto, after, ones):
                                pool.memset(m[:, :], 1.0).then_inc(pool_step, 1)
                            pool.memset(mean_col[:, :], 1.0 / GW).then_inc(pool_step, 1)
                            pool.wait_ge(pool_step, 4)
                            pool.affine_select(out=upto[:, :], in_=upto[:, :], compare_op=ALU.is_ge, fill=0.0, base=0,
                                               pattern=[[1, P]], channel_multiplier=-1).then_inc(consts, 1)
                            pool.affine_select(out=after[:, :], in_=after[:, :], compare_op=ALU.is_gt, fill=0.0, base=0,
                                               pattern=[[-1, P]], channel_multiplier=1).then_inc(consts, 1)
                            ln_gpsimd(pool)
                            for m in (square_sum[:, :, :], rs[:, :], yn[0][:, :, :, :].bitcast(F32), yn[1][:, :, :, :].bitcast(F32),
                                      WOT[0][:, :, :].bitcast(F32), WOT[1][:, :, :].bitcast(F32)):
                                pool.memset(m, 0.0)

                        @block.tensor
                        def _(pe):
                            ln_tensor(pe)
                            pe.wait_ge(loaded, 16 * 8)
                            for c in range(C):
                                last = pe.transpose(ps[:, 0, c * H:(c + 1) * H], wdt_nat[:, c * P:(c + 1) * P],
                                                    ident[0:H, 0:H])
                            last.then_inc(pe_step, 1)
                            pe.wait_ge(dve_step, 1)
                            for h in range(2):
                                for c in range(C):
                                    last = mm3(pe, ps[0:H, 1 + h, :], [x[:, c, :] for x in wdtT],
                                               xn_cols(c, h * HALF, (h + 1) * HALF), c == 0, c == C - 1)
                            last.then_inc(pe_step, 1)
                            pe.wait_ge(act_step, 2)
                            for t in range(T):
                                last = pe.transpose(ps[:, 3, t * H:(t + 1) * H], dtT[:, t * P:(t + 1) * P],
                                                    ident[0:H, 0:H])
                            last.then_inc(pe_step, 1)
                            pe.wait_ge(consts, 2)
                            pe.wait_ge(dve_step, 13)
                            for b, m in ((4, upto), (5, ones), (6, after)):
                                last = pe.matmul(ps[:, b, :], m[:, :], a[:, :, :].rearrange(flat), start=True, stop=True)
                            last.then_inc(pe_step, 1)

                        @block.scalar
                        def _(act):
                            ln_scalar(act)
                            act.wait_ge(pe_step, 1)
                            act.activation(wdtT[0][:, :, :], ps[:, 0, 0:C * H].rearrange("p (c n) -> p c n", c=C), ACT.Copy)\
                               .then_inc(act_step, 1)
                            act.wait_ge(pe_step, 2)
                            act.activation(dtT[:, :].rearrange("p (h n) -> p h n", h=2), ps[0:H, 1:3, :], ACT.Copy)\
                               .then_inc(act_step, 1)
                            act.wait_ge(dve_step, 3)
                            act.activation(u[:, :], mag[:, :], ACT.Exp, scale=-1.0).then_inc(act_step, 1)
                            act.activation(rate[:, :], alog[:, :], ACT.Exp).then_inc(act_step, 1)
                            act.wait_ge(dve_step, 4)
                            act.activation(lnw[:, :], w[:, :], ACT.Ln).then_inc(act_step, 1)
                            act.wait_ge(pe_step, 4)
                            for b, dst in ((4, grown[:, :, :].rearrange(flat)), (5, through[:, :, :].rearrange(flat)), (6, dec[:, :])):
                                act.activation(dst, ps[:, b, :], ACT.Exp).then_inc(act_step, 1)

                        @block.vector
                        def _(dve):
                            ln_vector(dve)
                            dve.wait_ge(act_step, 1)
                            dve.tensor_tensor(wdtT[1][:, :, :], ps[:, 0, 0:C * H].rearrange("p (c n) -> p c n", c=C),
                                              wdtT[0][:, :, :].bitcast(F32), ALU.subtract).then_inc(dve_step, 1)
                            dve.wait_ge(pe_step, 3)
                            dve.wait_ge(loaded, 16 * 8)
                            vq = v[:, :].rearrange("p (q h) -> p q h", h=H)
                            dt_flat = dt[:, :, :].rearrange(flat)
                            n = 1

                            def then(instruction):
                                nonlocal n
                                instruction.then_inc(dve_step, 1)
                                n += 1
                                dve.wait_ge(dve_step, n)

                            then(dve.tensor_tensor(vq, ps[:, 3, :].rearrange("p (q h) -> p q h", h=H),
                                                   dt_b[:, :].unsqueeze(1).to_broadcast([P, Q, H]), ALU.add))
                            then(dve.scalar_tensor_tensor(mag[:, :], v[:, :], -1.0, v[:, :], ALU.mult, ALU.max))
                            dve.wait_ge(act_step, 4)
                            then(dve.tensor_scalar(w[:, :], u[:, :], 1.0, None, ALU.add))
                            then(dve.tensor_scalar(zero[:, :], w[:, :], 1.0, None, ALU.is_equal))
                            dve.wait_ge(act_step, 5)
                            then(dve.tensor_tensor(lnw[:, :], lnw[:, :], zero[:, :], ALU.add))
                            then(dve.tensor_tensor(lnw[:, :], lnw[:, :], u[:, :], ALU.mult))
                            then(dve.scalar_tensor_tensor(w[:, :], w[:, :], -1.0, zero[:, :], ALU.add, ALU.add))
                            then(dve.reciprocal(mag[:, :], w[:, :]))
                            then(dve.tensor_tensor(lnw[:, :], lnw[:, :], mag[:, :], ALU.mult))
                            then(dve.scalar_tensor_tensor(dt_flat, v[:, :], 0.0, lnw[:, :], ALU.max, ALU.add))
                            then(dve.scalar_tensor_tensor(a[:, :, :], dt[:, :, :], -1.0,
                                                          rate[:, :].unsqueeze(1).to_broadcast([P, Q, H]), ALU.mult, ALU.mult))
                            then(dve.tensor_scalar(a[:, :, :].rearrange(flat), a[:, :, :].rearrange(flat), -1e30, None, ALU.max))
                            then(dve.tensor_copy(a_hi[:, :, :], a[:, :, :]))
                            dve.tensor_tensor(a_lo[:, :, :], a[:, :, :], a_hi[:, :, :].bitcast(F32), ALU.subtract)
                            dve.wait_ge(consts, 2)
                            dve.tensor_copy(after_r[:, :], after[:, :])
                            dve.wait_ge(act_step, 8)
                            then(dve.tensor_tensor(to_end[:, :, :].rearrange(flat), dec[:, :], dt_flat, ALU.mult))

                RING = 4
                WT = [[sb(st, f"WT{k}_{part}", [P, C, P], F32R) for part in ("hi", "lo")] for k in range(2)]
                gate = sb(st, "gate", [P, 4, S])
                XT = sb(st, "XT", [P, 6, S])
                raw = sb(st, "conv_raw", [P, 2, K - 1 + S])
                acc = sb(st, "conv_acc", [P, 2, S])
                X = sb(st, "X", [P, 2, GW])
                B = sb(st, "B", [P, 2, N])
                xdt = sb(st, "xdt", [P, 2, GW])
                xend = sb(st, "xend", [P, 2, GW])
                steps_a = [sb(st, f"steps_a_{part}", [P, HG, P], F32R) for part in ("hi", "lo")]
                E = sb(st, "decay", [P, 2, HG, P])
                Gm = sb(st, "Gm", [P, 2, P])
                carried = sb(st, "carried", [P, GW])
                state = sb(st, "state", [P, GW])
                yT = sb(st, "yT", [P, 2, 4, P])
                var = sb(st, "m_var", [P, Q])

                def prepare(c):
                    return [("xc", c), ("bc", c), ("dec", c, 0), ("dec", c, 1)] + [("sa", c + 1)] * (c + 1 < Q) + [("g", c)]

                steps = [("nat", 0), ("sa", 0), ("nat", 1), ("out", Q - 2)]
                for k in range(10):
                    if k == 9:
                        steps += prepare(0)
                    steps.append(("proj", k, 0))
                    steps += {0: [("ss", Q - 1)], 1: [("out", Q - 1)]}.get(k, [])
                    if k < 9:
                        steps.append(("proj", k, 1))
                    steps.append(("nat", k + 2))
                    if 1 <= k <= 6:
                        steps.append(("silu", k - 1))
                    if k < 6:
                        steps.append(("taps", k))
                steps += [("nat", 12)] + prepare(1)
                for c in range(Q):
                    if c and c + 1 < Q:
                        steps += prepare(c + 1)
                    if c:
                        steps += [("hi", c - 1), ("lo", c - 1), ("in", c)]
                    steps += {0: [], 1: [("proj", 9, 1), ("nat", 13)]}.get(c, [("out", c - 2)])
                    if c + 1 < Q:
                        steps.append(("st", c))
                    if c:
                        steps.append(("sum", c - 1))
                    steps += [("y", c), ("square", c), ("gated", c)]
                    if c:
                        steps.append(("ss", c - 1))
                steps += [("sum", Q - 1), ("hi", Q - 1), ("lo", Q - 1)]
                LATE = 2
                ON_PE = ("nat", "proj", "xc", "bc", "dec", "g", "in", "st", "y", "ss", "out")
                ring_of = {"proj": "a", "xc": "a", "bc": "a", "dec": "a"}
                order = {r: [s for s in steps if s[0] in ON_PE and ring_of.get(s[0], "v") == r] for r in "av"}
                at = {s: n for r in order.values() for n, s in enumerate(r)}

                def bank_of(s):
                    r = ring_of.get(s[0], "v")
                    return ps[:, (0 if r == "a" else 4) + at[s] % RING, :]

                def use_before(s):
                    n, per = at[s], len(order[ring_of.get(s[0], "v")])
                    return n - RING if n >= RING else max(m for m in range(per) if m % RING == n % RING) - per

                def yn_part(c):
                    return [x[:, c % 2, :, :] for x in yn]

                def previous(s):
                    return at[s] - len(order[ring_of.get(s[0], "v")])

                full = {r: Tally(sem(st, f"full_{r}"), len(order[r])) for r in "av"}
                free = {r: Tally(sem(st, f"free_{r}"), len(order[r])) for r in "av"}
                nat_hi = Tally(sem(st, "nat_hi"), NATS)
                taps = Tally(sem(st, "taps"), 6 * (K - 1))
                raw_copied = Tally(sem(st, "raw_copied"), 12)
                silu_done = Tally(sem(st, "silu_done"), 6)
                steps_a_ready = Tally(sem(st, "steps_a_ready"), Q)
                x_scaled = Tally(sem(st, "x_scaled"), 2 * Q)
                mixed = Tally(sem(st, "mixed"), Q)
                state_kept = Tally(sem(st, "state_kept"), Q - 2)
                squared = Tally(sem(st, "squared"), Q)
                summed = Tally(sem(st, "m_summed"), Q)
                rs_ready = Tally(sem(st, "m_rs_ready"), Q)
                gated = Tally(sem(st, "m_gated"), Q)
                yn_hi = Tally(sem(st, "yn_hi"), Q)
                yn_lo = Tally(sem(st, "yn_lo"), Q)
                tail_full = sem(st, "m_tail_full")
                tail_var = sem(st, "m_tail_var")
                tallies = {
                    "pe": [full["a"], full["v"]],
                    "act": [free["a"], nat_hi, raw_copied, silu_done, squared, yn_hi],
                    "dve": [free["v"], taps, mixed, state_kept, gated, yn_lo, summed],
                    "pool": [steps_a_ready, x_scaled, rs_ready],
                }
                bc8 = [P, HG, PD]

                def heads(t):
                    return t.rearrange("p (h d) -> p h d", h=HG)

                def of_group(t, i, c):
                    return t[:, c, bass.ds(i * HG, HG)]

                def nat_dst(n):
                    if n < 10:
                        return lambda b: b.rearrange("p (c n) -> p c n", c=C), [x[:, :, :] for x in WT[n % 2]]
                    k = n - 10
                    return lambda b: b.rearrange("p (c n) -> p c n", c=C), [x[:, :, k * P:(k + 1) * P] for x in WOT]

                with nc.Block() as block:
                    @block.sync
                    def _(sp):
                        def refill(i, n, after):
                            for m in after:
                                full["v"].wait(sp, i, at[("nat", m - NB)] if m >= NB else
                                               at[("nat", [x for x in range(NATS) if x % NB == m % NB][-1])])
                            load_tile(sp, i + (1 if n < NB else 0), n)

                        waits = {9: (10,), 10: ()}
                        with sp.Fori(0, G - 1) as i:
                            for n in list(range(NB, NATS)) + list(range(NB)):
                                refill(i, n, waits.get(n, (n,)))
                        for n in range(NB, NATS):
                            refill(G - 1, n, waits.get(n, (n,)))

                    @block.tensor
                    def _(pe):
                        for x in tallies["pe"]:
                            x.start(pe)
                        with pe.Fori(0, G) as i:
                            for s in steps:
                                kind, k = s[0], s[1]
                                if kind not in ON_PE:
                                    continue
                                r = ring_of.get(kind, "v")
                                free[r].wait(pe, i, use_before(s))
                                b = bank_of(s)
                                if kind == "nat":
                                    pe.wait_ge(nat_loaded[k % NB].sem, i * (nat_loaded[k % NB].per * 16) + (k // NB + 1) * 16)
                                    for c in range(C):
                                        last = pe.transpose(b[:, c * P:(c + 1) * P], nat[k % NB][:, c * P:(c + 1) * P],
                                                            ident[:, :])
                                elif kind == "proj":
                                    free["v"].wait(pe, i, at[("nat", k)])
                                    for c in range(C):
                                        last = mm3(pe, b, [x[:, c, :] for x in WT[k % 2]],
                                                   xn_cols(c, s[2] * HALF, (s[2] + 1) * HALF), c == 0, c == C - 1)
                                elif kind == "xc":
                                    silu_done.wait(pe, i, 3)
                                    for j in range(4):
                                        last = pe.transpose(b[:, j * P:(j + 1) * P], XT[:, j, k * P:(k + 1) * P], ident[:, :])
                                elif kind == "bc":
                                    silu_done.wait(pe, i, 4)
                                    last = pe.transpose(b[:, 0:P], XT[:, 4, k * P:(k + 1) * P], ident[:, :])
                                elif kind == "dec":
                                    steps_a_ready.wait(pe, i, k)
                                    for m in range(2):
                                        last = pe.matmul(b, after_r[:, :],
                                                         steps_a[m][:, 4 * s[2]:4 * s[2] + 4, :].rearrange("p h t -> p (h t)"),
                                                         start=(m == 0), stop=(m == 1), skip_group_check=True)
                                elif kind == "g":
                                    silu_done.wait(pe, i, 5)
                                    cols = slice(k * P, (k + 1) * P)
                                    last = pe.matmul(b[:, 0:P], XT[:, 4, cols], XT[:, 5, cols], start=True, stop=True,
                                                     skip_group_check=True)
                                elif kind == "in":
                                    free["v"].wait(pe, i, at[("st", k - 1)])
                                    last = pe.matmul(b, XT[:, 5, k * P:(k + 1) * P], state[:, :], start=True, stop=True,
                                                     skip_group_check=True)
                                elif kind == "st":
                                    x_scaled.wait(pe, i, 2 * k)
                                    free["a"].wait(pe, i, at[("bc", k)])
                                    last = pe.matmul(b, B[:, k % 2, :], xend[:, k % 2, :], start=True, stop=True,
                                                     skip_group_check=True)
                                elif kind == "y":
                                    mixed.wait(pe, i, k)
                                    x_scaled.wait(pe, i, 2 * k + 1)
                                    if k:
                                        free["v"].wait(pe, i, at[("in", k)])
                                    for j in range(4):
                                        cols = b[:, j * P:(j + 1) * P]
                                        for m in range(2):
                                            h = 2 * j + m
                                            last = pe.matmul(cols[m * PD:(m + 1) * PD, :], xdt[:, k % 2, h * PD:(h + 1) * PD],
                                                             E[:, k % 2, h, :], start=True, stop=(k == 0),
                                                             skip_group_check=True)
                                        if k:
                                            last = pe.matmul(cols, carried[:, j * P:(j + 1) * P], ident[:, :],
                                                             start=False, stop=True, skip_group_check=True)
                                elif kind == "ss":
                                    summed.wait(pe, i, k if k < Q - 1 else -1)
                                    last = pe.matmul(b[:, 0:1], square_sum[:, k % 2, :], mean_col[:, :],
                                                     start=True, stop=True, skip_group_check=True)
                                elif kind == "out":
                                    yn_lo.wait(pe, i, k if k < Q - LATE else k - Q)
                                    for j in range(4):
                                        last = mm3(pe, b, [x[:, j, :] for x in yn_part(k)],
                                                   [x[:, j, :] for x in WOT], j == 0, j == 3)
                                full[r].mark(last)
                        free["a"].wait(pe, G, -1)
                        free["v"].wait(pe, G, -1)
                        summed.wait(pe, G, -1)
                        pe.matmul(ps[:, 0, 0:1], square_sum[:, (Q - 1) % 2, :], mean_col[:, :], start=True, stop=True,
                                  skip_group_check=True).then_inc(tail_full, 1)
                        for c in range(Q - LATE, Q):
                            yn_lo.wait(pe, G, c - Q)
                            for j in range(4):
                                last = mm3(pe, ps[:, 1 + c % 2, :], [x[:, j, :] for x in yn_part(c)],
                                           [x[:, j, :] for x in WOT], j == 0, j == 3)
                            last.then_inc(tail_full, 1)

                    @block.scalar
                    def _(act):
                        for x in tallies["act"]:
                            x.start(act)
                        with act.Fori(0, G) as i:
                            for s in steps:
                                kind, k = s[0], s[1]
                                b = bank_of(s) if s in at else None
                                if kind in ring_of:
                                    full["a"].wait(act, i, at[s])
                                if kind == "nat":
                                    full["v"].wait(act, i, at[s])
                                    if k < 10:
                                        if k >= 2:
                                            full["a"].wait(act, i, at[("proj", k - 2, 1)])
                                    elif k == 10:
                                        full["v"].wait(act, i, at[("out", Q - 1)])
                                    src, dst = nat_dst(k)
                                    nat_hi.mark(act.activation(dst[0], src(b), ACT.Copy))
                                elif kind == "proj" and k >= 6:
                                    yn_lo.wait(act, i, -1)
                                    free["a"].mark(act.activation(gate[:, k - 6, s[2] * HALF:(s[2] + 1) * HALF], b, ACT.Silu))
                                elif kind == "proj":
                                    j, h = k, s[2]
                                    ct = i * 4 + j if j < 4 else i + (I // P + (j - 4) * G)
                                    cols = slice(h * HALF, (h + 1) * HALF)
                                    if h == 0:
                                        taps.wait(act, i, (K - 1) * (j - 1) - 1)
                                        silu_done.wait(act, i, j - 2)
                                    raw_copied.mark(act.activation(raw[:, j % 2, K - 1 + h * HALF:K - 1 + (h + 1) * HALF], b,
                                                                   ACT.Copy))
                                    free["a"].mark(act.activation(acc[:, j % 2, cols], b, ACT.Identity,
                                                                  scale=conv_w[:, bass.ds(ct, 1), K - 1],
                                                                  bias=conv_b[:, bass.ds(ct, 1)]))
                                elif kind == "silu":
                                    taps.wait(act, i, (K - 1) * (k + 1) - 1)
                                    if k == 0:
                                        summed.wait(act, i, -1)
                                    silu_done.mark(act.activation(XT[:, k, :], acc[:, k % 2, :], ACT.Silu))
                                elif kind == "xc":
                                    x_scaled.wait(act, i, 2 * (k - 2) + 1)
                                    free["a"].mark(act.activation(X[:, k % 2, :], b, ACT.Copy))
                                elif kind == "bc":
                                    if k >= 2:
                                        full["v"].wait(act, i, at[("st", k - 2)])
                                    free["a"].mark(act.activation(B[:, k % 2, :], b[:, 0:P], ACT.Copy))
                                elif kind == "dec":
                                    if k >= 2 and s[2] == 0:
                                        full["v"].wait(act, i, at[("y", k - 2)])
                                    free["a"].mark(act.activation(
                                        E[:, k % 2, 4 * s[2]:4 * s[2] + 4, :].rearrange("p h t -> p (h t)"), b, ACT.Exp))
                                elif kind == "square":
                                    free["v"].wait(act, i, at[("y", k)])
                                    squared.mark(act.activation(XT[:, 0:4, k * P:(k + 1) * P], yT[:, k % 2, :, :], ACT.Square))
                                elif kind == "hi":
                                    gated.wait(act, i, k)
                                    full["v"].wait(act, i, at[("out", k - 2)] if k >= 2 else
                                                   at[("out", k - 2 + Q)])
                                    yn_hi.mark(act.activation(yn[0][:, k % 2, :, :], gate[:, :, k * P:(k + 1) * P], ACT.Copy))

                    @block.gpsimd
                    def _(pool):
                        for x in tallies["pool"]:
                            x.start(pool)
                        pool.memset(raw[:, :, 0:K - 1], 0.0).then_inc(zeroed, 1)
                        with pool.Fori(0, G) as i:
                            for s in steps:
                                kind, k = s[0], s[1]
                                if kind == "sa":
                                    full["a"].wait(pool, i, at[("dec", k - 1, 1)] if k else
                                                   at[("dec", Q - 1, 1)] - len(order["a"]))
                                    for dst, part in zip(steps_a, (a_hi, a_lo)):
                                        last = pool.tensor_tensor(
                                            dst[:, :, :], upto[:, :].unsqueeze(1).to_broadcast([P, HG, P]),
                                            of_group(part, i, k).bitcast(F32).unsqueeze(2).to_broadcast([P, HG, P]), ALU.mult)
                                    steps_a_ready.mark(last)
                                elif kind == "g":
                                    c = k
                                    free["a"].wait(pool, i, at[("xc", c)])
                                    full["v"].wait(pool, i, at[("y", c - 2)] if c >= 2 else at[("y", Q - 2 + c)] - len(order["v"]))
                                    for dst, by in ((xend, to_end), (xdt, dt)):
                                        x_scaled.mark(pool.tensor_tensor(heads(dst[:, c % 2, :]), heads(X[:, c % 2, :]),
                                                                         of_group(by, i, c).unsqueeze(2).to_broadcast(bc8), ALU.mult))
                                elif kind == "ss":
                                    free["v"].wait(pool, i, at[s])
                                    rs_ready.mark(pool.tensor_tensor(rs[:, k:k + 1], var[:, k:k + 1], minus_half[:, :], ALU.pow))
                        pool.wait_ge(tail_var, 1)
                        rs_ready.mark(pool.tensor_tensor(rs[:, Q - 1:Q], var[:, Q - 1:Q], minus_half[:, :], ALU.pow))

                    @block.vector
                    def _(dve):
                        for x in tallies["dve"]:
                            x.start(dve)
                        dve.wait_ge(zeroed, 1)
                        with dve.Fori(0, G) as i:
                            for s in steps:
                                kind, k = s[0], s[1]
                                b = bank_of(s) if s in at else None
                                if kind in ON_PE and kind not in ring_of and kind != "nat":
                                    full["v"].wait(dve, i, at[s])
                                if kind == "nat":
                                    nat_hi.wait(dve, i, k)
                                    src, dst = nat_dst(k)
                                    free["v"].mark(dve.tensor_tensor(dst[1], src(b), dst[0].bitcast(F32), ALU.subtract))
                                elif kind == "taps":
                                    j = k
                                    ct = i * 4 + j if j < 4 else i + (I // P + (j - 4) * G)
                                    free["a"].wait(dve, i, at[("proj", j, 1)])
                                    for m in range(K - 1):
                                        if m:
                                            taps.wait(dve, i, (K - 1) * j + m - 1)
                                        taps.mark(dve.scalar_tensor_tensor(
                                            acc[:, j % 2, :], raw[:, j % 2, m:m + S], conv_w[:, bass.ds(ct, 1), m], acc[:, j % 2, :],
                                            ALU.mult, ALU.add))
                                elif kind == "g":
                                    free["v"].mark(dve.tensor_tensor(Gm[:, k % 2, :], b[:, 0:P], upto[:, :], ALU.mult))
                                    free["v"].wait(dve, i, at[s])
                                    free["a"].wait(dve, i, at[("dec", k, 1)])
                                    mixed.mark(dve.tensor_tensor(E[:, k % 2, :, :], E[:, k % 2, :, :],
                                                                 Gm[:, k % 2, :].unsqueeze(1).to_broadcast([P, HG, P]), ALU.mult))
                                elif kind == "in":
                                    if k >= 2:
                                        full["v"].wait(dve, i, at[("y", k - 1)])
                                    free["v"].mark(dve.tensor_tensor(heads(carried[:, :]), heads(b),
                                                                     of_group(grown, i, k).unsqueeze(2).to_broadcast(bc8), ALU.mult))
                                elif kind == "st":
                                    if k == 0:
                                        free["v"].mark(dve.tensor_copy(state[:, :], b))
                                    else:
                                        state_kept.mark(dve.tensor_tensor(heads(state[:, :]), heads(state[:, :]),
                                                                          of_group(through, i, k).unsqueeze(2).to_broadcast(bc8), ALU.mult))
                                        state_kept.wait(dve, i, k - 1)
                                        free["v"].mark(dve.tensor_tensor(state[:, :], state[:, :], b, ALU.add))
                                elif kind == "y":
                                    c = k
                                    squared.wait(dve, i, c - 2)
                                    gated.wait(dve, i, c - 2)
                                    for j in range(4):
                                        ins = dve.scalar_tensor_tensor(yT[:, c % 2, j, :], XT[:, j, c * P:(c + 1) * P],
                                                                       d_col[:, bass.ds(i * 4 + j, 1)], b[:, j * P:(j + 1) * P],
                                                                       ALU.mult, ALU.add)
                                    free["v"].mark(ins)
                                elif kind == "ss":
                                    free["v"].mark(dve.tensor_scalar(var[:, k:k + 1], b[:, 0:1], EPS, None, ALU.add))
                                elif kind == "gated":
                                    free["a"].wait(dve, i, at[("proj", 9, k // 4)])
                                    free["v"].wait(dve, i, at[("y", k)])
                                    for j in range(4):
                                        here = gate[:, j, k * P:(k + 1) * P]
                                        ins = dve.scalar_tensor_tensor(here, yT[:, k % 2, j, :], nw_col[:, bass.ds(i * 4 + j, 1)],
                                                                       here, ALU.mult, ALU.mult)
                                    gated.mark(ins)
                                elif kind == "sum":
                                    squared.wait(dve, i, k)
                                    full["v"].wait(dve, i, at[("ss", (k - 2) % Q)] if k else at[("ss", Q - 2)] - len(order["v"]))
                                    summed.mark(dve.tensor_reduce(square_sum[:, k % 2, :],
                                                                  XT[:, 0:4, k * P:(k + 1) * P].rearrange("p j n -> p n j"),
                                                                  AX.X, ALU.add))
                                elif kind == "lo":
                                    yn_hi.wait(dve, i, k)
                                    yn_lo.mark(dve.tensor_tensor(yn[1][:, k % 2, :, :], gate[:, :, k * P:(k + 1) * P],
                                                                 yn[0][:, k % 2, :, :].bitcast(F32), ALU.subtract))
                                elif kind == "out":
                                    rs_ready.wait(dve, i, -1 if k == Q - 2 else (k + 1) % Q)
                                    free["v"].mark(dve.scalar_tensor_tensor(x_res[:, k, :], b, rs[:, k:k + 1], x_res[:, k, :],
                                                                            ALU.mult, ALU.add))
                        dve.wait_ge(tail_full, 1)
                        dve.tensor_scalar(var[:, Q - 1:Q], ps[:, 0, 0:1], EPS, None, ALU.add).then_inc(tail_var, 1)
                        rs_ready.wait(dve, G, 0)
                        for c in range(Q - LATE, Q):
                            dve.wait_ge(tail_full, 2 + c - (Q - LATE))
                            dve.scalar_tensor_tensor(x_res[:, c, :], ps[:, 1 + c % 2, :], rs[:, c:c + 1], x_res[:, c, :],
                                                     ALU.mult, ALU.add)

        run = dict(zip(TAGS, (experts_ffn, attention, experts_ffn, lora_ffn, mamba, lora_ffn)))
        for tag in [TAGS[n] for n in stages]:
            run[tag](tag)


_INS = ['L0_attn_hidden_states', 'L0_attn_wq', 'L0_attn_wkv', 'L0_attn_wo', 'L0_ffn_W_gate', 'L0_ffn_b_gate',
        'L0_ffn_W_e', 'L0_ffn_b_e', 'L1_attn_in_proj_w', 'L1_attn_conv_weight', 'L1_attn_conv_bias',
        'L1_attn_dt_bias', 'L1_attn_A_log', 'L1_attn_D', 'L1_attn_norm_weight', 'L1_attn_out_proj_w',
        'L1_ffn_W_up', 'L1_ffn_gate_w', 'L1_ffn_expert_bias', 'L1_ffn_lora_A', 'L1_ffn_lora_B']
_STAGES = range(6)


def kernel(**inputs):
    import numpy as _np
    import concourse.bacc as _bacc
    from concourse import mybir as _mybir
    from concourse.bass_utils import run_bass_kernel_spmd as _run

    nc = _bacc.Bacc("TRN2", target_bir_lowering=False, num_devices=1)
    arrays, args = {}, []
    for name in _INS:
        a = _np.ascontiguousarray(inputs[name])
        arrays[f"in_{name}_dram"] = a
        args.append(nc.dram_tensor(f"in_{name}_dram", a.shape, _mybir.dt.from_np(a.dtype), kind="ExternalInput").ap())
    out = nc.dram_tensor("out_0_dram", (1, S, D), _mybir.dt.float32, kind="ExternalOutput").ap()
    build(nc, _STAGES, *args, out)
    r = _run(nc, [arrays], core_ids=[0])
    return r.results[0]["out_0_dram"]
```
